# Optimizing a Trainium2 kernel written in Bass

```python
import numpy as np
import jax
import jax.numpy as jnp

def _softmax(x, axis=-1):
    return jax.nn.softmax(x, axis=axis)

def _gelu(x):
    return jax.nn.gelu(x, approximate=True)

def _silu(x):
    return jax.nn.silu(x)

def _sigmoid(x):
    return jax.nn.sigmoid(x)

def _layernorm(x, axis=-1, eps=1e-05):
    m = jnp.mean(x, axis=axis, keepdims=True)
    v = jnp.var(x, axis=axis, keepdims=True)
    return (x - m) / jnp.sqrt(v + eps)

def _scatter_add(tgt, idx, src, axis=0):
    return tgt.at[idx].add(src)

def _segment_sum(src, seg, n):
    return jax.ops.segment_sum(src, seg, n)
kernel_name = 'mk_decoder_preln_d1_seqx_r8_d22f24'

def setup_inputs(seed: int=0):
    np.random.seed(seed)
    _w = jnp.asarray

    def _rec_inputs():
        import jax
        import jax.numpy as jnp
        _rk = jax.random.key(seed)
        x = 7.22e-05 + 1 * jax.random.normal(jax.random.fold_in(_rk, 1), (16, 128, 256), jnp.float32)
        _lenS = 128 - jax.random.randint(jax.random.fold_in(_rk, 7), (16,), 0, max(1, 128 // 4) + 1, jnp.int32)
        _lenS2 = 128 - jax.random.randint(jax.random.fold_in(_rk, 8), (16,), 0, max(1, 128 // 4) + 1, jnp.int32)
        _ctx_1024P = jax.random.normal(jax.random.fold_in(_rk, 11), (16, 16, 128), jnp.float32)
        _ctx_1024c = jax.random.dirichlet(jax.random.fold_in(_rk, 511), 0.3 * jnp.ones((16,), jnp.float32), (16, 128))
        _ctx_1024t = jnp.einsum('bsk,bkd->bsd', _ctx_1024c, _ctx_1024P)
        _ctx_1024t = _ctx_1024t * jax.lax.rsqrt(jnp.mean(jnp.square(_ctx_1024t)) + 1e-12) * 0.953939
        ctx_1024 = -1.39393e-06 + 0.999914 * (_ctx_1024t + 0.3 * jax.random.normal(jax.random.fold_in(_rk, 611), (16, 128, 128), jnp.float32))
        fside_BxSx2_0 = jax.random.uniform(jax.random.fold_in(_rk, 12), (16, 128, 2), jnp.float32, 0.0, 0.999707)
        return (x, ctx_1024, fside_BxSx2_0)
    x, ctx_1024, fside_BxSx2_0 = _rec_inputs()

    def _L0_attn_setup():
        import jax, jax.numpy as jnp
        import numpy as np
        H = 16
        D_MODEL = 256
        HEAD_DIM = D_MODEL // H
        B, S = (4, 256)
        key = jax.random.key(seed)
        ks = jax.random.split(key, 9)
        std = D_MODEL ** (-0.5)
        hidden_states = jax.random.normal(ks[0], (B, S, D_MODEL), dtype=jnp.float32)
        q_w = jax.random.normal(ks[1], (H * HEAD_DIM, D_MODEL), dtype=jnp.float32) * std
        k_w = jax.random.normal(ks[2], (HEAD_DIM, D_MODEL), dtype=jnp.float32) * std
        v_w = jax.random.normal(ks[3], (HEAD_DIM, D_MODEL), dtype=jnp.float32) * std
        o_w = jax.random.normal(ks[4], (D_MODEL, H * HEAD_DIM), dtype=jnp.float32) * std
        q_b = jnp.zeros((H * HEAD_DIM,), dtype=jnp.float32)
        k_b = jnp.zeros((HEAD_DIM,), dtype=jnp.float32)
        v_b = jnp.zeros((HEAD_DIM,), dtype=jnp.float32)
        o_b = jnp.zeros((D_MODEL,), dtype=jnp.float32)
        return {'hidden_states': hidden_states, 'q_w': q_w, 'q_b': q_b, 'k_w': k_w, 'k_b': k_b, 'v_w': v_w, 'v_b': v_b, 'o_w': o_w, 'o_b': o_b}
    _L0_attn_all = _L0_attn_setup()
    _L0_attn_in = {k: v for k, v in _L0_attn_all.items() if k in ('q_w', 'q_b', 'k_w', 'k_b', 'v_w', 'v_b', 'o_w', 'o_b')}
    del _L0_attn_all

    def _L0_xattn_setup():
        import jax, jax.numpy as jnp
        import numpy as np
        DIM = 256
        CTX_DIM = 128
        N_HEADS = 32
        HEAD_DIM = DIM // N_HEADS
        POS_DIM = 2
        B, N, CTXN = (2, 256, 256)
        ROPE_BASE = 10000.0

        def apply_axial_rope(x, pos):
            b, n, h, d = x.shape
            p = pos.shape[-1]
            dpa = d // p
            half = dpa // 2
            freqs = ROPE_BASE ** (-jnp.arange(half, dtype=x.dtype) / half)
            ang = pos[..., :, None] * freqs
            cos = jnp.cos(ang)[:, :, None, :, :]
            sin = jnp.sin(ang)[:, :, None, :, :]
            xr = x.reshape(b, n, h, p, half, 2)
            x1, x2 = (xr[..., 0], xr[..., 1])
            out = jnp.stack([x1 * cos - x2 * sin, x1 * sin + x2 * cos], axis=-1)
            return out.reshape(b, n, h, d)
        key = jax.random.key(seed)
        ks = jax.random.split(key, 8)
        x = jax.random.normal(ks[0], (B, N, DIM), jnp.float32)
        ctx = jax.random.normal(ks[1], (B, CTXN, CTX_DIM), jnp.float32)
        pos_map = jax.random.uniform(ks[2], (B, N, POS_DIM), jnp.float32)
        ctx_pos_map = jax.random.uniform(ks[3], (B, CTXN, POS_DIM), jnp.float32)
        Wq = jax.random.normal(ks[4], (DIM, DIM), jnp.float32) / np.sqrt(DIM)
        Wkv = jax.random.normal(ks[5], (CTX_DIM, 2 * DIM), jnp.float32) / np.sqrt(CTX_DIM)
        Wout = jax.random.normal(ks[6], (DIM, DIM), jnp.float32) / np.sqrt(DIM)
        bout = jnp.zeros((DIM,), jnp.float32)
        return {'x': x, 'ctx': ctx, 'pos_map': pos_map, 'ctx_pos_map': ctx_pos_map, 'Wq': Wq, 'Wkv': Wkv, 'Wout': Wout, 'bout': bout}
    _L0_xattn_all = _L0_xattn_setup()
    _L0_xattn_in = {k: v for k, v in _L0_xattn_all.items() if k in ('Wq', 'Wkv', 'Wout', 'bout')}
    del _L0_xattn_all

    def _L0_ffn_setup():
        import jax, jax.numpy as jnp
        import numpy as np
        B, S, H = (2, 256, 256)
        E, K = (16, 4)
        I_MOE, I_SH = (176, 704)
        key = jax.random.key(seed)
        ks = jax.random.split(key, 9)

        def w(k, shape, fan_in):
            return jax.random.normal(k, shape, jnp.float32) * fan_in ** (-0.5)
        return {'hidden_states': jax.random.normal(ks[0], (B, S, H), jnp.float32), 'router_w': w(ks[1], (E, H), H), 'w_gate': w(ks[2], (E, H, I_MOE), H), 'w_up': w(ks[3], (E, H, I_MOE), H), 'w_down': w(ks[4], (E, I_MOE, H), I_MOE), 'sh_gate': w(ks[5], (H, I_SH), H), 'sh_up': w(ks[6], (H, I_SH), H), 'sh_down': w(ks[7], (I_SH, H), I_SH), 'sh_gate_w': w(ks[8], (H, 1), H)}
    _L0_ffn_all = _L0_ffn_setup()
    _L0_ffn_in = {k: v for k, v in _L0_ffn_all.items() if k in ('router_w', 'w_gate', 'w_up', 'w_down', 'sh_gate', 'sh_up', 'sh_down', 'sh_gate_w')}
    del _L0_ffn_all
    return {'x': x, 'ctx_1024': ctx_1024, 'fside_BxSx2_0': fside_BxSx2_0, 'L0_attn_q_w': _L0_attn_in['q_w'], 'L0_attn_q_b': _L0_attn_in['q_b'], 'L0_attn_k_w': _L0_attn_in['k_w'], 'L0_attn_k_b': _L0_attn_in['k_b'], 'L0_attn_v_w': _L0_attn_in['v_w'], 'L0_attn_v_b': _L0_attn_in['v_b'], 'L0_attn_o_w': _L0_attn_in['o_w'], 'L0_attn_o_b': _L0_attn_in['o_b'], 'L0_xattn_Wq': _L0_xattn_in['Wq'], 'L0_xattn_Wkv': _L0_xattn_in['Wkv'], 'L0_xattn_Wout': _L0_xattn_in['Wout'], 'L0_xattn_bout': _L0_xattn_in['bout'], 'L0_ffn_router_w': _L0_ffn_in['router_w'], 'L0_ffn_w_gate': _L0_ffn_in['w_gate'], 'L0_ffn_w_up': _L0_ffn_in['w_up'], 'L0_ffn_w_down': _L0_ffn_in['w_down'], 'L0_ffn_sh_gate': _L0_ffn_in['sh_gate'], 'L0_ffn_sh_up': _L0_ffn_in['sh_up'], 'L0_ffn_sh_down': _L0_ffn_in['sh_down'], 'L0_ffn_sh_gate_w': _L0_ffn_in['sh_gate_w']}

def reference(x, ctx_1024, fside_BxSx2_0, L0_attn_q_w, L0_attn_q_b, L0_attn_k_w, L0_attn_k_b, L0_attn_v_w, L0_attn_v_b, L0_attn_o_w, L0_attn_o_b, L0_xattn_Wq, L0_xattn_Wkv, L0_xattn_Wout, L0_xattn_bout, L0_ffn_router_w, L0_ffn_w_gate, L0_ffn_w_up, L0_ffn_w_down, L0_ffn_sh_gate, L0_ffn_sh_up, L0_ffn_sh_down, L0_ffn_sh_gate_w):
    import jax
    import jax.numpy as jnp

    def _L0_attn_ref(hidden_states, q_w, q_b, k_w, k_b, v_w, v_b, o_w, o_b):
        import jax, jax.numpy as jnp
        import numpy as np
        H = 16
        D_MODEL = 256
        HEAD_DIM = D_MODEL // H
        B, S = (4, 256)
        b, s, _ = hidden_states.shape
        q = (hidden_states @ q_w.T + q_b).reshape(b, s, H, HEAD_DIM)
        k = hidden_states @ k_w.T + k_b
        v = hidden_states @ v_w.T + v_b
        scores = jnp.einsum('bqhd,bkd->bhqk', q, k) / HEAD_DIM ** 0.5
        causal = jnp.triu(jnp.ones((s, s), dtype=bool), k=1)
        scores = jnp.where(causal[None, None], -jnp.inf, scores)
        attn = jax.nn.softmax(scores.astype(jnp.float32), axis=-1).astype(q.dtype)
        out = jnp.einsum('bhqk,bkd->bqhd', attn, v).reshape(b, s, H * HEAD_DIM)
        return out @ o_w.T + o_b

    def _L0_xattn_ref(x, ctx, pos_map, ctx_pos_map, Wq, Wkv, Wout, bout):
        import jax, jax.numpy as jnp
        import numpy as np
        DIM = 256
        CTX_DIM = 128
        N_HEADS = 32
        HEAD_DIM = DIM // N_HEADS
        POS_DIM = 2
        B, N, CTXN = (2, 256, 256)
        ROPE_BASE = 10000.0

        def apply_axial_rope(x, pos):
            b, n, h, d = x.shape
            p = pos.shape[-1]
            dpa = d // p
            half = dpa // 2
            freqs = ROPE_BASE ** (-jnp.arange(half, dtype=x.dtype) / half)
            ang = pos[..., :, None] * freqs
            cos = jnp.cos(ang)[:, :, None, :, :]
            sin = jnp.sin(ang)[:, :, None, :, :]
            xr = x.reshape(b, n, h, p, half, 2)
            x1, x2 = (xr[..., 0], xr[..., 1])
            out = jnp.stack([x1 * cos - x2 * sin, x1 * sin + x2 * cos], axis=-1)
            return out.reshape(b, n, h, d)
        b, n, _ = x.shape
        ctx_n = ctx.shape[1]
        q = (x @ Wq).reshape(b, n, N_HEADS, HEAD_DIM)
        k, v = jnp.split(ctx @ Wkv, 2, axis=-1)
        k = k.reshape(b, ctx_n, N_HEADS, HEAD_DIM)
        v = v.reshape(b, ctx_n, N_HEADS, HEAD_DIM)
        q = apply_axial_rope(q, pos_map)
        k = apply_axial_rope(k, ctx_pos_map)
        scale = 1.0 / np.sqrt(HEAD_DIM).astype(np.float32)
        logits = jnp.einsum('bqhd,bkhd->bhqk', q, k) * scale
        w = jax.nn.softmax(logits, axis=-1)
        attn = jnp.einsum('bhqk,bkhd->bqhd', w, v)
        attn = attn.reshape(b, n, N_HEADS * HEAD_DIM)
        return attn @ Wout + bout

    def _L0_ffn_ref(hidden_states, router_w, w_gate, w_up, w_down, sh_gate, sh_up, sh_down, sh_gate_w):
        import jax, jax.numpy as jnp
        import numpy as np
        B, S, H = (2, 256, 256)
        E, K = (16, 4)
        I_MOE, I_SH = (176, 704)
        orig = hidden_states.shape
        h = hidden_states.reshape(-1, orig[-1])
        N = h.shape[0]
        logits = h @ router_w.T
        probs = jax.nn.softmax(logits.astype(jnp.float32), axis=-1)
        top_vals, top_idx = jax.lax.top_k(probs, K)
        top_vals = top_vals / jnp.maximum(top_vals.sum(-1, keepdims=True), 1e-09)
        top_vals = top_vals.astype(h.dtype)
        comb = jnp.zeros((N, E), h.dtype).at[jnp.arange(N)[:, None], top_idx].add(top_vals)
        g = jnp.einsum('nh,ehi->eni', h, w_gate)
        u = jnp.einsum('nh,ehi->eni', h, w_up)
        y = jnp.einsum('eni,eih->enh', jax.nn.silu(g) * u, w_down)
        routed = jnp.einsum('enh,ne->nh', y, comb)
        shared = jax.nn.silu(h @ sh_gate) * (h @ sh_up) @ sh_down
        sg = jax.nn.sigmoid(h @ sh_gate_w)
        return (routed + sg * shared).reshape(orig)
    x = x + _L0_attn_ref(_layernorm(x, axis=-1), L0_attn_q_w, L0_attn_q_b, L0_attn_k_w, L0_attn_k_b, L0_attn_v_w, L0_attn_v_b, L0_attn_o_w, L0_attn_o_b)
    x = x + _L0_xattn_ref(_layernorm(x, axis=-1), ctx_1024, fside_BxSx2_0, fside_BxSx2_0, L0_xattn_Wq, L0_xattn_Wkv, L0_xattn_Wout, L0_xattn_bout)
    x = x + _L0_ffn_ref(_layernorm(x, axis=-1), L0_ffn_router_w, L0_ffn_w_gate, L0_ffn_w_up, L0_ffn_w_down, L0_ffn_sh_gate, L0_ffn_sh_up, L0_ffn_sh_down, L0_ffn_sh_gate_w)
    return x

_drawn_inputs = setup_inputs


def setup_inputs(seed=0):
    import zlib

    import numpy as np

    out = dict(_drawn_inputs(seed))
    spreads = {'L0_attn_q_b': (0.0, 0.1),
     'L0_attn_k_b': (0.0, 0.1),
     'L0_attn_v_b': (0.0, 0.1),
     'L0_attn_o_b': (0.0, 0.1),
     'L0_xattn_bout': (0.0, 0.1)}
    factors = {}
    for name, (base, spread) in spreads.items():
        noise = np.random.default_rng([zlib.crc32(name.encode()), seed]).standard_normal(out[name].shape)
        drawn = base * np.exp(spread * noise) if base else spread * noise
        out[name] = jnp.asarray(drawn.astype(out[name].dtype))
    for name, factor in factors.items():
        out[name] = (out[name] * factor).astype(out[name].dtype)
    return out
```

```python
from contextlib import ExitStack

import concourse.bass as bass
from concourse import mybir

F32 = mybir.dt.float32
F32R = mybir.dt.float32r
BF16 = mybir.dt.bfloat16
ALU = mybir.AluOpType
ACT = mybir.ActivationFunctionType
AX = mybir.AxisListType

P = 128
NB = 16
D = 256
KC = D // P
UH = 16
HD_A = 16
HD_B = 8
NH_B = 32
CTX = 128
EPS = 1e-5
MASKED = -1e30
SLOTS = 4
MROW = 96
KALL = MROW + 2
STACK_DMAS = 6

NE, TOPK, FE = 16, 4, 176
NSH = 4
FH = (NE + NSH) * FE
TOK = NB * P
TT = 512
NT = TOK // TT
CA, CB = 5, 6
CG = CA + CB
UG = CG * NT
NG = 2
NU = NG * UG + CB * NT
RAW = CB * P
LASTC = FH - (FH // P) * P

FREQ1 = 10000.0 ** -0.5
TWO_PI_HI = 6.28125
TWO_PI_LO = 2 * 3.141592653589793 - 6.28125
ROUND = 1.5 * 2 ** 23
PI_IN = 3.1415925


def need(eng, sem, value):
    if isinstance(value, int) and value <= 0:
        return
    eng.wait_ge(sem, value)


def valid(j, c, n):
    return not isinstance(j, int) or 0 <= 4 * j + c < n


def cap(value, most):
    return min(value, most) if isinstance(value, int) else value


def steps(eng, step, first, looped, last):
    for c in range(first, 1):
        step(0, c)
    with eng.Fori(0, looped) as j:
        for c in range(1, 5):
            step(j, c)
    for c in range(1 + 4 * looped, last + 1):
        step(0, c)


def prepare(nc, io, g, tmp):
    def sb(name, shape, dt=F32):
        return tmp.enter_context(nc.sbuf_tensor(name, shape, dt))

    def sem(name):
        return tmp.enter_context(nc.semaphore(name))

    qo_nat = sb("qo_nat", [P, 2, KC, D])
    kvr_nat = sb("kvr_nat", [NE + 1, 3, D])
    bias_row = sb("bias_row", [1, D + 96])
    qb_dh = sb("qb_dh", [1, D])
    one = sb("one", [1, 1])
    wq_nat = sb("wq_nat", [P, KC, D])
    pos = sb("pos", [P, NB, 2])
    ang = sb("ang", [P, 2, NB, 4])
    turns = sb("turns", [P, 2, NB * 4])
    trig = sb("trig", [P, 2, NB, 4])
    wide = sb("wide", [P, 2, NB, P])
    x, s1, s2, mid, acc = g["x"], g["s1"], g["s2"], g["mid"], g["acc"]
    ident, nident, identb = g["ident"], g["nident"], g["identb"]

    w_in, row_in, pos_in, ob_in, wb_in = (sem(n) for n in ("w_in", "row_in", "pos_in", "ob_in", "wb_in"))
    cleared, built, consts = sem("cleared"), sem("built"), sem("consts")
    wT_done, wT_out, turned, trig_done, widened = (sem(n) for n in ("wT_done", "wT_out", "turned", "trig_done", "widened"))
    tab_done, tab_out, rows_zero, permuted = sem("tab_done"), sem("tab_out"), sem("rows_zero"), sem("permuted")
    turned_row = sem("turned_row")

    with nc.Block() as block:
        @block.sync
        def _(sp):
            for i, name in enumerate(("q_w", "o_w")):
                sp.dma_start(qo_nat[:, i], io[name].rearrange("(r p) n -> p r n", p=P)).then_inc(w_in, 16)
            for i, name in enumerate(("k_w", "v_w", "router_w")):
                sp.dma_start(kvr_nat[0:UH, i], io[name]).then_inc(w_in, 16)
            sp.dma_start(kvr_nat[NE:NE + 1, 2], io["sh_gate_w"].rearrange("k n -> n k")).then_inc(w_in, 16)
            sp.dma_start(pos[:], io["pos"].rearrange("b p c -> p b c")).then_inc(pos_in, 16)
            for n in range(4):
                sp.dma_start(x[:, 4 * n:4 * n + 4, :], io["x"][4 * n:4 * n + 4].rearrange("b p d -> p b d")).then_inc(g["x_in"], 16)
            sp.dma_start(g["ob"][:, 0, :], io["o_b"].rearrange("(a n) -> a n", a=1).partition_broadcast(P)).then_inc(ob_in, 16)
            sp.dma_start(g["ob"][:, 1, :], io["bout"].rearrange("(a n) -> a n", a=1).partition_broadcast(P)).then_inc(ob_in, 16)
            sp.wait_ge(g["x_in"], 64)
            sp.wait_ge(ob_in, 32)

        @block.scalar
        def _(act):
            act.wait_ge(rows_zero, 1)
            act.dma_start(bias_row[:, 0:D], io["q_b"].rearrange("(a n) -> a n", a=1)).then_inc(row_in, 16)
            for r in range(3):
                act.dma_start(bias_row[:, D + 32 * r:D + 32 * r + HD_A], io["k_b"].rearrange("(a n) -> a n", a=1)).then_inc(row_in, 16)
            act.dma_start(g["vb_row"][:], io["v_b"].rearrange("(a n) -> a n", a=1)).then_inc(row_in, 16)
            act.dma_start(wq_nat[:], io["Wq"].rearrange("(k p) n -> p k n", p=P)).then_inc(wb_in, 16)
            act.dma_start(g["wkv"][:], io["Wkv"]).then_inc(wb_in, 16)
            act.dma_start(g["wout"][:], io["Wout"].rearrange("(k p) n -> p k n", p=P)).then_inc(wb_in, 16)
            act.wait_ge(turned, 7)
            nc.scalar.activation(trig[:].rearrange("p s b f -> p (s b f)"), ang[:].rearrange("p s b f -> p (s b f)"),
                                 ACT.Sin).then_inc(trig_done, 1)
            for n in range(8):
                act.wait_ge(tab_done, n + 1)
                nc.scalar.copy(g["rope"][:, n // 4, 4 * (n % 4):4 * (n % 4) + 4, :].rearrange("p b t -> p (b t)"),
                               s2[:, n % 2, 0, :]).then_inc(tab_out, 1)
            act.wait_ge(row_in, 80)
            act.wait_ge(wb_in, 48)

        @block.gpsimd
        def _(pool):
            nc.gpsimd.memset(bias_row[:], 0.0).then_inc(rows_zero, 1)
            nc.gpsimd.memset(ident[:], 0.0).then_inc(cleared, 1)
            nc.gpsimd.memset(nident[:], 0.0).then_inc(cleared, 1)
            nc.gpsimd.memset(g["mask_q"][:], 0.0).then_inc(cleared, 1)
            nc.gpsimd.memset(g["mask_k"][:], 0.0).then_inc(cleared, 1)
            pool.wait_ge(cleared, 4)
            for t, v in ((ident, 1.0), (nident, -1.0)):
                nc.gpsimd.affine_select(out=t[:], in_=t[:], compare_op=ALU.not_equal, fill=v, base=0,
                                        pattern=[[-1, P]], channel_multiplier=1).then_inc(built, 1)
            nc.gpsimd.affine_select(out=g["mask_q"][:], in_=g["mask_q"][:], compare_op=ALU.is_ge, fill=MASKED, base=0,
                                    pattern=[[0, 4], [-1, P]], channel_multiplier=1).then_inc(built, 1)
            nc.gpsimd.affine_select(out=g["mask_k"][:], in_=g["mask_k"][:], compare_op=ALU.is_ge, fill=MASKED, base=0,
                                    pattern=[[0, 4], [1, P]], channel_multiplier=-1).then_inc(built, 1)
            pool.wait_ge(built, 1)
            nc.gpsimd.tensor_copy(identb[:], ident[:]).then_inc(built, 1)
            nc.gpsimd.memset(g["ln_eps"][:], EPS).then_inc(built, 1)
            nc.gpsimd.memset(g["zero"][:], 0.0).then_inc(built, 1)
            nc.gpsimd.memset(g["ln_pow"][:], -0.5).then_inc(built, 1)
            nc.gpsimd.memset(g["ones_row"][:], 1.0).then_inc(built, 1)

        @block.vector
        def _(dve):
            nc.vector.memset(one[:], 1.0).then_inc(consts, 1)
            nc.vector.memset(g["wkT"][:], 0.0).then_inc(consts, 1)
            dve.wait_ge(row_in, 80)
            nc.vector.tensor_copy(qb_dh[:].rearrange("p (d h) -> p h d", h=UH), bias_row[:, 0:D].rearrange("p (h d) -> p h d", d=HD_A)).then_inc(turned_row, 1)
            dve.wait_ge(pos_in, 16)
            av = ang[:].rearrange("p s b (c f) -> p s b c f", f=2)
            nc.vector.tensor_copy(av[:, 0, :, :, 0], pos[:]).then_inc(turned, 1)
            nc.vector.tensor_scalar(av[:, 0, :, :, 1], pos[:], FREQ1, None, ALU.mult).then_inc(turned, 1)
            dve.wait_ge(turned, 2)
            af = ang[:].rearrange("p s b f -> p s (b f)")
            nc.vector.tensor_scalar(af[:, 1, :], af[:, 0, :], 3.141592653589793 / 2, None, ALU.add).then_inc(turned, 1)
            dve.wait_ge(turned, 3)
            nc.vector.tensor_scalar(turns[:], af, 1 / (2 * 3.141592653589793), ROUND, ALU.mult, ALU.add).then_inc(turned, 1)
            dve.wait_ge(turned, 4)
            nc.vector.tensor_scalar(turns[:], turns[:], ROUND, None, ALU.subtract).then_inc(turned, 1)
            dve.wait_ge(turned, 5)
            a1, t1 = (v.rearrange("p s b f -> p (s b f)") if v is not turns else v for v in (ang[:], turns))
            tf = turns[:].rearrange("p s n -> p (s n)")
            nc.vector.scalar_tensor_tensor(a1, tf, -TWO_PI_HI, a1, ALU.mult, ALU.add).then_inc(turned, 1)
            dve.wait_ge(turned, 6)
            nc.vector.scalar_tensor_tensor(a1, tf, -TWO_PI_LO, a1, ALU.mult, ALU.add).then_inc(consts, 1)
            dve.wait_ge(consts, 3)
            nc.vector.tensor_scalar(a1, a1, PI_IN, -PI_IN, ALU.min, ALU.max).then_inc(turned, 1)
            dve.wait_ge(wb_in, 48)
            for half in range(2):
                for k in range(KC):
                    nc.vector.tensor_copy(g["wqB"][:, k, half, :].rearrange("p (c f h) -> p h f c", c=2, f=4),
                                          wq_nat[:, k, P * half:P * half + P].rearrange("p (h f c) -> p h f c", h=UH, f=4)).then_inc(permuted, 1)
                nc.vector.tensor_copy(g["wkB"][:, half, :].rearrange("p (c f h) -> p h f c", c=2, f=4),
                                      g["wkv"][:, P * half:P * half + P].rearrange("p (h f c) -> p h f c", h=UH, f=4)).then_inc(permuted, 1)
            dve.wait_ge(wT_done, 1)
            for k in range(KC):
                for r in range(2):
                    nc.vector.tensor_copy(g["wqT"][:, k, :].rearrange("p (d h) -> p h d", h=UH)[:, 8 * r:8 * r + 8, :],
                                          s1[:, 0, P * (2 * k + r):P * (2 * k + r) + P].rearrange("p (h d) -> p h d", d=HD_A)).then_inc(wT_out, 1)
            dve.wait_ge(wT_done, 2)
            nc.vector.tensor_copy(g["woT"][:].rearrange("p k n -> p (k n)"), s1[:, 1, :]).then_inc(wT_out, 1)
            dve.wait_ge(wT_done, 3)
            small = mid[:, 0:192].rearrange("p (w k n) -> p w k n", w=3, k=KC)
            for r in range(3):
                nc.vector.tensor_copy(g["wkT"][:, :, 32 * r:32 * r + HD_A], small[:, 0, :, 0:HD_A]).then_inc(wT_out, 1)
            nc.vector.tensor_copy(g["wvT"][:], small[:, 1, :, 0:HD_A]).then_inc(wT_out, 1)
            nc.vector.tensor_copy(g["wr"][:], small[:, 2, :, 0:NE + 1]).then_inc(wT_out, 1)
            dve.wait_ge(wT_done, 4)
            nc.vector.tensor_copy(g["qkb"][:, 0:2], acc[:, 0:2]).then_inc(wT_out, 1)
            nc.vector.tensor_copy(g["qkb"][0:96, 2:3], acc[0:96, 2:3]).then_inc(wT_out, 1)
            dve.wait_ge(trig_done, 1)
            for s in range(2):
                for c in range(2):
                    for b in range(0, NB, 8):
                        src = trig[:, s, b:b + 8, :].rearrange("p b f -> p (b f)").unsqueeze(2).broadcast_to([P, 32, UH])
                        dst = wide[:, s, b:b + 8, 64 * c:64 * c + 64].rearrange("p b (f h) -> p b f h", h=UH)
                        for bb in range(8):
                            last = nc.vector.tensor_scalar(dst[:, bb], src[:, 4 * bb:4 * bb + 4, :], -1.0 if (s, c) == (0, 0) else 1.0, None, ALU.mult)
                            last.then_inc(widened, 1)

        @block.tensor
        def _(pe):
            pe.wait_ge(built, 2)
            pe.wait_ge(w_in, 96)
            for i in range(2):
                for k in range(KC):
                    for r in range(2):
                        last = nc.tensor.transpose(s1[:, i, P * (2 * k + r):P * (2 * k + r) + P], qo_nat[:, i, r, P * k:P * k + P], ident[:])
                last.then_inc(wT_done, 1)
            for w in range(3):
                for k in range(KC):
                    n = NE + 1 if w == 2 else UH
                    last = nc.tensor.transpose(mid[:, 64 * w + 32 * k:64 * w + 32 * k + n], kvr_nat[0:n, w, P * k:P * k + P], ident[0:n, 0:n])
            last.then_inc(wT_done, 1)
            pe.wait_ge(row_in, 80)
            pe.wait_ge(consts, 1)
            pe.wait_ge(turned_row, 1)
            for c in range(2):
                nc.tensor.matmul(acc[:, c:c + 1], qb_dh[:, P * c:P * c + P], one[:], start=True, stop=True)
            nc.tensor.matmul(acc[0:96, 2:3], bias_row[:, D:D + 96], one[:], start=True, stop=True).then_inc(wT_done, 1)
            for n in range(8):
                pe.wait_ge(widened, 2 * NB * (n // 4 + 1))
                need(pe, tab_out, n - 1)
                for q in range(4):
                    last = nc.tensor.transpose(s2[:, n % 2, 0, P * q:P * q + P], wide[:, n // 4, 4 * (n % 4) + q, :], ident[:])
                last.then_inc(tab_done, 1)


def self_attention(nc, g, tmp):
    def sb(name, shape, dt=F32):
        return tmp.enter_context(nc.sbuf_tensor(name, shape, dt))

    def sem(name):
        return tmp.enter_context(nc.semaphore(name))

    x, s1, s2, mid, acc = g["x"], g["s1"], g["s2"], g["mid"], g["acc"]
    qs = sb("qs", [KALL, SLOTS, UH, P], F32R)
    ks = sb("ks", [KALL, SLOTS, P], F32R)
    v = sb("v", [P, SLOTS, HD_A + 1])
    stats = sb("stats", [P, SLOTS, 6])
    mv = sb("mv", [P, SLOTS, 2])
    rstd = sb("rstd", [P, SLOTS, 2])
    xn = sb("xn", [P, 2, D])
    xnT = sb("xnT", [P, 2, KC, P])
    qf = sb("qf", [P, 2, KC, P])
    qhi = sb("qhi", [P, 2, KC, P], F32R)
    qlo = sb("qlo", [P, 2, KC, P], F32R)
    kf = sb("kf", [96, 2, P])
    mx = sb("mx", [P, UH])
    mxs = sb("mxs", [P, 2, 2, UH])
    mT = sb("mT", [32, 2, P], F32R)
    pt = sb("pt", [P, 2, 8, P])
    rc = sb("rc", [P, UH])
    o = sb("o", [P, 2, D])
    oT = sb("oT", [P, 2, KC, P])

    stack_in = [sem(f"stack_in{i}") for i in range(SLOTS)]
    mrow_in = [sem(f"mrow_in{i}") for i in range(SLOTS)]
    (init, ln_stats, ln_aggr, eps_done, rstd_done, xn_done, trx_done, xnT_done, proj_done, qkv_out, q_hi, q_split,
     k_hi, ks_done, ob_added, s1_done, max_done, mx_hi, mx_split, mT_done, mT_out, s2_done, exp_done, pv_done, rc_done,
     o_normed, trO_done, oT_done, out_done, x_added) = (sem("a_" + n) for n in (
        "init", "ln_stats", "ln_aggr", "eps_done", "rstd_done", "xn_done", "trx_done", "xnT_done", "proj_done", "qkv_out",
        "q_hi", "q_split", "k_hi", "ks_done", "ob_added", "s1_done", "max_done", "mx_hi", "mx_split", "mT_done", "mT_out",
        "s2_done", "exp_done", "pv_done", "rc_done", "o_normed", "trO_done", "oT_done", "out_done", "x_added"))
    AHEAD = 3

    def at(j, c):
        return 4 * j + c, c % SLOTS, j + c // SLOTS

    with nc.Block() as block:
        @block.sync
        def _(sp):
            sp.wait_ge(init, 3)

            def step(j, c):
                if valid(j, c + 1, NB):
                    b, s, r = at(j, c + 1)
                    sp.wait_ge(mT_out, b + 1)
                    sp.dma_start(qs[MROW:KALL, s].bitcast(F32), mT[:, s % 2, :].bitcast(F32)).then_inc(mrow_in[s], 16)
                if valid(j, c + AHEAD, NB):
                    b, s, r = at(j, c + AHEAD)
                    sp.wait_ge(q_split, b + 1)
                    need(sp, s2_done, 2 * b - 6)
                    for row, part in ((0, qhi), (32, qhi), (64, qlo)):
                        for k in range(KC):
                            sp.dma_start(qs[row + 8 * k:row + 8 * k + 8, s].bitcast(F32),
                                         part[:, s % 2, k, :].bitcast(F32)).then_inc(stack_in[s], 16)

            steps(sp, step, -AHEAD, 3, NB)

        @block.gpsimd
        def _(pool):
            nc.gpsimd.memset(v[:], 1.0).then_inc(init, 1)

            def step(j, c):
                if not valid(j, c + AHEAD, NB):
                    return
                b, s, r = at(j, c + AHEAD)
                p = s % 2
                pool.wait_ge(ln_aggr, b + 1)
                nc.gpsimd.tensor_tensor(rstd[:, s, 0:1], mv[:, s, 1:2], g["ln_eps"][:, 0:1], ALU.add).then_inc(eps_done, 1)
                pool.wait_ge(eps_done, b + 1)
                nc.gpsimd.tensor_tensor(rstd[:, s, 1:2], rstd[:, s, 0:1], g["ln_pow"][:, 0:1], ALU.pow).then_inc(rstd_done, 1)
                pool.wait_ge(xn_done, b + 1)
                nc.gpsimd.tensor_tensor(x[:, b, :], x[:, b, :], g["ob"][:, 0, :], ALU.add).then_inc(ob_added, 1)
                pool.wait_ge(qkv_out, b + 1)
                if not (isinstance(b, int) and b < 2):
                    _, s_2, r_2 = at(j, c + AHEAD - 2)
                    pool.wait_ge(stack_in[s_2], 16 * STACK_DMAS * (r_2 + 1))
                nc.gpsimd.tensor_tensor(qhi[:, p].rearrange("p k t -> p (k t)"), qf[:, p].rearrange("p k t -> p (k t)"), g["zero"][:, 0:1].broadcast_to([P, D]), ALU.add).then_inc(q_hi, 1)
                pool.wait_ge(q_hi, b + 1)
                nc.gpsimd.tensor_tensor(qlo[:, p], qf[:, p], qhi[:, p].bitcast(F32), ALU.subtract).then_inc(q_split, 1)
                need(pool, s2_done, 2 * b - 6)
                nc.gpsimd.tensor_tensor(ks[0:96, s], kf[:, p], g["zero"][0:96, 0:1].broadcast_to([96, P]), ALU.add).then_inc(k_hi, 1)

            steps(pool, step, -AHEAD, 3, NB)

        @block.vector
        def _(dve):
            nc.vector.memset(qs[:].bitcast(F32), 0.0).then_inc(init, 1)
            nc.vector.memset(ks[:].bitcast(F32), 1.0).then_inc(init, 1)

            def step(j, c):
                ahead, p1, p2, done = (valid(j, c + d, NB) for d in (AHEAD, 1, 0, -1))
                b, s, r = at(j, c + AHEAD)
                b1, sl1, _ = at(j, c + 1)

                def row_max(n):
                    if p1:
                        dve.wait_ge(s1_done, 4 * b1 + n + 1)
                        nc.vector.tensor_reduce(mx[:, 4 * n:4 * n + 4], s1[:, n % 2, :].rearrange("p (h k) -> p h k", h=4),
                                                AX.X, ALU.max).then_inc(max_done, 1)

                if ahead:
                    nc.vector.bn_stats(stats[:, s, :], x[:, b, :]).then_inc(ln_stats, 1)
                row_max(0)
                if ahead:
                    dve.wait_ge(ln_stats, b + 1)
                row_max(1)
                if ahead:
                    nc.vector.bn_aggr(mv[:, s, :], stats[:, s, :]).then_inc(ln_aggr, 1)
                if ahead:
                    dve.wait_ge(rstd_done, b + 1)
                    need(dve, trx_done, b - 1)
                    nc.vector.tensor_scalar(xn[:, s % 2, :], x[:, b, :], mv[:, s, 0:1], rstd[:, s, 1:2],
                                            ALU.subtract, ALU.mult).then_inc(xn_done, 1)
                row_max(2)
                if done:
                    b0, _, _ = at(j, c - 1)
                    dve.wait_ge(out_done, b0 + 1)
                    dve.wait_ge(ob_added, b0 + 1)
                    nc.vector.tensor_tensor(x[:, b0, :], mid[:, 0:D], x[:, b0, :], ALU.add).then_inc(x_added, 1)
                row_max(3)
                if p1:
                    dve.wait_ge(max_done, 4 * b1 + 4)
                    need(dve, mT_done, b1 - 1)
                    nc.vector.tensor_copy(mxs[:, sl1 % 2, 0, :].bitcast(F32R), mx[:]).then_inc(mx_hi, 1)
                    dve.wait_ge(mx_hi, b1 + 1)
                    nc.vector.tensor_tensor(mxs[:, sl1 % 2, 1, :], mx[:], mxs[:, sl1 % 2, 0, :], ALU.subtract).then_inc(mx_split, 1)
                if p2:
                    bb, sl, _ = at(j, c)
                    dve.wait_ge(pv_done, 2 * bb + 2)
                    pv = acc[:, 0:UH * (HD_A + 1)].rearrange("p (h d) -> p h d", h=UH)
                    nc.vector.reciprocal(rc[:], pv[:, :, HD_A]).then_inc(rc_done, 1)
                    dve.wait_ge(rc_done, bb + 1)
                    nc.vector.tensor_tensor(o[:, sl % 2, :].rearrange("p (h d) -> p h d", h=UH), pv[:, :, 0:HD_A],
                                            rc[:].unsqueeze(2).broadcast_to([P, UH, HD_A]), ALU.mult).then_inc(o_normed, 1)
                if ahead:
                    dve.wait_ge(k_hi, b + 1)
                    nc.vector.tensor_tensor(ks[32:64, s], kf[32:64, s % 2], ks[32:64, s].bitcast(F32), ALU.subtract).then_inc(ks_done, 1)

            steps(dve, step, -AHEAD, 3, NB)

        @block.scalar
        def _(act):
            def step(j, c):
                def exps(u):
                    if valid(j, c, NB):
                        b, s, _ = at(j, c)
                        act.wait_ge(s2_done, 2 * b + u + 1)
                        need(act, pv_done, 2 * b + u - 1)
                        nc.scalar.activation(pt[:, u].rearrange("p h q -> p (h q)"), s2[:, u].rearrange("p a n -> p (a n)"),
                                             ACT.Exp, scale=HD_A ** -0.5).then_inc(exp_done, 1)

                exps(0)
                if valid(j, c - 1, NB):
                    b, s, _ = at(j, c - 1)
                    act.wait_ge(trO_done, b + 1)
                    nc.scalar.copy(oT[:, s % 2].rearrange("p k t -> p (k t)"), mid[:, 0:D]).then_inc(oT_done, 1)
                exps(1)
                if valid(j, c + AHEAD, NB):
                    b, s, _ = at(j, c + AHEAD)
                    p = s % 2
                    act.wait_ge(trx_done, b + 1)
                    nc.scalar.copy(xnT[:, p].rearrange("p k t -> p (k t)"), mid[:, 0:D]).then_inc(xnT_done, 1)
                    act.wait_ge(proj_done, b + 1)
                    need(act, q_split, b - 1)
                    need(act, ks_done, b - 1)
                    if isinstance(b, int) and b == 0:
                        act.wait_ge(init, 3)
                    for k in range(KC):
                        nc.scalar.activation(qf[:, p, k, :], mid[:, P * k:P * k + P], ACT.Identity, bias=g["qkb"][:, k:k + 1])
                    nc.scalar.activation(kf[:, p, :], mid[0:96, 256:384], ACT.Identity, bias=g["qkb"][0:96, 2:3])
                    nc.scalar.copy(v[:, s, 0:HD_A], mid[:, 384:400]).then_inc(qkv_out, 1)
                if valid(j, c + 1, NB):
                    b, s, _ = at(j, c + 1)
                    act.wait_ge(mT_done, b + 1)
                    if not (isinstance(b, int) and b < 2):
                        _, s_2, r_2 = at(j, c - 1)
                        act.wait_ge(mrow_in[s_2], 16 * (r_2 + 1))
                    nc.scalar.copy(mT[:, s % 2, :], mid[0:32, 0:P]).then_inc(mT_out, 1)

            steps(act, step, -AHEAD, 3, NB)

        @block.tensor
        def _(pe):
            def step(j, c):
                b1, sl1, r1 = at(j, c + 1)
                b2, sl2, r2 = at(j, c)
                b0, sl0, _ = at(j, c - 1)
                b3, sl3, _ = at(j, c + AHEAD)
                ahead, p1, p2, done = (valid(j, c + d, NB) for d in (AHEAD, 1, 0, -1))

                def scores(n):
                    if not p1:
                        return
                    if n == 0:
                        pe.wait_ge(stack_in[sl1], 16 * STACK_DMAS * (r1 + 1))
                        pe.wait_ge(ks_done, b1 + 1)
                    need(pe, max_done, 4 * b1 + n - 1)
                    nc.tensor.matmul(s1[:, n % 2, :], g["identb"][:], g["mask_q"][:], start=True, stop=False)
                    for h in range(4):
                        last = nc.tensor.matmul(s1[:, n % 2, P * h:P * h + P], qs[0:MROW, sl1, 4 * n + h, :], ks[0:MROW, sl1, :],
                                                start=False, stop=(h == 3))
                    last.then_inc(s1_done, 1)

                def shifted(u):
                    if not p2:
                        return
                    if u == 0:
                        pe.wait_ge(mrow_in[sl2], 16 * (r2 + 1))
                    need(pe, exp_done, 2 * b2 + u - 1)
                    for q in range(2):
                        nc.tensor.matmul(s2[:, u, q, :], g["identb"][:], g["mask_k"][:], start=True, stop=False)
                        last = nc.tensor.matmul(s2[:, u, q, :], ks[:, sl2, :], qs[:, sl2, 8 * u + 4 * q:8 * u + 4 * q + 4, :],
                                                start=False, stop=True)
                    last.then_inc(s2_done, 1)

                def values(u):
                    if not p2:
                        return
                    pe.wait_ge(exp_done, 2 * b2 + u + 1)
                    if u == 0:
                        need(pe, o_normed, b2)
                    for h in range(8):
                        col = (8 * u + h) * (HD_A + 1)
                        last = nc.tensor.matmul(acc[:, col:col + HD_A + 1], pt[:, u, h, :], v[:, sl2, :], start=True, stop=True)
                    last.then_inc(pv_done, 1)

                scores(0)
                shifted(0)
                scores(1)
                if done:
                    pe.wait_ge(o_normed, b0 + 1)
                    pe.wait_ge(mT_out, cap(b0 + 2, NB))
                    for k in range(KC):
                        last = nc.tensor.transpose(mid[:, P * k:P * k + P], o[:, sl0 % 2, P * k:P * k + P], g["ident"][:])
                    last.then_inc(trO_done, 1)
                scores(2)
                shifted(1)
                if done:
                    pe.wait_ge(oT_done, b0 + 1)
                    for k in range(KC):
                        last = nc.tensor.matmul(mid[:, 0:D], oT[:, sl0 % 2, k, :], g["woT"][:, k, :], start=(k == 0), stop=(k == KC - 1))
                    last.then_inc(out_done, 1)
                scores(3)
                values(0)
                if ahead:
                    pe.wait_ge(xn_done, b3 + 1)
                    need(pe, qkv_out, b3)
                    need(pe, mT_out, b3 - 2)
                    need(pe, x_added, b3 - 3)
                    for k in range(KC):
                        last = nc.tensor.transpose(mid[:, P * k:P * k + P], xn[:, sl3 % 2, P * k:P * k + P], g["ident"][:])
                    last.then_inc(trx_done, 1)
                values(1)
                if ahead:
                    pe.wait_ge(xnT_done, b3 + 1)
                    for m in range(2):
                        for k in range(KC):
                            nc.tensor.matmul(mid[:, P * m:P * m + P], g["wqT"][:, k, P * m:P * m + P], xnT[:, sl3 % 2, k, :],
                                             start=(k == 0), stop=(k == KC - 1))
                    for k in range(KC):
                        nc.tensor.matmul(mid[0:96, 256:384], g["wkT"][:, k, :], xnT[:, sl3 % 2, k, :], start=(k == 0), stop=(k == KC - 1))
                    for k in range(KC):
                        nc.tensor.matmul(mid[:, 384:400], xnT[:, sl3 % 2, k, :], g["wvT"][:, k, :], start=(k == 0), stop=False)
                    nc.tensor.matmul(mid[:, 384:400], g["ones_row"][:], g["vb_row"][:], start=False, stop=True).then_inc(proj_done, 1)
                if p1:
                    pe.wait_ge(mx_split, b1 + 1)
                    pe.wait_ge(qkv_out, cap(b1 + 3, NB))
                    if not ahead:
                        need(pe, x_added, cap(b1 - 1, NB))
                    nc.tensor.matmul(mid[0:32, 0:P], mxs[:, sl1 % 2].rearrange("p a h -> p (a h)"), g["nident"][:],
                                     start=True, stop=True).then_inc(mT_done, 1)

            steps(pe, step, -AHEAD, 3, NB)


def cross_attention(nc, io, g, tmp):
    def sb(name, shape, dt=F32):
        return tmp.enter_context(nc.sbuf_tensor(name, shape, dt))

    def sem(name):
        return tmp.enter_context(nc.semaphore(name))

    x, s1, s2, mid, acc = g["x"], g["s1"], g["s2"], g["mid"], g["acc"]
    NUNIT = 2 * NB
    QK = 4 * P
    qs = sb("b_qs", [KALL, SLOTS, UH, P], F32R)
    ks = sb("b_ks", [KALL, SLOTS, UH, P], F32R)
    v = sb("b_v", [P, 2, NH_B, HD_B + 1])
    stats = sb("b_stats", [P, 2, 6])
    mv = sb("b_mv", [P, 2, 2])
    rstd = sb("b_rstd", [P, 2, 2])
    xn = sb("b_xn", [P, 2, D])
    ctx = sb("b_ctx", [P, 2, CTX])
    xcT = sb("b_xcT", [P, 2, KC + 1, P])
    swapped = sb("b_swapped", [P, QK])
    by_cos = sb("b_by_cos", [P, QK])
    by_sin = sb("b_by_sin", [P, QK])
    qkhi = sb("b_qkhi", [P, 2, 2, 2, P], F32R)
    qklo = sb("b_qklo", [P, 2, 2, 2, P], F32R)
    mx = sb("b_mx", [P, UH])
    mxs = sb("b_mxs", [P, 2, 2, UH])
    mT = sb("b_mT", [32, 2, P], F32R)
    pt = sb("b_pt", [P, 2, 8, P])
    rc = sb("b_rc", [P, UH])
    o = sb("b_o", [P, 2, D])
    oT = sb("b_oT", [P, 2, KC, P])

    stack_in = [sem(f"b_stack_in{i}") for i in range(SLOTS)]
    mrow_in = [sem(f"b_mrow_in{i}") for i in range(SLOTS)]
    ctx_in = [sem(f"ctx_in{i}") for i in range(2)]
    (init, ln_stats, ln_aggr, eps_done, rstd_done, xn_done, trx_done, xcT_done, qk_done, qk_swapped, qk_out, sin_done,
     turned, qk_hi, qk_lo, ob_added, v_done, v_out, s1_done, max_done, mx_hi, mx_split, mT_done, mT_out, s2_done, exp_done,
     pv_done, rc_done, o_normed, trO_done, oT_done, out_done, x_added) = (sem("b_s_" + n) for n in (
        "init", "ln_stats", "ln_aggr", "eps_done", "rstd_done", "xn_done", "trx_done", "xcT_done", "qk_done", "qk_swapped",
        "qk_out", "sin_done", "turned", "qk_hi", "qk_lo", "ob_added", "v_done", "v_out", "s1_done", "max_done", "mx_hi",
        "mx_split", "mT_done", "mT_out", "s2_done", "exp_done", "pv_done", "rc_done", "o_normed", "trO_done", "oT_done",
        "out_done", "x_added"))
    AHEAD = 3
    HALF_DMAS = 2 * 3

    def at(j, c):
        return 4 * j + c, c % SLOTS, j + c // SLOTS

    def batch(j, c):
        return 2 * j + c // 2, (c // 2) % 2

    def has(j, c):
        return valid(j, c, NUNIT)

    with nc.Block() as block:
        @block.sync
        def _(sp):
            sp.wait_ge(init, 3)

            def step(j, c):
                if c % 2 and has(j, c + AHEAD):
                    b, p = batch(j, c + AHEAD)
                    need(sp, trx_done, b - 1)
                    sp.dma_start(ctx[:, p, :], io["ctx"][b]).then_inc(ctx_in[p], 16)
                if has(j, c + 1):
                    b, s, r = at(j, c + 1)
                    sp.wait_ge(mT_out, b + 1)
                    sp.dma_start(qs[MROW:KALL, s].bitcast(F32), mT[:, s % 2, :].bitcast(F32)).then_inc(mrow_in[s], 16)
                if has(j, c + 2):
                    b, s, r = at(j, c + 2)
                    half = c % 2
                    bt, par = batch(j, c + 2 - half)
                    sp.wait_ge(qk_lo, bt + 1)
                    need(sp, s2_done, 2 * b - 6)
                    for dst, w, parts in ((qs, 0, (qkhi, qkhi, qklo)), (ks, 1, (qkhi, qklo, qkhi))):
                        for n in range(3):
                            sp.dma_start(dst[8 * n:8 * n + 8, s].bitcast(F32),
                                         parts[n][:, par, w, half, :].bitcast(F32)).then_inc(stack_in[s], 16)

            steps(sp, step, -AHEAD, 7, NUNIT)

        @block.gpsimd
        def _(pool):
            nc.gpsimd.memset(v[:], 1.0).then_inc(init, 1)

            def step(j, c):
                if c % 2 == 0 or not has(j, c + AHEAD):
                    return
                b, p = batch(j, c + AHEAD)
                pool.wait_ge(ln_aggr, b + 1)
                nc.gpsimd.tensor_tensor(rstd[:, p, 0:1], mv[:, p, 1:2], g["ln_eps"][:, 0:1], ALU.add).then_inc(eps_done, 1)
                pool.wait_ge(eps_done, b + 1)
                nc.gpsimd.tensor_tensor(rstd[:, p, 1:2], rstd[:, p, 0:1], g["ln_pow"][:, 0:1], ALU.pow).then_inc(rstd_done, 1)
                pool.wait_ge(xn_done, b + 1)
                nc.gpsimd.tensor_tensor(x[:, b, :], x[:, b, :], g["ob"][:, 1, :], ALU.add).then_inc(ob_added, 1)
                pool.wait_ge(qk_swapped, b + 1)
                need(pool, turned, b)
                nc.gpsimd.tensor_tensor(by_sin[:].rearrange("p (a t) -> p a t", a=4), swapped[:].rearrange("p (a t) -> p a t", a=4),
                                        g["rope"][:, 0, b, :].unsqueeze(1).broadcast_to([P, 4, P]), ALU.mult).then_inc(sin_done, 1)
                pool.wait_ge(qk_hi, b + 1)
                nc.gpsimd.tensor_tensor(qklo[:, p].rearrange("p a b t -> p (a b t)"), by_cos[:],
                                        qkhi[:, p].rearrange("p a b t -> p (a b t)").bitcast(F32), ALU.subtract).then_inc(qk_lo, 1)

            steps(pool, step, -AHEAD, 7, NUNIT)

        @block.vector
        def _(dve):
            nc.vector.memset(qs[:].bitcast(F32), 0.0).then_inc(init, 1)
            nc.vector.memset(ks[0:MROW].bitcast(F32), 0.0)
            nc.vector.memset(ks[MROW:KALL].bitcast(F32), 1.0).then_inc(init, 1)

            def step(j, c):
                ahead = c % 2 == 1 and has(j, c + AHEAD)
                b, p = batch(j, c + AHEAD) if c % 2 else (0, 0)
                p1, p2 = has(j, c + 1), has(j, c)
                b1, sl1, _ = at(j, c + 1)

                def row_max(n):
                    if p1:
                        dve.wait_ge(s1_done, 4 * b1 + n + 1)
                        nc.vector.tensor_reduce(mx[:, 4 * n:4 * n + 4], s1[:, n % 2, :].rearrange("p (h k) -> p h k", h=4),
                                                AX.X, ALU.max).then_inc(max_done, 1)

                if ahead:
                    nc.vector.bn_stats(stats[:, p, :], x[:, b, :]).then_inc(ln_stats, 1)
                    dve.wait_ge(ln_stats, b + 1)
                row_max(0)
                if ahead:
                    nc.vector.bn_aggr(mv[:, p, :], stats[:, p, :]).then_inc(ln_aggr, 1)
                row_max(1)
                if ahead:
                    dve.wait_ge(rstd_done, b + 1)
                    need(dve, trx_done, b - 1)
                    nc.vector.tensor_scalar(xn[:, p, :], x[:, b, :], mv[:, p, 0:1], rstd[:, p, 1:2],
                                            ALU.subtract, ALU.mult).then_inc(xn_done, 1)
                row_max(2)
                if c % 2 == 0 and has(j, c - 1):
                    b0, _ = batch(j, c - 2)
                    dve.wait_ge(out_done, b0 + 1)
                    dve.wait_ge(ob_added, b0 + 1)
                    nc.vector.tensor_tensor(x[:, b0, :], mid[:, 0:D], x[:, b0, :], ALU.add).then_inc(x_added, 1)
                row_max(3)
                if p1:
                    dve.wait_ge(max_done, 4 * b1 + 4)
                    need(dve, mT_done, b1 - 1)
                    nc.vector.tensor_copy(mxs[:, sl1 % 2, 0, :].bitcast(F32R), mx[:]).then_inc(mx_hi, 1)
                    dve.wait_ge(mx_hi, b1 + 1)
                    nc.vector.tensor_tensor(mxs[:, sl1 % 2, 1, :], mx[:], mxs[:, sl1 % 2, 0, :], ALU.subtract).then_inc(mx_split, 1)
                if ahead:
                    dve.wait_ge(qk_swapped, b + 1)
                    need(dve, qk_lo, b)
                    nc.vector.tensor_tensor(by_cos[:].rearrange("p (a t) -> p a t", a=4), mid[:].rearrange("p (a t) -> p a t", a=4),
                                            g["rope"][:, 1, b, :].unsqueeze(1).broadcast_to([P, 4, P]), ALU.mult).then_inc(qk_out, 1)
                if p2:
                    bb, sl, _ = at(j, c)
                    half = c % 2
                    bt, par = batch(j, c - half)
                    dve.wait_ge(pv_done, 2 * bb + 2)
                    pv = acc[:, 0:UH * (HD_B + 1)].rearrange("p (h d) -> p h d", h=UH)
                    nc.vector.reciprocal(rc[:], pv[:, :, HD_B]).then_inc(rc_done, 1)
                    dve.wait_ge(rc_done, bb + 1)
                    nc.vector.tensor_tensor(o[:, par, P * half:P * half + P].rearrange("p (h d) -> p h d", h=UH), pv[:, :, 0:HD_B],
                                            rc[:].unsqueeze(2).broadcast_to([P, UH, HD_B]), ALU.mult).then_inc(o_normed, 1)
                if ahead:
                    dve.wait_ge(sin_done, b + 1)
                    dve.wait_ge(qk_out, b + 1)
                    nc.vector.tensor_tensor(by_cos[:], by_cos[:], by_sin[:], ALU.add).then_inc(turned, 1)

            steps(dve, step, -AHEAD, 7, NUNIT)

        @block.scalar
        def _(act):
            def step(j, c):
                def exps(u):
                    if has(j, c):
                        b, s, _ = at(j, c)
                        act.wait_ge(s2_done, 2 * b + u + 1)
                        need(act, pv_done, 2 * b + u - 1)
                        nc.scalar.activation(pt[:, u].rearrange("p h q -> p (h q)"), s2[:, u].rearrange("p a n -> p (a n)"),
                                             ACT.Exp, scale=HD_B ** -0.5).then_inc(exp_done, 1)

                if c % 2 == 0 and has(j, c + 2):
                    b, p = batch(j, c + 2)
                    act.wait_ge(turned, b + 1)
                    if not (isinstance(b, int) and b < 2):
                        _, s_2, r_2 = at(j, c - 1)
                        act.wait_ge(stack_in[s_2], 16 * HALF_DMAS * (r_2 + 1))
                    nc.scalar.copy(qkhi[:, p].rearrange("p a b t -> p (a b t)"), by_cos[:]).then_inc(qk_hi, 1)
                exps(0)
                if c % 2 == 0 and has(j, c - 1):
                    b, p = batch(j, c - 2)
                    act.wait_ge(trO_done, b + 1)
                    nc.scalar.copy(oT[:, p].rearrange("p k t -> p (k t)"), mid[:, 0:D]).then_inc(oT_done, 1)
                exps(1)
                if c % 2 == 1 and has(j, c + AHEAD):
                    b, p = batch(j, c + AHEAD)
                    act.wait_ge(trx_done, b + 1)
                    nc.scalar.copy(xcT[:, p].rearrange("p k t -> p (k t)"), mid[:, 0:3 * P]).then_inc(xcT_done, 1)
                    act.wait_ge(qk_done, b + 1)
                    need(act, sin_done, b)
                    nc.scalar.copy(swapped[0:64, :], mid[64:P, :])
                    nc.scalar.copy(swapped[64:P, :], mid[0:64, :]).then_inc(qk_swapped, 1)
                if c % 2 == 0 and has(j, c + 2):
                    b, p = batch(j, c + 2)
                    act.wait_ge(v_done, b + 1)
                    if isinstance(b, int) and b == 0:
                        act.wait_ge(init, 3)
                    nc.scalar.copy(v[:, p, :, 0:HD_B], mid[:, 0:D].rearrange("p (h d) -> p h d", h=NH_B)).then_inc(v_out, 1)
                if has(j, c + 1):
                    b, s, _ = at(j, c + 1)
                    act.wait_ge(mT_done, b + 1)
                    if not (isinstance(b, int) and b < 2):
                        _, s_2, r_2 = at(j, c - 1)
                        act.wait_ge(mrow_in[s_2], 16 * (r_2 + 1))
                    nc.scalar.copy(mT[:, s % 2, :], mid[0:32, 0:P]).then_inc(mT_out, 1)

            steps(act, step, -AHEAD, 7, NUNIT)

        @block.tensor
        def _(pe):
            def step(j, c):
                odd = c % 2 == 1
                b1, sl1, r1 = at(j, c + 1)
                b2, sl2, r2 = at(j, c)
                p1, p2 = has(j, c + 1), has(j, c)
                half2 = c % 2
                _, vpar = batch(j, c - half2)

                def scores(n):
                    if not p1:
                        return
                    if n == 0:
                        pe.wait_ge(stack_in[sl1], 16 * HALF_DMAS * (r1 + 1))
                    need(pe, max_done, 4 * b1 + n - 1)
                    for h in range(4):
                        last = nc.tensor.matmul(s1[:, n % 2, P * h:P * h + P], qs[0:MROW, sl1, 4 * n + h, :], ks[0:MROW, sl1, 4 * n + h, :],
                                                start=True, stop=True)
                    last.then_inc(s1_done, 1)

                def shifted(u):
                    if not p2:
                        return
                    if u == 0:
                        pe.wait_ge(mrow_in[sl2], 16 * (r2 + 1))
                    need(pe, exp_done, 2 * b2 + u - 1)
                    for h in range(8):
                        last = nc.tensor.matmul(s2[:, u, h // 4, P * (h % 4):P * (h % 4) + P], ks[:, sl2, 8 * u + h, :],
                                                qs[:, sl2, 8 * u + h, :], start=True, stop=True)
                    last.then_inc(s2_done, 1)

                def values(u):
                    if not p2:
                        return
                    pe.wait_ge(exp_done, 2 * b2 + u + 1)
                    if u == 0:
                        need(pe, o_normed, b2)
                    for h in range(8):
                        col = (8 * u + h) * (HD_B + 1)
                        last = nc.tensor.matmul(acc[:, col:col + HD_B + 1], pt[:, u, h, :], v[:, vpar, UH * half2 + 8 * u + h, :],
                                                start=True, stop=True)
                    last.then_inc(pv_done, 1)

                scores(0)
                shifted(0)
                scores(1)
                if not odd and has(j, c - 1):
                    b, p = batch(j, c - 2)
                    pe.wait_ge(o_normed, 2 * b + 2)
                    pe.wait_ge(mT_out, cap(2 * b + 3, NUNIT))
                    for k in range(KC):
                        last = nc.tensor.transpose(mid[:, P * k:P * k + P], o[:, p, P * k:P * k + P], g["ident"][:])
                    last.then_inc(trO_done, 1)
                if odd and has(j, c + AHEAD):
                    b, p = batch(j, c + AHEAD)
                    pe.wait_ge(xn_done, b + 1)
                    need(pe, mT_out, 2 * b - 2)
                    if not p2:
                        need(pe, v_out, b)
                    pe.wait_ge(ctx_in[p], 16 * (j + (c + AHEAD) // 4 + 1))
                    for k in range(KC):
                        nc.tensor.transpose(mid[:, P * k:P * k + P], xn[:, p, P * k:P * k + P], g["ident"][:])
                    nc.tensor.transpose(mid[:, 2 * P:3 * P], ctx[:, p, :], g["ident"][:]).then_inc(trx_done, 1)
                scores(2)
                shifted(1)
                if not odd and has(j, c - 1):
                    b, p = batch(j, c - 2)
                    pe.wait_ge(oT_done, b + 1)
                    for k in range(KC):
                        last = nc.tensor.matmul(mid[:, 0:D], oT[:, p, k, :], g["wout"][:, k, :], start=(k == 0), stop=(k == KC - 1))
                    last.then_inc(out_done, 1)
                scores(3)
                values(0)
                if odd and has(j, c + AHEAD):
                    b, p = batch(j, c + AHEAD)
                    pe.wait_ge(xcT_done, b + 1)
                    for half in range(2):
                        for k in range(KC):
                            nc.tensor.matmul(mid[:, P * half:P * half + P], g["wqB"][:, k, half, :], xcT[:, p, k, :], start=(k == 0), stop=(k == KC - 1))
                    for half in range(2):
                        last = nc.tensor.matmul(mid[:, P * (2 + half):P * (3 + half)], g["wkB"][:, half, :], xcT[:, p, KC, :], start=True, stop=True)
                    last.then_inc(qk_done, 1)
                if not odd and has(j, c + 2):
                    b, p = batch(j, c + 2)
                    pe.wait_ge(qk_out, b + 1)
                    need(pe, mT_out, 2 * b - 1)
                    need(pe, x_added, b - 1)
                    nc.tensor.matmul(mid[:, 0:D], xcT[:, p, KC, :], g["wkv"][:, D:2 * D], start=True, stop=True).then_inc(v_done, 1)
                values(1)
                if p1:
                    pe.wait_ge(mx_split, b1 + 1)
                    if odd:
                        pe.wait_ge(qk_out, cap(batch(j, c + AHEAD)[0] + 1, NB))
                    else:
                        pe.wait_ge(v_out, cap(batch(j, c + 2)[0] + 1, NB))
                        if not has(j, c + 2):
                            pe.wait_ge(x_added, batch(j, c)[0])
                    nc.tensor.matmul(mid[0:32, 0:P], mxs[:, sl1 % 2].rearrange("p a h -> p (a h)"), g["nident"][:],
                                     start=True, stop=True).then_inc(mT_done, 1)

            steps(pe, step, -AHEAD, 7, NUNIT)


def unit(j, c):
    if c >= UG:
        j, c = j + 1, c - UG
    if isinstance(j, int) and j == NG:
        t, q = divmod(c, CB)
        rows = LASTC if q == CB - 1 else P
        return NG, c, t, q, CG * NG + q, rows, q == 0, q == CB - 1
    if c < CA * NT:
        t, q = divmod(c, CA)
        return j, c, t, q, CG * j + q, P, q == 0, q == CA - 1
    t, q = divmod(c - CA * NT, CB)
    return j, c, t, CB + q, CG * j + CA + q, P, q == 0, q == CB - 1


def mixture(nc, io, g, out, tmp):
    def sb(name, shape, dt=F32):
        return tmp.enter_context(nc.sbuf_tensor(name, shape, dt))

    def sem(name):
        return tmp.enter_context(nc.semaphore(name))

    x, ident, identb, s1, s2, last2 = g["x"], g["ident"], g["identb"], g["s1"], g["s2"], g["last2"]
    NSLOT = 2 * CB
    xhi = sb("xhi", [P, KC, TOK], F32R)
    xlo = sb("xlo", [P, KC, TOK], F32R)
    y = sb("y", [P, 2, TOK])
    combT = sb("combT", [96, TOK], BF16)
    sel = sb("sel", [96, FH], BF16)
    wgu = sb("wgu", [P, NSLOT, 2, KC, 2, P], F32R)
    wd = sb("wd", [P, NSLOT, 2, D], F32R)
    raw_gu = sb("raw_gu", [P, 2, KC, RAW])
    raw_d = sb("raw_d", [P, CB, D])
    logits_ps, yT = last2[:, 1, :], last2

    raw_in, sel_ok, w_hi, w_lo = sem("raw_in"), sem("sel_ok"), sem("w_hi"), sem("w_lo")
    (ln_stats, ln_aggr, eps_done, rstd_done, xn_done, trx_done, x_full, x_hi, x_lo, logit_done) = (sem("m_" + n) for n in (
        "ln_stats", "ln_aggr", "eps_done", "rstd_done", "xn_done", "trx_done", "x_full", "x_hi", "x_lo", "logit_done"))
    r_dve, r_exp, comb_trans, comb_out = sem("r_dve"), sem("r_exp"), sem("comb_trans"), sem("comb_out")
    (gate_done, up_done, silu_done, prod_done, h_done, h_hi, h_lo, down_done, y_added) = (sem("u_" + n) for n in (
        "gate_done", "up_done", "silu_done", "prod_done", "h_done", "h_hi", "h_lo", "down_done", "y_added"))
    y_zero, yt_done, x_final, stored = sem("y_zero"), sem("yt_done"), sem("x_final"), sem("stored")
    comb_ready, raw_tail = sem("comb_ready"), sem("raw_tail")
    GROUP_DMAS = 9
    FREE = 4

    stats = sb("m_stats", [P, NB, 6])
    mv = sb("m_mv", [P, NB, 2])
    rstd = sb("m_rstd", [P, 2, NB])
    xn = sb("m_xn", [P, 2, D])
    xf = sb("m_xf", [P, 2, KC, P])
    lg = sb("lg", [P, NB, NE])
    pr = sb("pr", [P, NB, NE + 4])
    rest = sb("rest", [P, NB, NE + 4])
    top = sb("top", [P, NB, 8])
    red = sb("red", [P, 4, NB])
    comb = sb("comb", [P, NB, NE + NSH])
    c3 = sb("c3", [P, NB, 96], BF16)
    sg = sb("silu_gate", [P, 2, TT])
    prod = sb("prod", [P, TT])
    h = sb("h_full", [P, 2, TT])
    hhi = sb("h_hi", [P, 4, TT], F32R)
    hlo = sb("h_lo", [P, 4, TT], F32R)

    def mix_steps(eng, step, last):
        for c in range(2):
            step(0, c)
        with eng.Fori(0, NG) as j:
            for c in range(2, UG + 2):
                step(j, c)
        for c in range(NG * UG + 2, last + 1):
            step(c // UG, c % UG) if c < (NG + 1) * UG else step(NG, c - NG * UG)

    def exists(j, c):
        return not isinstance(j, int) or 0 <= UG * j + c < NU

    def back(j, c, n):
        c -= n
        return (j, c) if c >= 0 else (j - 1, c + UG)

    def split_at(j, c):
        if isinstance(j, int) and j == NG:
            return (CB - 1, CB - 1, LASTC) if c == 2 else None
        if 3 <= c <= 18 and c % 3 == 0:
            return CB + c // 3 - 1, c // 3 - 1, P
        if c >= 24 and c % 4 == 0 and c // 4 - 6 < CA:
            return c // 4 - 6, c // 4 - 6, P
        return None

    def split_count(j, c):
        if isinstance(j, int) and j == NG:
            return CG * NG + CB - 1
        return CG * j + (CA + c // 3 - 1 if c <= 18 else CG + c // 4 - 6)

    def raw_wait(eng, j, c):
        if isinstance(j, int) and j == NG:
            eng.wait_ge(raw_tail, 16)
        else:
            eng.wait_ge(raw_in, 16 * GROUP_DMAS * (2 * j + (2 if c <= 18 else 3)))

    def twice(eng, count, step):
        step(0)
        with eng.Fori(1, count) as j:
            step(j)

    with nc.Block() as block:
        @block.sync
        def _(sp):
            down = io["w_down"].rearrange("e i n -> (e i) n")

            def columns(e, n, lo, first, width):
                for w, name in enumerate(("w_gate", "w_up")):
                    for k in range(KC):
                        sp.dma_start(raw_gu[:, w, k, lo:lo + n * width].rearrange("p (e i) -> p e i", e=n),
                                     io[name][e:e + n, P * k:P * k + P, first:first + width].rearrange("e p i -> p e i")).then_inc(raw_in, 16)

            for j in range(NG):
                need(sp, w_lo, CG * j)
                cut = CA * P - 3 * FE
                columns(8 * j, 3, 0, 0, FE)
                columns(8 * j + 3, 1, 3 * FE, 0, cut)
                row = CG * P * j
                sp.dma_start(raw_d[:, 0:CA, :], down[row:row + CA * P, :].rearrange("(c p) n -> p c n", p=P)).then_inc(raw_in, 16)
                sp.wait_ge(w_lo, CG * j + CA)
                columns(8 * j + 3, 1, 0, cut, FE - cut)
                columns(8 * j + 4, 4, FE - cut, 0, FE)
                row += CA * P
                sp.dma_start(raw_d[:, 0:CB, :], down[row:row + CB * P, :].rearrange("(c p) n -> p c n", p=P)).then_inc(raw_in, 16)
            sp.wait_ge(w_lo, CG * NG)
            for w, name in enumerate(("sh_gate", "sh_up")):
                for k in range(KC):
                    for half in range(2):
                        cols = slice(2 * FE * half, 2 * FE * (half + 1))
                        sp.dma_start(raw_gu[:, w, k, cols], io[name][P * k:P * k + P, cols]).then_inc(raw_in, 16)
            sp.dma_start(raw_d[:, 0:CA, :], io["sh_down"][0:CA * P, :].rearrange("(c p) n -> p c n", p=P)).then_inc(raw_in, 16)
            sp.dma_start(raw_d[0:LASTC, CA, :], io["sh_down"][CA * P:NSH * FE, :]).then_inc(raw_tail, 16)
            for n in range(4):
                sp.wait_ge(x_final, 4 * n + 4)
                sp.dma_start(out[4 * n:4 * n + 4].rearrange("b p d -> p b d"), x[:, 4 * n:4 * n + 4, :]).then_inc(stored, 16)
            sp.wait_ge(stored, 64)

        @block.gpsimd
        def _(pool):
            def split_lo(slot, raw, rows, n):
                pool.wait_ge(w_hi, n + 1)
                nc.gpsimd.tensor_tensor(wgu[:, slot, :, :, 1, 0:rows].rearrange("p w k n -> p (w k) n"),
                                        raw_gu[:, :, :, P * raw:P * raw + rows].rearrange("p w k n -> p (w k) n"),
                                        wgu[:, slot, :, :, 0, 0:rows].rearrange("p w k n -> p (w k) n").bitcast(F32), ALU.subtract)
                nc.gpsimd.tensor_tensor(wd[0:rows, slot, 1, :], raw_d[0:rows, raw, :],
                                        wd[0:rows, slot, 0, :].bitcast(F32), ALU.subtract).then_inc(w_lo, 1)

            nc.gpsimd.memset(sel[:], 1.0).then_inc(sel_ok, 1)
            pool.wait_ge(sel_ok, 1)
            nc.gpsimd.affine_select(out=sel[0:32], in_=sel[0:32], compare_op=ALU.is_ge, fill=0.0, base=0,
                                    pattern=[[1, FH]], channel_multiplier=-FE).then_inc(sel_ok, 1)
            pool.wait_ge(sel_ok, 2)
            nc.gpsimd.affine_select(out=sel[0:32], in_=sel[0:32], compare_op=ALU.is_ge, fill=0.0, base=FE - 1,
                                    pattern=[[-1, FH]], channel_multiplier=FE).then_inc(sel_ok, 1)
            nc.gpsimd.memset(c3[:], 0.0).then_inc(y_zero, 1)
            pool.wait_ge(ln_aggr, NB)
            nc.gpsimd.tensor_tensor(rstd[:, 0, :], mv[:, :, 1], g["ln_eps"][:, 0:1].broadcast_to([P, NB]), ALU.add).then_inc(eps_done, 1)
            pool.wait_ge(eps_done, 1)
            nc.gpsimd.tensor_tensor(rstd[:, 1, :], rstd[:, 0, :], g["ln_pow"][:, 0:1].broadcast_to([P, NB]), ALU.pow).then_inc(rstd_done, 1)
            nc.gpsimd.memset(y[:, 0], 0.0).then_inc(down_done, FREE)
            nc.gpsimd.memset(y[:, 1], 0.0).then_inc(y_added, 1)
            for q in range(CA):
                split_lo(q, q, P, q)

            def step(j, c):
                u = UG * j + c
                if exists(j, c):
                    rows = unit(j, c)[5]
                    pool.wait_ge(h_hi, u + 1)
                    pool.wait_ge(down_done, u - 3 + FREE)
                    nc.gpsimd.tensor_tensor(hlo[0:rows, c % 4, :], h[0:rows, c % 2, :], hhi[0:rows, c % 4, :].bitcast(F32),
                                            ALU.subtract).then_inc(h_lo, 1)
                at = split_at(j, c)
                if at:
                    split_lo(*at, split_count(j, c))

            mix_steps(pool, step, NU - 1)

        @block.scalar
        def _(act):
            def split_hi(slot, raw, rows, n):
                nc.scalar.copy(wgu[:, slot, :, :, 0, 0:rows].rearrange("p w k n -> p (w k) n"),
                               raw_gu[:, :, :, P * raw:P * raw + rows].rearrange("p w k n -> p (w k) n"))
                nc.scalar.copy(wd[0:rows, slot, 0, :], raw_d[0:rows, raw, :]).then_inc(w_hi, 1)

            act.wait_ge(raw_in, 16 * GROUP_DMAS)
            for q in range(CA):
                split_hi(q, q, P, q)

            def full_and_hi(j):
                for i in range(2):
                    b = 2 * j + i
                    act.wait_ge(trx_done, b + 1)
                    need(act, logit_done, b - 1)
                    need(act, x_lo, b - 1)
                    nc.scalar.copy(xf[:, i].rearrange("p k t -> p (k t)"), s1[:, i, 0:D]).then_inc(x_full, 1)
                    nc.scalar.copy(xhi[:, :, bass.ds(P * b, P)], s1[:, i, 0:D].rearrange("p (k t) -> p k t", k=KC)).then_inc(x_hi, 1)

            twice(act, NB // 2, full_and_hi)
            act.wait_ge(r_dve, 2)
            nc.scalar.activation(pr[:, :, 0:NE], lg[:], ACT.Exp).then_inc(r_exp, 1)
            nc.scalar.activation(comb[:, :, NE], logits_ps[:, 0:NB * (NE + 1)].rearrange("p (b e) -> p b e", b=NB)[:, :, NE],
                                 ACT.Exp, scale=-1.0).then_inc(r_exp, 1)
            for n in range(4):
                act.wait_ge(comb_trans, n + 1)
                nc.scalar.copy(combT[:, TT * n:TT * n + TT], s2[0:96, n % 2, 1, 0:TT // 2].bitcast(BF16)).then_inc(comb_out, 1)

            def step(j, c):
                u = UG * j + c
                if exists(j, c):
                    rows = unit(j, c)[5]
                    act.wait_ge(gate_done, u + 1)
                    need(act, prod_done, u - 1)
                    nc.scalar.activation(sg[0:rows, c % 2, :], s1[0:rows, c % 2, :], ACT.Silu).then_inc(silu_done, 1)
                jb, cb = back(j, c, 1)
                if exists(jb, cb):
                    rows = unit(jb, cb)[5]
                    act.wait_ge(h_done, u)
                    act.wait_ge(down_done, u - 4 + FREE)
                    nc.scalar.copy(hhi[0:rows, cb % 4, :], h[0:rows, cb % 2, :]).then_inc(h_hi, 1)
                at = split_at(j, c)
                if at:
                    raw_wait(act, j, c)
                    act.wait_ge(down_done, FREE + UG * j + (0 if c <= 18 else CA * NT))
                    split_hi(*at, None)

            mix_steps(act, step, NU)

        @block.vector
        def _(dve):
            nc.vector.memset(pr[:, :, NE:NE + 4], -1.0).then_inc(r_dve, 1)
            for b in range(NB):
                nc.vector.bn_stats(stats[:, b, :], x[:, b, :]).then_inc(ln_stats, 1)
            dve.wait_ge(ln_stats, NB)
            for b in range(NB):
                nc.vector.bn_aggr(mv[:, b, :], stats[:, b, :]).then_inc(ln_aggr, 1)
            dve.wait_ge(rstd_done, 1)

            def normalised(j):
                for i in range(2):
                    b = 2 * j + i
                    need(dve, trx_done, b - 1)
                    nc.vector.tensor_scalar(xn[:, i, :], x[:, b, :], mv[:, bass.ds(b, 1), 0:1].rearrange("p a c -> p (a c)"), rstd[:, 1, bass.ds(b, 1)],
                                            ALU.subtract, ALU.mult).then_inc(xn_done, 1)

            def lo_parts(j):
                for i in range(2):
                    b = 2 * j + i
                    dve.wait_ge(x_hi, b + 1)
                    nc.vector.tensor_tensor(xlo[:, :, bass.ds(P * b, P)], xf[:, i], xhi[:, :, bass.ds(P * b, P)].bitcast(F32),
                                            ALU.subtract).then_inc(x_lo, 1)

            normalised(0)
            with dve.Fori(1, NB // 2) as j:
                normalised(j)
                lo_parts(j - 1)
            lo_parts(NB // 2 - 1)
            made = [1]

            def then(ins, *more):
                made[0] += 1
                ins.then_inc(r_dve, 1)
                dve.wait_ge(r_dve, made[0])

            lps = logits_ps[:, 0:NB * (NE + 1)].rearrange("p (b e) -> p b e", b=NB)[:, :, 0:NE]
            wide = lambda a: a.unsqueeze(2).broadcast_to([P, NB, NE])
            dve.wait_ge(logit_done, NB)
            nc.vector.tensor_reduce(red[:, 0, :], lps, AX.X, ALU.max).then_inc(ln_stats, 1)
            dve.wait_ge(ln_stats, NB + 1)
            then(nc.vector.tensor_tensor(lg[:], lps, wide(red[:, 0, :]), ALU.subtract))
            dve.wait_ge(r_exp, 1)
            then(nc.vector.tensor_reduce(red[:, 1, :], pr[:, :, 0:NE], AX.X, ALU.add))
            then(nc.vector.reciprocal(red[:, 1, :], red[:, 1, :]))
            then(nc.vector.tensor_tensor(pr[:, :, 0:NE], pr[:, :, 0:NE], wide(red[:, 1, :]), ALU.mult))
            for b in range(NB):
                last = nc.vector.max(out=top[:, b, :], in_=pr[:, b, 0:NE])
            then(last)
            then(nc.vector.memset(top[:, :, TOPK:8], -1.0))
            for b in range(NB):
                last = nc.vector.match_replace(out=rest[:, b, :], in_to_replace=top[:, b, :], in_values=pr[:, b, :], imm_value=0.0)
            then(last)
            then(nc.vector.tensor_tensor(comb[:, :, 0:NE], pr[:, :, 0:NE], rest[:, :, 0:NE], ALU.subtract))
            then(nc.vector.tensor_reduce(red[:, 2, :], comb[:, :, 0:NE], AX.X, ALU.add))
            then(nc.vector.tensor_scalar(red[:, 2, :], red[:, 2, :], 1e-9, None, ALU.max))
            then(nc.vector.reciprocal(red[:, 2, :], red[:, 2, :]))
            then(nc.vector.tensor_tensor(comb[:, :, 0:NE], comb[:, :, 0:NE], wide(red[:, 2, :]), ALU.mult))
            dve.wait_ge(r_exp, 2)
            then(nc.vector.tensor_scalar(red[:, 3, :], comb[:, :, NE], 1.0, None, ALU.add))
            then(nc.vector.reciprocal(red[:, 3, :], red[:, 3, :]))
            then(nc.vector.tensor_copy(comb[:, :, NE:NE + NSH], red[:, 3, :].unsqueeze(2).broadcast_to([P, NB, NSH])))
            dve.wait_ge(y_zero, 1)
            for i in range(3):
                part = nc.vector.tensor_copy(c3[:, :, 32 * i:32 * i + NE + NSH], comb[:])
                if i == 2:
                    part.then_inc(comb_ready, 1)
                else:
                    then(part)
                    then(nc.vector.tensor_tensor(comb[:], comb[:], c3[:, :, 32 * i:32 * i + NE + NSH], ALU.subtract))
            dve.wait_ge(sel_ok, 3)
            nc.vector.tensor_copy(sel[32:64], sel[0:32]).then_inc(sel_ok, 1)
            nc.vector.tensor_copy(sel[64:96], sel[0:32]).then_inc(sel_ok, 1)

            def step(j, c):
                u = UG * j + c
                if exists(j, c):
                    rows = unit(j, c)[5]
                    need(dve, h_done, u)
                    dve.wait_ge(silu_done, u + 1)
                    dve.wait_ge(up_done, u + 1)
                    nc.vector.tensor_tensor(prod[0:rows, :], s2[0:rows, c % 2, 0, :], sg[0:rows, c % 2, :], ALU.mult).then_inc(prod_done, 1)
                    dve.wait_ge(prod_done, u + 1)
                    need(dve, h_lo, u - 1)
                    nc.vector.tensor_tensor(h[0:rows, c % 2, :], s2[0:rows, c % 2, 1, :], prod[0:rows, :], ALU.mult).then_inc(h_done, 1)
                jb, cb = back(j, c, 2)
                if exists(jb, cb) and unit(jb, cb)[7]:
                    gj, gc, t = unit(jb, cb)[0:3]
                    dve.wait_ge(down_done, UG * jb + cb + 1 + FREE)
                    nc.vector.tensor_tensor(y[:, :, TT * t:TT * t + TT], last2[:], y[:, :, TT * t:TT * t + TT], ALU.add).then_inc(y_added, 1)

            mix_steps(dve, step, NU + 1)
            for b in range(NB):
                dve.wait_ge(yt_done, b + 1)
                nc.vector.tensor_tensor(x[:, b, :], s1[:, b % 2, 0:D], x[:, b, :], ALU.add).then_inc(x_final, 1)

        def tiles(j, c):
            if isinstance(j, int) and j == NG:
                return 2 * NT * NG + c // CB
            return 2 * NT * j + (c // CA if c < CA * NT else NT + (c - CA * NT) // CB)

        @block.tensor
        def _(pe):
            def transposed_and_routed(j):
                for i in range(2):
                    b = 2 * j + i
                    pe.wait_ge(xn_done, b + 1)
                    need(pe, x_hi, b - 1)
                    for k in range(KC):
                        last = nc.tensor.transpose(s1[:, i, P * k:P * k + P], xn[:, i, P * k:P * k + P], ident[:])
                    last.then_inc(trx_done, 1)
                for i in range(2):
                    b = 2 * j + i
                    pe.wait_ge(x_full, b + 1)
                    for k in range(KC):
                        last = nc.tensor.matmul(logits_ps[:, bass.ds((NE + 1) * b, NE + 1)], xf[:, i, k, :], g["wr"][:, k, :],
                                                start=(k == 0), stop=(k == KC - 1))
                    last.then_inc(logit_done, 1)

            twice(pe, NB // 2, transposed_and_routed)

            def comb_transposes():
                pe.wait_ge(comb_ready, 1)
                for n in range(4):
                    need(pe, comb_out, n - 1)
                    for q in range(4):
                        last = nc.tensor.transpose(s2[0:96, n % 2, 1, 0:TT // 2].bitcast(BF16)[:, P * q:P * q + P], c3[:, 4 * n + q, :], identb[:])
                    last.then_inc(comb_trans, 1)
                pe.wait_ge(sel_ok, 5)
                pe.wait_ge(comb_out, 4)

            pe.wait_ge(x_lo, NB)
            pe.wait_ge(x_hi, NB)

            def three(ps, w_hi_ap, w_lo_ap, m_hi, m_lo, start, stop):
                nc.tensor.matmul(ps, w_hi_ap, m_hi, start=start, stop=False)
                nc.tensor.matmul(ps, w_hi_ap, m_lo, start=False, stop=False)
                return nc.tensor.matmul(ps, w_lo_ap, m_hi, start=False, stop=stop)

            def step(j, c):
                u = UG * j + c
                if exists(j, c):
                    gj, gc, t, slot, chunk, rows, first, last_of = unit(j, c)
                    pe.wait_ge(w_lo, chunk + 1)
                    toks = slice(TT * t, TT * t + TT)
                    need(pe, silu_done, u - 1)
                    for w, ps, done in ((0, s1[0:rows, c % 2, :], gate_done), (1, s2[0:rows, c % 2, 0, :], up_done)):
                        if w == 1:
                            need(pe, prod_done, u - 1)
                        for k in range(KC):
                            last = three(ps, wgu[:, slot, w, k, 0, 0:rows], wgu[:, slot, w, k, 1, 0:rows], xhi[:, k, toks], xlo[:, k, toks],
                                         k == 0, k == KC - 1)
                        if w == 0:
                            last.then_inc(gate_done, 1)
                    if isinstance(u, int) and u == 0:
                        comb_transposes()
                    need(pe, h_done, u - 1)
                    nc.tensor.matmul(s2[0:rows, c % 2, 1, :], sel[:, bass.ds(P * chunk, rows)], combT[:, toks], start=True, stop=True).then_inc(up_done, 1)
                jb, cb = back(j, c, 2)
                if exists(jb, cb):
                    gj, gc, t, slot, chunk, rows, first, last_of = unit(jb, cb)
                    if first:
                        pe.wait_ge(y_added, tiles(gj, gc) + 1)
                    pe.wait_ge(h_lo, u - 1)
                    r = cb % 4
                    for m in range(2):
                        last = three(last2[:, m, :], wd[0:rows, slot, 0, P * m:P * m + P], wd[0:rows, slot, 1, P * m:P * m + P],
                                     hhi[0:rows, r, :], hlo[0:rows, r, :], first, last_of)
                    last.then_inc(down_done, 1)

            mix_steps(pe, step, NU + 1)
            pe.wait_ge(silu_done, NU)
            for b in range(NB):
                pe.wait_ge(y_added, (2 * NG + 1) * NT + 1)
                need(pe, x_final, b - 1)
                for m in range(2):
                    last = nc.tensor.transpose(s1[:, b % 2, P * m:P * m + P], y[:, m, P * b:P * b + P], ident[:])
                last.then_inc(yt_done, 1)


def build(nc, io, out):
    with ExitStack() as ctx:
        def sb(name, shape, dt=F32):
            return ctx.enter_context(nc.sbuf_tensor(name, shape, dt))

        g = {
            "x": sb("x_sb", [P, NB, D]),
            "ident": sb("ident", [P, P]), "nident": sb("nident", [P, P]), "identb": sb("identb", [P, P], BF16),
            "ln_eps": sb("ln_eps", [P, 4]), "ln_pow": sb("ln_pow", [P, 4]), "ones_row": sb("ones_row", [1, P]), "zero": sb("zero", [P, 4]),
            "wr": sb("wr", [P, KC, NE + 1]),
            "s1": ctx.enter_context(nc.psum_tensor("s1", [P, 2, 512], F32)),
            "s2": ctx.enter_context(nc.psum_tensor("s2", [P, 2, 2, 512], F32)),
            "x_in": ctx.enter_context(nc.semaphore("x_in")),
        }
        last2 = ctx.enter_context(nc.psum_tensor("last2", [P, 2, 512], F32))
        g["last2"], g["mid"], g["acc"] = last2, last2[:, 0, :], last2[:, 1, :]
        with ExitStack() as att:
            def sa(name, shape, dt=F32):
                return att.enter_context(nc.sbuf_tensor(name, shape, dt))

            g.update({
                "ob": sa("ob", [P, 2, D]), "vb_row": sa("vb_row", [1, HD_A]),
                "wqT": sa("wqT", [P, KC, D]), "woT": sa("woT", [P, KC, D]), "wkT": sa("wkT", [P, KC, 96]),
                "wvT": sa("wvT", [P, KC, HD_A]), "qkb": sa("qkb", [P, 3]),
                "wqB": sa("wqB", [P, KC, 2, P]), "wkB": sa("wkB", [P, 2, P]), "wkv": sa("wkv", [P, 2 * D]),
                "wout": sa("wout", [P, KC, D]), "rope": sa("rope", [P, 2, NB, P]),
                "mask_q": sa("mask_q", [P, 4, P], BF16), "mask_k": sa("mask_k", [P, 4, P], BF16),
            })
            with ExitStack() as tmp:
                prepare(nc, io, g, tmp)
            with ExitStack() as tmp:
                self_attention(nc, g, tmp)
            with ExitStack() as tmp:
                cross_attention(nc, io, g, tmp)
        with ExitStack() as tmp:
            mixture(nc, io, g, out, tmp)


_INS = [("x", "x"), ("ctx", "ctx_1024"), ("pos", "fside_BxSx2_0"), ("q_w", "L0_attn_q_w"), ("q_b", "L0_attn_q_b"),
        ("k_w", "L0_attn_k_w"), ("k_b", "L0_attn_k_b"), ("v_w", "L0_attn_v_w"), ("v_b", "L0_attn_v_b"),
        ("o_w", "L0_attn_o_w"), ("o_b", "L0_attn_o_b"), ("Wq", "L0_xattn_Wq"), ("Wkv", "L0_xattn_Wkv"),
        ("Wout", "L0_xattn_Wout"), ("bout", "L0_xattn_bout"), ("router_w", "L0_ffn_router_w"),
        ("w_gate", "L0_ffn_w_gate"), ("w_up", "L0_ffn_w_up"), ("w_down", "L0_ffn_w_down"),
        ("sh_gate", "L0_ffn_sh_gate"), ("sh_up", "L0_ffn_sh_up"), ("sh_down", "L0_ffn_sh_down"),
        ("sh_gate_w", "L0_ffn_sh_gate_w")]


def kernel(**inputs):
    import numpy as _np
    import concourse.bacc as _bacc
    from concourse import mybir as _mybir
    from concourse.bass_utils import run_bass_kernel_spmd as _run

    nc = _bacc.Bacc("TRN2", target_bir_lowering=False, num_devices=1)
    arrays, io = {}, {}
    for short, name in _INS:
        a = _np.ascontiguousarray(inputs[name])
        arrays[f"in_{short}"] = a
        io[short] = nc.dram_tensor(f"in_{short}", a.shape, _mybir.dt.from_np(a.dtype), kind="ExternalInput").ap()
    out = nc.dram_tensor("out_0", inputs["x"].shape, _mybir.dt.float32, kind="ExternalOutput").ap()
    build(nc, io, out)
    r = _run(nc, [arrays], core_ids=[0])
    return r.results[0]["out_0"]
```

```python
from contextlib import ExitStack

import concourse.bass as bass
from concourse import mybir

F32 = mybir.dt.float32
F32R = mybir.dt.float32r
BF16 = mybir.dt.bfloat16
ALU = mybir.AluOpType
ACT = mybir.ActivationFunctionType
AX = mybir.AxisListType

P = 128
NB = 16
D = 256
KC = D // P
UH = 16
HD_A = 16
HD_B = 8
NH_B = 32
CTX = 128
EPS = 1e-5
MASKED = -1e30
SLOTS = 4
MROW = 96
VW = 32
STACK_DMAS = 6

NE, TOPK, FE = 16, 4, 176
NSH = 4
FH = (NE + NSH) * FE
TOK = NB * P
TT = 512
NT = TOK // TT
CA, CB = 5, 6
CG = CA + CB
UG = CG * NT
NG = 2
NU = NG * UG + CB * NT
RAW = CB * P
LASTC = FH - (FH // P) * P

FREQ1 = 10000.0 ** -0.5
TWO_PI_HI = 6.28125
TWO_PI_LO = 2 * 3.141592653589793 - 6.28125
ROUND = 1.5 * 2 ** 23
PI_IN = 3.1415925


def need(eng, sem, value):
    if isinstance(value, int) and value <= 0:
        return
    eng.wait_ge(sem, value)


def valid(j, c, n):
    return not isinstance(j, int) or 0 <= 4 * j + c < n


def cap(value, most):
    return min(value, most) if isinstance(value, int) else value


def steps(eng, step, first, enter, looped, last):
    for c in range(first, enter):
        step(0, c)
    with eng.Fori(0, looped) as j:
        for c in range(enter, enter + 4):
            step(j, c)
    for c in range(enter + 4 * looped, last + 1):
        step(0, c)


def prepare(nc, io, g, tmp):
    def sb(name, shape, dt=F32):
        return tmp.enter_context(nc.sbuf_tensor(name, shape, dt))

    def sem(name):
        return tmp.enter_context(nc.semaphore(name))

    qo_nat = sb("qo_nat", [P, 2, KC, D])
    kvr_nat = sb("kvr_nat", [NE + 1, 3, D])
    bias_row = sb("bias_row", [1, D + 96])
    qb_dh = sb("qb_dh", [1, D])
    one = sb("one", [1, 1])
    wq_nat = sb("wq_nat", [P, KC, D])
    pos = sb("pos", [P, NB, 2])
    ang = sb("ang", [P, 2, NB, 4])
    turns = sb("turns", [P, 2, NB * 4])
    trig = sb("trig", [P, 2, NB, 4])
    wide = sb("wide", [P, 2, NB, P])
    x, s1, s2, mid, acc = g["x"], g["s1"], g["s2"], g["mid"], g["acc"]
    ident, nident, identb = g["ident"], g["nident"], g["identb"]

    w_in, row_in, pos_in, ob_in, wb_in = (sem(n) for n in ("w_in", "row_in", "pos_in", "ob_in", "wb_in"))
    cleared, built, consts = sem("cleared"), sem("built"), sem("consts")
    wT_done, wT_out, turned, trig_done, widened = (sem(n) for n in ("wT_done", "wT_out", "turned", "trig_done", "widened"))
    tab_done, tab_out, rows_zero, permuted = sem("tab_done"), sem("tab_out"), sem("rows_zero"), sem("permuted")
    turned_row = sem("turned_row")

    with nc.Block() as block:
        @block.sync
        def _(sp):
            for i, name in enumerate(("q_w", "o_w")):
                sp.dma_start(qo_nat[:, i], io[name].rearrange("(r p) n -> p r n", p=P)).then_inc(w_in, 16)
            for i, name in enumerate(("k_w", "v_w", "router_w")):
                sp.dma_start(kvr_nat[0:UH, i], io[name]).then_inc(w_in, 16)
            sp.dma_start(kvr_nat[NE:NE + 1, 2], io["sh_gate_w"].rearrange("k n -> n k")).then_inc(w_in, 16)
            sp.dma_start(pos[:], io["pos"].rearrange("b p c -> p b c")).then_inc(pos_in, 16)
            for n in range(4):
                sp.dma_start(x[:, 4 * n:4 * n + 4, :], io["x"][4 * n:4 * n + 4].rearrange("b p d -> p b d")).then_inc(g["x_in"], 16)
            sp.dma_start(g["ob"][:, 0, :], io["o_b"].rearrange("(a n) -> a n", a=1).partition_broadcast(P)).then_inc(ob_in, 16)
            sp.dma_start(g["ob"][:, 1, :], io["bout"].rearrange("(a n) -> a n", a=1).partition_broadcast(P)).then_inc(ob_in, 16)
            sp.wait_ge(g["x_in"], 64)
            sp.wait_ge(ob_in, 32)

        @block.scalar
        def _(act):
            act.wait_ge(rows_zero, 1)
            act.dma_start(bias_row[:, 0:D], io["q_b"].rearrange("(a n) -> a n", a=1)).then_inc(row_in, 16)
            for r in range(3):
                act.dma_start(bias_row[:, D + 32 * r:D + 32 * r + HD_A], io["k_b"].rearrange("(a n) -> a n", a=1)).then_inc(row_in, 16)
            act.dma_start(g["vb_row"][:], io["v_b"].rearrange("(a n) -> a n", a=1)).then_inc(row_in, 16)
            act.dma_start(wq_nat[:], io["Wq"].rearrange("(k p) n -> p k n", p=P)).then_inc(wb_in, 16)
            act.dma_start(g["wkv"][:], io["Wkv"]).then_inc(wb_in, 16)
            act.dma_start(g["wout"][:], io["Wout"].rearrange("(k p) n -> p k n", p=P)).then_inc(wb_in, 16)
            act.wait_ge(turned, 7)
            nc.scalar.activation(trig[:].rearrange("p s b f -> p (s b f)"), ang[:].rearrange("p s b f -> p (s b f)"),
                                 ACT.Sin).then_inc(trig_done, 1)
            for n in range(8):
                act.wait_ge(tab_done, n + 1)
                nc.scalar.copy(g["rope"][:, n // 4, 4 * (n % 4):4 * (n % 4) + 4, :].rearrange("p b t -> p (b t)"),
                               s2[:, n % 2, 0, :]).then_inc(tab_out, 1)
            act.wait_ge(row_in, 80)
            act.wait_ge(wb_in, 48)

        @block.gpsimd
        def _(pool):
            nc.gpsimd.memset(bias_row[:], 0.0).then_inc(rows_zero, 1)
            nc.gpsimd.memset(ident[:], 0.0).then_inc(cleared, 1)
            nc.gpsimd.memset(nident[:], 0.0).then_inc(cleared, 1)
            nc.gpsimd.memset(g["mask_q"][:], 0.0).then_inc(cleared, 1)
            nc.gpsimd.memset(g["mask_k"][:], 0.0).then_inc(cleared, 1)
            pool.wait_ge(cleared, 4)
            for t, v in ((ident, 1.0), (nident, -1.0)):
                nc.gpsimd.affine_select(out=t[:], in_=t[:], compare_op=ALU.not_equal, fill=v, base=0,
                                        pattern=[[-1, P]], channel_multiplier=1).then_inc(built, 1)
            nc.gpsimd.affine_select(out=g["mask_q"][:], in_=g["mask_q"][:], compare_op=ALU.is_ge, fill=MASKED, base=0,
                                    pattern=[[0, 4], [-1, P]], channel_multiplier=1).then_inc(built, 1)
            nc.gpsimd.affine_select(out=g["mask_k"][:], in_=g["mask_k"][:], compare_op=ALU.is_ge, fill=MASKED, base=0,
                                    pattern=[[0, 4], [1, P]], channel_multiplier=-1).then_inc(built, 1)
            pool.wait_ge(built, 1)
            nc.gpsimd.tensor_copy(identb[:], ident[:]).then_inc(built, 1)
            nc.gpsimd.memset(g["ln_eps"][:], EPS).then_inc(built, 1)
            nc.gpsimd.memset(g["zero"][:], 0.0).then_inc(built, 1)
            nc.gpsimd.memset(g["ln_pow"][:], -0.5).then_inc(built, 1)
            nc.gpsimd.memset(g["ones_row"][:], 1.0).then_inc(built, 1)
            nc.gpsimd.memset(g["qs"][:].bitcast(F32), 0.0).then_inc(built, 1)

        @block.vector
        def _(dve):
            nc.vector.memset(one[:], 1.0).then_inc(consts, 1)
            nc.vector.memset(g["kst"][MROW:MROW + 2].bitcast(F32), 1.0)
            nc.vector.memset(g["wkT"][:], 0.0).then_inc(consts, 1)
            dve.wait_ge(built, 1)
            gather = g["gather"][:].rearrange("p (g w) -> p g w", g=4)
            parts = ident[:].rearrange("p (g w) -> p g w", g=4)
            nc.vector.tensor_copy(gather, parts[:, :, 0:HD_B + 1])
            nc.vector.tensor_reduce(g["of_head"][:], ident[:].rearrange("p (r i) -> p i r", i=4), AX.X, ALU.add)
            dve.wait_ge(row_in, 80)
            nc.vector.tensor_copy(qb_dh[:].rearrange("p (d h) -> p h d", h=UH), bias_row[:, 0:D].rearrange("p (h d) -> p h d", d=HD_A)).then_inc(turned_row, 1)
            dve.wait_ge(pos_in, 16)
            av = ang[:].rearrange("p s b (c f) -> p s b c f", f=2)
            nc.vector.tensor_copy(av[:, 0, :, :, 0], pos[:]).then_inc(turned, 1)
            nc.vector.tensor_scalar(av[:, 0, :, :, 1], pos[:], FREQ1, None, ALU.mult).then_inc(turned, 1)
            dve.wait_ge(turned, 2)
            af = ang[:].rearrange("p s b f -> p s (b f)")
            nc.vector.tensor_scalar(af[:, 1, :], af[:, 0, :], 3.141592653589793 / 2, None, ALU.add).then_inc(turned, 1)
            dve.wait_ge(turned, 3)
            nc.vector.tensor_scalar(turns[:], af, 1 / (2 * 3.141592653589793), ROUND, ALU.mult, ALU.add).then_inc(turned, 1)
            dve.wait_ge(turned, 4)
            nc.vector.tensor_scalar(turns[:], turns[:], ROUND, None, ALU.subtract).then_inc(turned, 1)
            dve.wait_ge(turned, 5)
            a1, t1 = (v.rearrange("p s b f -> p (s b f)") if v is not turns else v for v in (ang[:], turns))
            tf = turns[:].rearrange("p s n -> p (s n)")
            nc.vector.scalar_tensor_tensor(a1, tf, -TWO_PI_HI, a1, ALU.mult, ALU.add).then_inc(turned, 1)
            dve.wait_ge(turned, 6)
            nc.vector.scalar_tensor_tensor(a1, tf, -TWO_PI_LO, a1, ALU.mult, ALU.add).then_inc(consts, 1)
            dve.wait_ge(consts, 3)
            nc.vector.tensor_scalar(a1, a1, PI_IN, -PI_IN, ALU.min, ALU.max).then_inc(turned, 1)
            dve.wait_ge(wb_in, 48)
            for half in range(2):
                for k in range(KC):
                    nc.vector.tensor_copy(g["wqB"][:, k, half, :].rearrange("p (c f h) -> p h f c", c=2, f=4),
                                          wq_nat[:, k, P * half:P * half + P].rearrange("p (h f c) -> p h f c", h=UH, f=4)).then_inc(permuted, 1)
                nc.vector.tensor_copy(g["wkB"][:, half, :].rearrange("p (c f h) -> p h f c", c=2, f=4),
                                      g["wkv"][:, P * half:P * half + P].rearrange("p (h f c) -> p h f c", h=UH, f=4)).then_inc(permuted, 1)
            dve.wait_ge(wT_done, 1)
            for k in range(KC):
                for r in range(2):
                    nc.vector.tensor_copy(g["wqT"][:, k, :].rearrange("p (d h) -> p h d", h=UH)[:, 8 * r:8 * r + 8, :],
                                          s1[:, 0, P * (2 * k + r):P * (2 * k + r) + P].rearrange("p (h d) -> p h d", d=HD_A)).then_inc(wT_out, 1)
            dve.wait_ge(wT_done, 2)
            nc.vector.tensor_copy(g["woT"][:].rearrange("p k n -> p (k n)"), s1[:, 1, :]).then_inc(wT_out, 1)
            dve.wait_ge(wT_done, 3)
            small = mid[:, 0:192].rearrange("p (w k n) -> p w k n", w=3, k=KC)
            for r in range(3):
                nc.vector.tensor_copy(g["wkT"][:, :, 32 * r:32 * r + HD_A], small[:, 0, :, 0:HD_A]).then_inc(wT_out, 1)
            nc.vector.tensor_copy(g["wvT"][:], small[:, 1, :, 0:HD_A]).then_inc(wT_out, 1)
            nc.vector.tensor_copy(g["wr"][:], small[:, 2, :, 0:NE + 1]).then_inc(wT_out, 1)
            dve.wait_ge(wT_done, 4)
            nc.vector.tensor_copy(g["qkb"][:, 0:2], acc[:, 0:2]).then_inc(wT_out, 1)
            nc.vector.tensor_copy(g["qkb"][0:96, 2:3], acc[0:96, 2:3]).then_inc(wT_out, 1)
            dve.wait_ge(trig_done, 1)
            for s in range(2):
                for c in range(2):
                    for b in range(0, NB, 8):
                        src = trig[:, s, b:b + 8, :].rearrange("p b f -> p (b f)").unsqueeze(2).broadcast_to([P, 32, UH])
                        dst = wide[:, s, b:b + 8, 64 * c:64 * c + 64].rearrange("p b (f h) -> p b f h", h=UH)
                        for bb in range(8):
                            last = nc.vector.tensor_scalar(dst[:, bb], src[:, 4 * bb:4 * bb + 4, :], -1.0 if (s, c) == (0, 0) else 1.0, None, ALU.mult)
                            last.then_inc(widened, 1)

        @block.tensor
        def _(pe):
            pe.wait_ge(built, 2)
            pe.wait_ge(w_in, 96)
            for i in range(2):
                for k in range(KC):
                    for r in range(2):
                        last = nc.tensor.transpose(s1[:, i, P * (2 * k + r):P * (2 * k + r) + P], qo_nat[:, i, r, P * k:P * k + P], ident[:])
                last.then_inc(wT_done, 1)
            for w in range(3):
                for k in range(KC):
                    n = NE + 1 if w == 2 else UH
                    last = nc.tensor.transpose(mid[:, 64 * w + 32 * k:64 * w + 32 * k + n], kvr_nat[0:n, w, P * k:P * k + P], ident[0:n, 0:n])
            last.then_inc(wT_done, 1)
            pe.wait_ge(row_in, 80)
            pe.wait_ge(consts, 1)
            pe.wait_ge(turned_row, 1)
            for c in range(2):
                nc.tensor.matmul(acc[:, c:c + 1], qb_dh[:, P * c:P * c + P], one[:], start=True, stop=True)
            nc.tensor.matmul(acc[0:96, 2:3], bias_row[:, D:D + 96], one[:], start=True, stop=True).then_inc(wT_done, 1)
            for n in range(8):
                pe.wait_ge(widened, 2 * NB * (n // 4 + 1))
                need(pe, tab_out, n - 1)
                for q in range(4):
                    last = nc.tensor.transpose(s2[:, n % 2, 0, P * q:P * q + P], wide[:, n // 4, 4 * (n % 4) + q, :], ident[:])
                last.then_inc(tab_done, 1)


def self_attention(nc, g, tmp):
    def sb(name, shape, dt=F32):
        return tmp.enter_context(nc.sbuf_tensor(name, shape, dt))

    def sem(name):
        return tmp.enter_context(nc.semaphore(name))

    x, s1, s2, mid, acc = g["x"], g["s1"], g["s2"], g["mid"], g["acc"]
    qs = g["qs"]
    ks = sb("ks", [P, SLOTS, P], F32R)
    v = sb("v", [P, SLOTS, VW])
    stats = sb("stats", [P, SLOTS, 6])
    mv = sb("mv", [P, SLOTS, 2])
    rstd = sb("rstd", [P, SLOTS, 2])
    xn = sb("xn", [P, 2, D])
    xnT = sb("xnT", [P, 2, KC, P])
    qf = sb("qf", [P, 2, KC, P])
    qhi = sb("qhi", [P, 2, KC, P], F32R)
    qlo = sb("qlo", [P, 2, KC, P], F32R)
    kf = sb("kf", [96, 2, P])
    mx = sb("mx", [P, UH])
    mxs = sb("mxs", [P, 2, 2, UH])
    mT = sb("mT", [32, 2, P], F32R)
    pt = sb("pt", [P, 2, 8, P])
    rc = sb("rc", [P, UH])
    sums = sb("sums", [P, 512])
    o = sb("o", [P, 2, D])
    oT = sb("oT", [P, 2, KC, P])

    stack_in = [sem(f"stack_in{i}") for i in range(SLOTS)]
    mrow_in = [sem(f"mrow_in{i}") for i in range(SLOTS)]
    (init, ln_stats, ln_aggr, eps_done, rstd_done, xn_done, trx_done, xnT_done, proj_done, qkv_out, q_hi, q_split,
     k_hi, ks_done, ob_added, s1_done, max_done, mx_hi, mx_split, mT_done, mT_out, s2_done, exp_done, pv_done, sums_out, tb_done, rc_done,
     o_normed, trO_done, oT_done, out_done, x_added) = (sem("a_" + n) for n in (
        "init", "ln_stats", "ln_aggr", "eps_done", "rstd_done", "xn_done", "trx_done", "xnT_done", "proj_done", "qkv_out",
        "q_hi", "q_split", "k_hi", "ks_done", "ob_added", "s1_done", "max_done", "mx_hi", "mx_split", "mT_done", "mT_out",
        "s2_done", "exp_done", "pv_done", "sums_out", "tb_done", "rc_done", "o_normed", "trO_done", "oT_done", "out_done", "x_added"))
    AHEAD = 4

    def at(j, c):
        return 4 * j + c, c % SLOTS, j + c // SLOTS

    with nc.Block() as block:
        @block.sync
        def _(sp):
            def step(j, c):
                if valid(j, c + 3, NB):
                    b, s, r = at(j, c + 3)
                    sp.wait_ge(q_split, b + 1)
                    need(sp, s2_done, 2 * b - 6)
                    for row, part in ((0, qhi), (32, qhi), (64, qlo)):
                        for k in range(KC):
                            sp.dma_start(qs[row + 8 * k:row + 8 * k + 8, s].bitcast(F32),
                                         part[:, s % 2, k, :].bitcast(F32)).then_inc(stack_in[s], 16)
                if valid(j, c + 1, NB):
                    b, s, r = at(j, c + 1)
                    sp.wait_ge(mT_out, b + 1)
                    sp.dma_start(qs[MROW:MROW + 2, s].bitcast(F32), mT[:, s % 2, :].bitcast(F32)).then_inc(mrow_in[s], 16)

            steps(sp, step, -AHEAD, 1, 2, NB)

        @block.gpsimd
        def _(pool):
            nc.gpsimd.memset(v[:], 1.0).then_inc(init, 1)

            def step(j, c):
                if valid(j, c + 3, NB):
                    b, s, r = at(j, c + 3)
                    p = s % 2
                    pool.wait_ge(qkv_out, b + 1)
                    if not (isinstance(b, int) and b < 2):
                        _, s_2, r_2 = at(j, c + 1)
                        pool.wait_ge(stack_in[s_2], 16 * STACK_DMAS * (r_2 + 1))
                    nc.gpsimd.tensor_tensor(qhi[:, p].rearrange("p k t -> p (k t)"), qf[:, p].rearrange("p k t -> p (k t)"), g["zero"][:, 0:1].broadcast_to([P, D]), ALU.add).then_inc(q_hi, 1)
                    pool.wait_ge(q_hi, b + 1)
                    nc.gpsimd.tensor_tensor(qlo[:, p], qf[:, p], qhi[:, p].bitcast(F32), ALU.subtract).then_inc(q_split, 1)
                    need(pool, s2_done, 2 * b - 6)
                    if isinstance(b, int) and b == 0:
                        pool.wait_ge(init, 2)
                    nc.gpsimd.tensor_tensor(ks[0:96, s], kf[:, p], g["zero"][0:96, 0:1].broadcast_to([96, P]), ALU.add).then_inc(k_hi, 1)
                if valid(j, c + AHEAD, NB):
                    b, s, r = at(j, c + AHEAD)
                    pool.wait_ge(ln_aggr, b + 1)
                    nc.gpsimd.tensor_tensor(rstd[:, s, 0:1], mv[:, s, 1:2], g["ln_eps"][:, 0:1], ALU.add).then_inc(eps_done, 1)
                    pool.wait_ge(eps_done, b + 1)
                    nc.gpsimd.tensor_tensor(rstd[:, s, 1:2], rstd[:, s, 0:1], g["ln_pow"][:, 0:1], ALU.pow).then_inc(rstd_done, 1)
                    pool.wait_ge(xn_done, b + 1)
                    nc.gpsimd.tensor_tensor(x[:, b, :], x[:, b, :], g["ob"][:, 0, :], ALU.add).then_inc(ob_added, 1)

            steps(pool, step, -AHEAD, 1, 2, NB)

        @block.vector
        def _(dve):
            nc.vector.memset(ks[:].bitcast(F32), 1.0).then_inc(init, 1)

            def step(j, c):
                ahead, split, p1, done = (valid(j, c + d, NB) for d in (AHEAD, 3, 2, -1))
                b, s, r = at(j, c + AHEAD)
                b1, sl1, _ = at(j, c + 2)
                b0, sl0, _ = at(j, c - 1)
                done = done and not (isinstance(b0, int) and b0 < 0)

                def row_max(n):
                    if p1:
                        if n == 0:
                            need(dve, mx_split, b1)
                        dve.wait_ge(s1_done, 4 * b1 + n + 1)
                        nc.vector.tensor_reduce(mx[:, 4 * n:4 * n + 4], s1[:, n % 2, :].rearrange("p (h k) -> p h k", h=4),
                                                AX.X, ALU.max).then_inc(max_done, 1)

                row_max(0)
                if ahead:
                    nc.vector.bn_stats(stats[:, s, :], x[:, b, :]).then_inc(ln_stats, 1)
                if done:
                    dve.wait_ge(tb_done, b0 + 1)
                    pv = acc[:].rearrange("p (i g w) -> p i g w", i=4, g=4)
                    rcv = rc[:].rearrange("p (i g) -> p i g", i=4)
                    nc.vector.reciprocal(rcv, pv[:, :, :, HD_A]).then_inc(rc_done, 1)
                    dve.wait_ge(rc_done, b0 + 1)
                    nc.vector.tensor_tensor(o[:, sl0 % 2, :].rearrange("p (g i d) -> p i g d", i=4, g=4), pv[:, :, :, 0:HD_A],
                                            rcv.unsqueeze(3).broadcast_to([P, 4, 4, HD_A]), ALU.mult).then_inc(o_normed, 1)
                row_max(1)
                if split:
                    b3, s3, _ = at(j, c + 3)
                    dve.wait_ge(k_hi, b3 + 1)
                    nc.vector.tensor_tensor(ks[32:64, s3], kf[32:64, s3 % 2], ks[32:64, s3].bitcast(F32), ALU.subtract).then_inc(ks_done, 1)
                if ahead:
                    dve.wait_ge(ln_stats, b + 1)
                row_max(2)
                if ahead:
                    nc.vector.bn_aggr(mv[:, s, :], stats[:, s, :]).then_inc(ln_aggr, 1)
                if ahead:
                    dve.wait_ge(rstd_done, b + 1)
                    need(dve, trx_done, b - 1)
                    nc.vector.tensor_scalar(xn[:, s % 2, :], x[:, b, :], mv[:, s, 0:1], rstd[:, s, 1:2],
                                            ALU.subtract, ALU.mult).then_inc(xn_done, 1)
                if done:
                    dve.wait_ge(out_done, b0 + 1)
                    dve.wait_ge(ob_added, b0 + 1)
                    nc.vector.tensor_tensor(x[:, b0, :], mid[:, 0:D], x[:, b0, :], ALU.add).then_inc(x_added, 1)
                row_max(3)
                if p1:
                    dve.wait_ge(max_done, 4 * b1 + 4)
                    need(dve, mT_done, b1 - 1)
                    nc.vector.tensor_copy(mxs[:, sl1 % 2, 0, :].bitcast(F32R), mx[:]).then_inc(mx_hi, 1)
                    dve.wait_ge(mx_hi, b1 + 1)
                    nc.vector.tensor_tensor(mxs[:, sl1 % 2, 1, :], mx[:], mxs[:, sl1 % 2, 0, :], ALU.subtract).then_inc(mx_split, 1)

            steps(dve, step, -AHEAD, 1, 2, NB)

        @block.scalar
        def _(act):
            def step(j, c):
                def exps(u):
                    if valid(j, c, NB):
                        b, s, _ = at(j, c)
                        act.wait_ge(s2_done, 2 * b + u + 1)
                        need(act, pv_done, 2 * b + u - 1)
                        nc.scalar.activation(pt[:, u].rearrange("p h q -> p (h q)"), s2[:, u].rearrange("p a n -> p (a n)"),
                                             ACT.Exp, scale=HD_A ** -0.5).then_inc(exp_done, 1)

                if valid(j, c - 1, NB):
                    b, s, _ = at(j, c - 1)
                    act.wait_ge(pv_done, 2 * b + 2)
                    need(act, tb_done, b)
                    nc.scalar.copy(sums[:], acc[:]).then_inc(sums_out, 1)
                exps(0)
                if valid(j, c - 1, NB):
                    b, s, _ = at(j, c - 1)
                    act.wait_ge(trO_done, b + 1)
                    nc.scalar.copy(oT[:, s % 2].rearrange("p k t -> p (k t)"), mid[:, 0:D]).then_inc(oT_done, 1)
                if valid(j, c + 1, NB):
                    b, s, _ = at(j, c + 1)
                    act.wait_ge(mT_done, b + 1)
                    if not (isinstance(b, int) and b < 2):
                        _, s_2, r_2 = at(j, c - 1)
                        act.wait_ge(mrow_in[s_2], 16 * (r_2 + 1))
                    nc.scalar.copy(mT[:, s % 2, :], acc[0:32, 384:512]).then_inc(mT_out, 1)
                exps(1)
                if valid(j, c + AHEAD, NB):
                    b, s, _ = at(j, c + AHEAD)
                    p = s % 2
                    act.wait_ge(trx_done, b + 1)
                    nc.scalar.copy(xnT[:, p].rearrange("p k t -> p (k t)"), mid[:, 0:D]).then_inc(xnT_done, 1)
                    act.wait_ge(proj_done, b + 1)
                    need(act, q_split, b - 1)
                    need(act, ks_done, b - 1)
                    if isinstance(b, int) and b == 0:
                        act.wait_ge(init, 2)
                    for k in range(KC):
                        nc.scalar.activation(qf[:, p, k, :], mid[:, P * k:P * k + P], ACT.Identity, bias=g["qkb"][:, k:k + 1])
                    nc.scalar.activation(kf[:, p, :], mid[0:96, 256:384], ACT.Identity, bias=g["qkb"][0:96, 2:3])
                    nc.scalar.copy(v[:, s, 0:HD_A], mid[:, 384:400]).then_inc(qkv_out, 1)

            steps(act, step, -AHEAD, 1, 2, NB)

        @block.tensor
        def _(pe):
            def step(j, c):
                b1, sl1, r1 = at(j, c + 2)
                b2, sl2, r2 = at(j, c)
                b0, sl0, _ = at(j, c - 1)
                b3, sl3, _ = at(j, c + AHEAD)
                ahead, p1, pm, p2, done = (valid(j, c + d, NB) for d in (AHEAD, 2, 1, 0, -1))

                def scores(n):
                    if not p1:
                        return
                    if n == 0:
                        pe.wait_ge(stack_in[sl1], 16 * STACK_DMAS * (r1 + 1))
                        pe.wait_ge(ks_done, b1 + 1)
                    need(pe, max_done, 4 * b1 + n - 1)
                    nc.tensor.matmul(s1[:, n % 2, :], g["identb"][:], g["mask_q"][:], start=True, stop=False)
                    for h in range(4):
                        last = nc.tensor.matmul(s1[:, n % 2, P * h:P * h + P], qs[0:MROW, sl1, 4 * n + h, :], ks[0:MROW, sl1, :],
                                                start=False, stop=(h == 3))
                    last.then_inc(s1_done, 1)

                def shifted(u):
                    if not p2:
                        return
                    if u == 0:
                        pe.wait_ge(mrow_in[sl2], 16 * (r2 + 1))
                    need(pe, exp_done, 2 * b2 + u - 1)
                    for q in range(2):
                        nc.tensor.matmul(s2[:, u, q, :], g["identb"][:], g["mask_k"][:], start=True, stop=False)
                        last = nc.tensor.matmul(s2[:, u, q, :], ks[:, sl2, :], qs[:, sl2, 8 * u + 4 * q:8 * u + 4 * q + 4, :],
                                                start=False, stop=True)
                    last.then_inc(s2_done, 1)

                def values(u):
                    if not p2:
                        return
                    pe.wait_ge(exp_done, 2 * b2 + u + 1)
                    if u == 0:
                        need(pe, o_normed, b2)
                        pe.wait_ge(mT_out, cap(b2 + 2, NB))
                    for q in range(2):
                        row = VW * (2 * u + q)
                        last = nc.tensor.matmul(acc[row:row + VW, :], v[:, sl2, :], pt[:, u, 4 * q:4 * q + 4, :], start=True, stop=True)
                    last.then_inc(pv_done, 1)

                scores(0)
                shifted(0)
                if done:
                    pe.wait_ge(sums_out, b0 + 1)
                    for i in range(4):
                        last = nc.tensor.transpose(acc[:, P * i:P * i + P], sums[:, P * i:P * i + P], g["ident"][:])
                    last.then_inc(tb_done, 1)
                scores(1)
                scores(2)
                if done:
                    pe.wait_ge(o_normed, b0 + 1)
                    pe.wait_ge(qkv_out, cap(b0 + AHEAD + 1, NB))
                    for k in range(KC):
                        last = nc.tensor.transpose(mid[:, P * k:P * k + P], o[:, sl0 % 2, P * k:P * k + P], g["ident"][:])
                    last.then_inc(trO_done, 1)
                if pm:
                    pe.wait_ge(mx_split, b2 + 2)
                    need(pe, o_normed, b2)
                    if isinstance(b2, int) and b2 <= 0:
                        need(pe, mT_out, b2 + 1)
                    nc.tensor.matmul(acc[0:32, 384:512], mxs[:, (sl2 + 1) % 2].rearrange("p a h -> p (a h)"), g["nident"][:],
                                     start=True, stop=True).then_inc(mT_done, 1)
                shifted(1)
                if done:
                    pe.wait_ge(oT_done, b0 + 1)
                    for k in range(KC):
                        last = nc.tensor.matmul(mid[:, 0:D], oT[:, sl0 % 2, k, :], g["woT"][:, k, :], start=(k == 0), stop=(k == KC - 1))
                    last.then_inc(out_done, 1)
                values(0)
                if ahead:
                    pe.wait_ge(xn_done, b3 + 1)
                    need(pe, qkv_out, b3)
                    need(pe, x_added, b3 - AHEAD)
                    for k in range(KC):
                        last = nc.tensor.transpose(mid[:, P * k:P * k + P], xn[:, sl3 % 2, P * k:P * k + P], g["ident"][:])
                    last.then_inc(trx_done, 1)
                scores(3)
                values(1)
                if ahead:
                    pe.wait_ge(xnT_done, b3 + 1)
                    for m in range(2):
                        for k in range(KC):
                            nc.tensor.matmul(mid[:, P * m:P * m + P], g["wqT"][:, k, P * m:P * m + P], xnT[:, sl3 % 2, k, :],
                                             start=(k == 0), stop=(k == KC - 1))
                    for k in range(KC):
                        nc.tensor.matmul(mid[0:96, 256:384], g["wkT"][:, k, :], xnT[:, sl3 % 2, k, :], start=(k == 0), stop=(k == KC - 1))
                    for k in range(KC):
                        nc.tensor.matmul(mid[:, 384:400], xnT[:, sl3 % 2, k, :], g["wvT"][:, k, :], start=(k == 0), stop=False)
                    nc.tensor.matmul(mid[:, 384:400], g["ones_row"][:], g["vb_row"][:], start=False, stop=True).then_inc(proj_done, 1)

            steps(pe, step, -AHEAD, 1, 2, NB)


def cross_attention(nc, io, g, tmp):
    def sb(name, shape, dt=F32):
        return tmp.enter_context(nc.sbuf_tensor(name, shape, dt))

    def sem(name):
        return tmp.enter_context(nc.semaphore(name))

    x, s1, s2, mid, acc = g["x"], g["s1"], g["s2"], g["mid"], g["acc"]
    NUNIT = 2 * NB
    QK = 4 * P
    kst, of_head = g["kst"], g["of_head"]
    qst = sb("b_qst", [MROW, SLOTS, 4, P], F32R)
    q_spread = sb("b_q_spread", [MROW + 2, 2, UH, P], F32R)
    k_spread = sb("b_k_spread", [MROW, 2, UH, P], F32R)
    v = sb("b_v", [P, 2, NH_B, VW])
    stats = sb("b_stats", [P, 2, 6])
    mv = sb("b_mv", [P, 2, 2])
    rstd = sb("b_rstd", [P, 2, 2])
    xn = sb("b_xn", [P, 2, D])
    ctx = sb("b_ctx", [P, 2, CTX])
    xcT = sb("b_xcT", [P, 2, KC + 1, P])
    swapped = sb("b_swapped", [P, QK])
    by_cos = sb("b_by_cos", [P, QK])
    by_sin = sb("b_by_sin", [P, QK])
    qkhi = sb("b_qkhi", [P, 2, 2, 2, P], F32R)
    qklo = sb("b_qklo", [P, 2, 2, 2, P], F32R)
    mx = sb("b_mx", [P, UH])
    mxs = sb("b_mxs", [P, 2, 2, UH])
    mT = sb("b_mT", [32, 2, P], F32R)
    pt = sb("b_pt", [P, 2, 8, P])
    sums = sb("b_sums", [P, 512])
    rc = sb("b_rc", [P, UH])
    o = sb("b_o", [P, 2, D])
    oT = sb("b_oT", [P, 2, KC, P])

    q_in = [sem(f"q_in{i}") for i in range(SLOTS)]
    k_in = [sem(f"k_in{i}") for i in range(SLOTS)]
    mrow_in = [sem(f"b_mrow_in{i}") for i in range(SLOTS)]
    ctx_in = [sem(f"ctx_in{i}") for i in range(2)]
    (init, ln_stats, ln_aggr, eps_done, rstd_done, xn_done, trx_done, xcT_done, qk_done, qk_swapped, qk_out, sin_done,
     turned, qk_hi, qk_lo, ob_added, v_done, v_out, s1_done, max_done, mx_hi, mx_split, mT_done, mT_out, s2_done, exp_done,
     q_spread_a, q_spread_p, k_spread_p, k_spread_v, sums_out, tb_done, pv_done, rc_done, o_normed, trO_done, oT_done, out_done, x_added) = (sem("b_s_" + n) for n in (
        "init", "ln_stats", "ln_aggr", "eps_done", "rstd_done", "xn_done", "trx_done", "xcT_done", "qk_done", "qk_swapped",
        "qk_out", "sin_done", "turned", "qk_hi", "qk_lo", "ob_added", "v_done", "v_out", "s1_done", "max_done", "mx_hi",
        "mx_split", "mT_done", "mT_out", "s2_done", "exp_done", "q_spread_a", "q_spread_p", "k_spread_p", "k_spread_v", "sums_out", "tb_done", "pv_done", "rc_done", "o_normed", "trO_done", "oT_done",
        "out_done", "x_added"))
    LN_AHEAD, PROJ_AHEAD, TURN_AHEAD, V_AHEAD = 7, 6, 5, 2
    FIRST, ENTER, LOOPED, LAST = -7, 5, 5, NUNIT + 1
    TERMS = 3

    def at(j, c):
        return 4 * j + c, c % SLOTS, j + c // SLOTS

    def batch(j, c):
        return 2 * j + c // 2, (c // 2) % 2

    def has(j, c):
        return valid(j, c, NUNIT)

    def k_spread_half(eng, ops, j, c, u, done):
        if not has(j, c + 3):
            return
        b, s, r = at(j, c + 3)
        eng.wait_ge(k_in[s], 16 * TERMS * (r + 1))
        need(eng, s1_done, 4 * b - 4)
        ops.tensor_tensor(k_spread[:, s % 2, 8 * u:8 * u + 8, :].rearrange("p (n i) t -> p n i t", n=2),
                          kst[0:MROW, s, 2 * u:2 * u + 2, :].unsqueeze(2).broadcast_to([MROW, 2, 4, P]),
                          of_head[0:MROW].unsqueeze(1).unsqueeze(3).broadcast_to([MROW, 2, 4, P]), ALU.mult).then_inc(done, 1)

    with nc.Block() as block:
        @block.sync
        def _(sp):
            def stack(j, c, dst, w, parts, done):
                b, s, r = at(j, c + 4)
                half = c % 2
                bt, par = batch(j, c + 4 - half)
                sp.wait_ge(qk_lo, bt + 1)
                for n in range(TERMS):
                    sp.dma_start(dst[32 * n:32 * n + 32, s].bitcast(F32),
                                 parts[n][:, par, w, half, :].bitcast(F32)).then_inc(done[s], 16)

            def step(j, c):
                if has(j, c + 4):
                    b, s, r = at(j, c + 4)
                    need(sp, q_spread_a, b - 3)
                    need(sp, q_spread_p, b - 3)
                    stack(j, c, qst, 0, (qkhi, qkhi, qklo), q_in)
                if has(j, c + 1):
                    b, s, r = at(j, c + 1)
                    sp.wait_ge(mT_out, b + 1)
                    sp.dma_start(q_spread[MROW:MROW + 2, s % 2].bitcast(F32), mT[:, s % 2, :].bitcast(F32)).then_inc(mrow_in[s], 16)
                if c % 2 and has(j, c + LN_AHEAD):
                    b, p = batch(j, c + LN_AHEAD)
                    need(sp, trx_done, b - 1)
                    sp.dma_start(ctx[:, p, :], io["ctx"][b]).then_inc(ctx_in[p], 16)
                if has(j, c + 4):
                    b, s, r = at(j, c + 4)
                    need(sp, s2_done, 2 * b - 6)
                    stack(j, c, kst, 1, (qkhi, qklo, qkhi), k_in)

            steps(sp, step, FIRST, ENTER, LOOPED, LAST)

        @block.gpsimd
        def _(pool):
            nc.gpsimd.memset(v[:], 1.0).then_inc(init, 1)

            def step(j, c):
                if has(j, c + 1):
                    b, s, r = at(j, c + 1)
                    pool.wait_ge(q_in[s], 16 * TERMS * (r + 1))
                    need(pool, s2_done, 2 * b - 2)
                    nc.gpsimd.tensor_tensor(q_spread[0:MROW, s % 2, 8:16, :].rearrange("p (n i) t -> p n i t", n=2),
                                            qst[:, s, 2:4, :].unsqueeze(2).broadcast_to([MROW, 2, 4, P]),
                                            of_head[0:MROW].unsqueeze(1).unsqueeze(3).broadcast_to([MROW, 2, 4, P]), ALU.mult).then_inc(q_spread_p, 1)
                k_spread_half(pool, nc.gpsimd, j, c, 0, k_spread_p)
                if c % 2 == 0 and has(j, c + PROJ_AHEAD):
                    b, p = batch(j, c + PROJ_AHEAD)
                    pool.wait_ge(qk_swapped, b + 1)
                    need(pool, turned, b)
                    nc.gpsimd.tensor_tensor(by_sin[:].rearrange("p (a t) -> p a t", a=4), swapped[:].rearrange("p (a t) -> p a t", a=4),
                                            g["rope"][:, 0, b, :].unsqueeze(1).broadcast_to([P, 4, P]), ALU.mult).then_inc(sin_done, 1)
                if c % 2 and has(j, c + TURN_AHEAD):
                    b, p = batch(j, c + TURN_AHEAD)
                    pool.wait_ge(qk_hi, b + 1)
                    nc.gpsimd.tensor_tensor(qklo[:, p].rearrange("p a b t -> p (a b t)"), by_cos[:],
                                            qkhi[:, p].rearrange("p a b t -> p (a b t)").bitcast(F32), ALU.subtract).then_inc(qk_lo, 1)
                if c % 2 and has(j, c + LN_AHEAD):
                    b, p = batch(j, c + LN_AHEAD)
                    pool.wait_ge(ln_aggr, b + 1)
                    nc.gpsimd.tensor_tensor(rstd[:, p, 0:1], mv[:, p, 1:2], g["ln_eps"][:, 0:1], ALU.add).then_inc(eps_done, 1)
                    pool.wait_ge(eps_done, b + 1)
                    nc.gpsimd.tensor_tensor(rstd[:, p, 1:2], rstd[:, p, 0:1], g["ln_pow"][:, 0:1], ALU.pow).then_inc(rstd_done, 1)
                    pool.wait_ge(xn_done, b + 1)
                    nc.gpsimd.tensor_tensor(x[:, b, :], x[:, b, :], g["ob"][:, 1, :], ALU.add).then_inc(ob_added, 1)

            steps(pool, step, FIRST, ENTER, LOOPED, LAST)

        @block.vector
        def _(dve):
            def step(j, c):
                even = c % 2 == 0
                b1, sl1, _ = at(j, c + 2)
                p1, done = has(j, c + 2), has(j, c - 1)

                def row_max(n):
                    if p1:
                        if n == 0:
                            need(dve, mx_split, b1)
                        dve.wait_ge(s1_done, 4 * b1 + n + 1)
                        nc.vector.tensor_reduce(mx[:, 4 * n:4 * n + 4], s1[:, n % 2, :].rearrange("p (h k) -> p h k", h=4),
                                                AX.X, ALU.max).then_inc(max_done, 1)

                row_max(0)
                if not even and has(j, c + TURN_AHEAD):
                    b, _ = batch(j, c + TURN_AHEAD)
                    dve.wait_ge(sin_done, b + 1)
                    dve.wait_ge(qk_out, b + 1)
                    nc.vector.tensor_tensor(by_cos[:], by_cos[:], by_sin[:], ALU.add).then_inc(turned, 1)
                row_max(1)
                if done:
                    b0, _, _ = at(j, c - 1)
                    half = (c - 1) % 2
                    bt, par = batch(j, c - 1 - half)
                    dve.wait_ge(tb_done, b0 + 1)
                    pv = acc[:].rearrange("p (i n) -> p i n", i=4)[:, :, 0:4 * (HD_B + 1)].rearrange("p i (g w) -> p i g w", g=4)
                    rcv = rc[:].rearrange("p (i g) -> p i g", i=4)
                    nc.vector.reciprocal(rcv, pv[:, :, :, HD_B]).then_inc(rc_done, 1)
                    dve.wait_ge(rc_done, b0 + 1)
                    nc.vector.tensor_tensor(o[:, par, P * half:P * half + P].rearrange("p (i g d) -> p i g d", i=4, g=4), pv[:, :, :, 0:HD_B],
                                            rcv.unsqueeze(3).broadcast_to([P, 4, 4, HD_B]), ALU.mult).then_inc(o_normed, 1)
                ln = not even and has(j, c + LN_AHEAD)
                b, p = batch(j, c + LN_AHEAD) if ln else (0, 0)
                if ln:
                    nc.vector.bn_stats(stats[:, p, :], x[:, b, :]).then_inc(ln_stats, 1)
                if ln:
                    dve.wait_ge(ln_stats, b + 1)
                row_max(2)
                if ln:
                    nc.vector.bn_aggr(mv[:, p, :], stats[:, p, :]).then_inc(ln_aggr, 1)
                row_max(3)
                if not even and has(j, c - 3) and has(j, c - 2):
                    b0, _ = batch(j, c - 3)
                    dve.wait_ge(out_done, b0 + 1)
                    dve.wait_ge(ob_added, b0 + 1)
                    nc.vector.tensor_tensor(x[:, b0, :], mid[:, 0:D], x[:, b0, :], ALU.add).then_inc(x_added, 1)
                if p1:
                    dve.wait_ge(max_done, 4 * b1 + 4)
                    need(dve, mT_done, b1 - 1)
                    nc.vector.tensor_copy(mxs[:, sl1 % 2, 0, :].bitcast(F32R), mx[:]).then_inc(mx_hi, 1)
                    dve.wait_ge(mx_hi, b1 + 1)
                    nc.vector.tensor_tensor(mxs[:, sl1 % 2, 1, :], mx[:], mxs[:, sl1 % 2, 0, :], ALU.subtract).then_inc(mx_split, 1)
                k_spread_half(dve, nc.vector, j, c, 1, k_spread_v)
                if ln:
                    dve.wait_ge(rstd_done, b + 1)
                    need(dve, trx_done, b - 1)
                    nc.vector.tensor_scalar(xn[:, p, :], x[:, b, :], mv[:, p, 0:1], rstd[:, p, 1:2],
                                            ALU.subtract, ALU.mult).then_inc(xn_done, 1)
                if even and has(j, c + PROJ_AHEAD):
                    b, p = batch(j, c + PROJ_AHEAD)
                    dve.wait_ge(qk_swapped, b + 1)
                    need(dve, qk_lo, b)
                    nc.vector.tensor_tensor(by_cos[:].rearrange("p (a t) -> p a t", a=4), mid[:].rearrange("p (a t) -> p a t", a=4),
                                            g["rope"][:, 1, b, :].unsqueeze(1).broadcast_to([P, 4, P]), ALU.mult).then_inc(qk_out, 1)

            steps(dve, step, FIRST, ENTER, LOOPED, LAST)

        @block.scalar
        def _(act):
            def step(j, c):
                even = c % 2 == 0

                def exps(u):
                    if has(j, c):
                        b, s, _ = at(j, c)
                        act.wait_ge(s2_done, 2 * b + u + 1)
                        need(act, pv_done, 2 * b + u - 1)
                        nc.scalar.activation(pt[:, u].rearrange("p h q -> p (h q)"), s2[:, u].rearrange("p a n -> p (a n)"),
                                             ACT.Exp, scale=HD_B ** -0.5).then_inc(exp_done, 1)

                def spread_queries():
                    if has(j, c + 1):
                        b, s, r = at(j, c + 1)
                        act.wait_ge(q_in[s], 16 * TERMS * (r + 1))
                        need(act, s2_done, 2 * b - 2)
                        for i in range(4):
                            last = nc.scalar.activation(q_spread[0:MROW, s % 2, 0:8].rearrange("p (n i) t -> p n i t", i=4)[:, :, i, :], qst[:, s, 0:2, :],
                                                        ACT.Copy, scale=of_head[0:MROW, i:i + 1])
                        last.then_inc(q_spread_a, 1)

                if has(j, c - 1):
                    b, s, _ = at(j, c - 1)
                    act.wait_ge(pv_done, 2 * b + 2)
                    need(act, tb_done, b)
                    nc.scalar.copy(sums[:], acc[:]).then_inc(sums_out, 1)
                exps(0)
                if even and has(j, c + V_AHEAD):
                    b, p = batch(j, c + V_AHEAD)
                    act.wait_ge(v_done, b + 1)
                    if isinstance(b, int) and b == 0:
                        act.wait_ge(init, 1)
                    nc.scalar.copy(v[:, p, :, 0:HD_B], mid[:, 0:D].rearrange("p (h d) -> p h d", h=NH_B)).then_inc(v_out, 1)
                if not even and has(j, c - 3) and has(j, c - 2):
                    b, p = batch(j, c - 3)
                    act.wait_ge(trO_done, b + 1)
                    nc.scalar.copy(oT[:, p].rearrange("p k t -> p (k t)"), mid[:, 0:D]).then_inc(oT_done, 1)
                if not even and has(j, c + TURN_AHEAD):
                    b, p = batch(j, c + TURN_AHEAD)
                    act.wait_ge(turned, b + 1)
                    if not (isinstance(b, int) and b < 2):
                        _, s_2, r_2 = at(j, c + 2)
                        act.wait_ge(q_in[s_2], 16 * TERMS * (r_2 + 1))
                        act.wait_ge(k_in[s_2], 16 * TERMS * (r_2 + 1))
                    nc.scalar.copy(qkhi[:, p].rearrange("p a b t -> p (a b t)"), by_cos[:]).then_inc(qk_hi, 1)
                if even and has(j, c + PROJ_AHEAD):
                    b, p = batch(j, c + PROJ_AHEAD)
                    act.wait_ge(trx_done, b + 1)
                    nc.scalar.copy(xcT[:, p].rearrange("p k t -> p (k t)"), mid[:, 0:3 * P]).then_inc(xcT_done, 1)
                if even:
                    spread_queries()
                if has(j, c + 1):
                    b, s, _ = at(j, c + 1)
                    act.wait_ge(mT_done, b + 1)
                    if not (isinstance(b, int) and b < 2):
                        _, s_2, r_2 = at(j, c - 1)
                        act.wait_ge(mrow_in[s_2], 16 * (r_2 + 1))
                    nc.scalar.copy(mT[:, s % 2, :], acc[0:32, 384:512]).then_inc(mT_out, 1)
                exps(1)
                if not even:
                    spread_queries()
                if even and has(j, c + PROJ_AHEAD):
                    b, p = batch(j, c + PROJ_AHEAD)
                    act.wait_ge(qk_done, b + 1)
                    need(act, sin_done, b)
                    nc.scalar.copy(swapped[0:64, :], mid[64:P, :])
                    nc.scalar.copy(swapped[64:P, :], mid[0:64, :]).then_inc(qk_swapped, 1)

            steps(act, step, FIRST, ENTER, LOOPED, LAST)

        @block.tensor
        def _(pe):
            def step(j, c):
                odd = c % 2 == 1
                b1, sl1, r1 = at(j, c + 2)
                b2, sl2, r2 = at(j, c)
                p1, p2 = has(j, c + 2), has(j, c)
                half2 = c % 2
                _, vpar = batch(j, c - half2)

                def scores(n):
                    if not p1:
                        return
                    if n == 0:
                        pe.wait_ge(q_in[sl1], 16 * TERMS * (r1 + 1))
                        pe.wait_ge(k_spread_p, b1 + 1)
                    if n == 2:
                        pe.wait_ge(k_spread_v, b1 + 1)
                    need(pe, max_done, 4 * b1 + n - 1)
                    nc.tensor.matmul(s1[:, n % 2, :], qst[:, sl1, n, :], k_spread[:, sl1 % 2, 4 * n:4 * n + 4, :],
                                     start=True, stop=True).then_inc(s1_done, 1)

                def shifted(u):
                    if not p2:
                        return
                    if u == 0:
                        pe.wait_ge(q_spread_a, b2 + 1)
                        pe.wait_ge(mrow_in[sl2], 16 * (r2 + 1))
                    else:
                        pe.wait_ge(q_spread_p, b2 + 1)
                    need(pe, exp_done, 2 * b2 + u - 1)
                    for q in range(2):
                        last = nc.tensor.matmul(s2[:, u, q, :], kst[:, sl2, 2 * u + q, :], q_spread[:, sl2 % 2, 8 * u + 4 * q:8 * u + 4 * q + 4, :],
                                                start=True, stop=True)
                    last.then_inc(s2_done, 1)

                def values(u, d):
                    if not has(j, c + d):
                        return
                    b, _, _ = at(j, c + d)
                    half = (c + d) % 2
                    bt, par = batch(j, c + d - half)
                    pe.wait_ge(exp_done, 2 * b + u + 1)
                    if u == 0:
                        need(pe, o_normed, b)
                        pe.wait_ge(mT_out, cap(b + 2, NUNIT))
                        if half == 0:
                            pe.wait_ge(v_out, bt + 1)
                    for h in range(8):
                        row, col = VW * (2 * u + h // 4), P * (h % 4)
                        head = UH * half + 4 * (h % 4) + 2 * u + h // 4
                        last = nc.tensor.matmul(acc[row:row + VW, col:col + P], v[:, par, head, :], pt[:, u, h, :],
                                                start=True, stop=True)
                    last.then_inc(pv_done, 1)

                scores(0)
                values(1, -1)
                if not odd and has(j, c + V_AHEAD):
                    b, p = batch(j, c + V_AHEAD)
                    need(pe, x_added, b - 2)
                    pe.wait_ge(qk_out, cap(b + 2, NB))
                    nc.tensor.matmul(mid[:, 0:D], xcT[:, p, KC, :], g["wkv"][:, D:2 * D], start=True, stop=True).then_inc(v_done, 1)
                shifted(0)
                scores(1)
                if has(j, c - 1):
                    b0, _, _ = at(j, c - 1)
                    pe.wait_ge(sums_out, b0 + 1)
                    for i in range(4):
                        last = nc.tensor.matmul(acc[:, P * i:P * i + 4 * (HD_B + 1)], sums[:, P * i:P * i + P], g["gather"][:], start=True, stop=True)
                    last.then_inc(tb_done, 1)
                if not odd and has(j, c + PROJ_AHEAD):
                    b, p = batch(j, c + PROJ_AHEAD)
                    pe.wait_ge(xn_done, b + 1)
                    need(pe, v_out, b - 1)
                    need(pe, qk_out, b)
                    pe.wait_ge(ctx_in[p], 16 * (j + (c + PROJ_AHEAD) // 4 + 1))
                    for k in range(KC):
                        nc.tensor.transpose(mid[:, P * k:P * k + P], xn[:, p, P * k:P * k + P], g["ident"][:])
                    nc.tensor.transpose(mid[:, 2 * P:3 * P], ctx[:, p, :], g["ident"][:]).then_inc(trx_done, 1)
                scores(2)
                if odd and has(j, c - 3) and has(j, c - 2):
                    b, p = batch(j, c - 3)
                    pe.wait_ge(o_normed, 2 * b + 2)
                    pe.wait_ge(qk_out, cap(b + 5, NB))
                    pe.wait_ge(v_out, cap(b + 3, NB))
                    for k in range(KC):
                        last = nc.tensor.transpose(mid[:, P * k:P * k + P], o[:, p, P * k:P * k + P], g["ident"][:])
                    last.then_inc(trO_done, 1)
                shifted(1)
                if has(j, c + 1):
                    pe.wait_ge(mx_split, b2 + 2)
                    need(pe, o_normed, b2)
                    if isinstance(b2, int) and b2 <= 0:
                        need(pe, mT_out, b2 + 1)
                    nc.tensor.matmul(acc[0:32, 384:512], mxs[:, (sl2 + 1) % 2].rearrange("p a h -> p (a h)"), g["nident"][:],
                                     start=True, stop=True).then_inc(mT_done, 1)
                scores(3)
                if odd and has(j, c - 3) and has(j, c - 2):
                    b, p = batch(j, c - 3)
                    pe.wait_ge(oT_done, b + 1)
                    for k in range(KC):
                        last = nc.tensor.matmul(mid[:, 0:D], oT[:, p, k, :], g["wout"][:, k, :], start=(k == 0), stop=(k == KC - 1))
                    last.then_inc(out_done, 1)
                if not odd and has(j, c + PROJ_AHEAD):
                    b, p = batch(j, c + PROJ_AHEAD)
                    pe.wait_ge(xcT_done, b + 1)
                    for half in range(2):
                        for k in range(KC):
                            nc.tensor.matmul(mid[:, P * half:P * half + P], g["wqB"][:, k, half, :], xcT[:, p, k, :], start=(k == 0), stop=(k == KC - 1))
                    for half in range(2):
                        last = nc.tensor.matmul(mid[:, P * (2 + half):P * (3 + half)], g["wkB"][:, half, :], xcT[:, p, KC, :], start=True, stop=True)
                    last.then_inc(qk_done, 1)
                values(0, 0)

            steps(pe, step, FIRST, ENTER, LOOPED, LAST)


def unit(j, c):
    if c >= UG:
        j, c = j + 1, c - UG
    if isinstance(j, int) and j == NG:
        t, q = divmod(c, CB)
        rows = LASTC if q == CB - 1 else P
        return NG, c, t, q, CG * NG + q, rows, q == 0, q == CB - 1
    if c < CA * NT:
        t, q = divmod(c, CA)
        return j, c, t, q, CG * j + q, P, q == 0, q == CA - 1
    t, q = divmod(c - CA * NT, CB)
    return j, c, t, CB + q, CG * j + CA + q, P, q == 0, q == CB - 1


def mixture(nc, io, g, out, tmp):
    def sb(name, shape, dt=F32):
        return tmp.enter_context(nc.sbuf_tensor(name, shape, dt))

    def sem(name):
        return tmp.enter_context(nc.semaphore(name))

    x, ident, identb, s1, s2, last2 = g["x"], g["ident"], g["identb"], g["s1"], g["s2"], g["last2"]
    NSLOT = 2 * CB
    xhi = sb("xhi", [P, KC, TOK], F32R)
    xlo = sb("xlo", [P, KC, TOK], F32R)
    y = sb("y", [P, 2, TOK])
    combT = sb("combT", [96, TOK], BF16)
    sel = sb("sel", [96, FH], BF16)
    wgu = sb("wgu", [P, NSLOT, 2, KC, 2, P], F32R)
    wd = sb("wd", [P, NSLOT, 2, D], F32R)
    raw_gu = sb("raw_gu", [P, 2, KC, RAW])
    raw_d = sb("raw_d", [P, CB, D])
    logits_ps, yT = last2[:, 1, :], last2

    raw_in, sel_ok, w_hi, w_lo = sem("raw_in"), sem("sel_ok"), sem("w_hi"), sem("w_lo")
    (ln_stats, ln_aggr, eps_done, rstd_done, xn_done, trx_done, x_full, x_hi, x_lo, lgT_done, lgT_out, logit_done) = (sem("m_" + n) for n in (
        "ln_stats", "ln_aggr", "eps_done", "rstd_done", "xn_done", "trx_done", "x_full", "x_hi", "x_lo", "lgT_done", "lgT_out", "logit_done"))
    r_dve, r_exp, comb_trans, comb_out = sem("r_dve"), sem("r_exp"), sem("comb_trans"), sem("comb_out")
    (gate_done, up_done, silu_done, prod_done, h_done, h_hi, h_lo, down_done, y_added) = (sem("u_" + n) for n in (
        "gate_done", "up_done", "silu_done", "prod_done", "h_done", "h_hi", "h_lo", "down_done", "y_added"))
    y_zero, yt_done, x_final, stored = sem("y_zero"), sem("yt_done"), sem("x_final"), sem("stored")
    comb_ready, raw_tail = sem("comb_ready"), sem("raw_tail")
    GROUP_DMAS = 9
    FREE = 4

    BT = TT // P
    NR = NB // BT
    stats = sb("m_stats", [P, NB, 6])
    mv = sb("m_mv", [P, NB, 2])
    rstd = sb("m_rstd", [P, 2, NB])
    lg = sb("lg", [P, NB, NE])
    pr = sb("pr", [P, NB, NE + 4])
    rest = sb("rest", [P, NB, NE + 4])
    top = sb("top", [P, NB, 8])
    red = sb("red", [P, 4, NB])
    comb = sb("comb", [P, NB, NE + NSH])
    c3 = sb("c3", [P, NB, 96], BF16)
    sg = sb("silu_gate", [P, 2, TT])
    prod = sb("prod", [P, TT])
    h = sb("h_full", [P, 2, TT])
    xn = h[:].rearrange("p a (i d) -> p (a i) d", d=D)
    xf = sg
    lgT = prod
    hhi = sb("h_hi", [P, 4, TT], F32R)
    hlo = sb("h_lo", [P, 4, TT], F32R)

    def mix_steps(eng, step, last):
        for c in range(2):
            step(0, c)
        with eng.Fori(0, NG) as j:
            for c in range(2, UG + 2):
                step(j, c)
        for c in range(NG * UG + 2, last + 1):
            step(c // UG, c % UG) if c < (NG + 1) * UG else step(NG, c - NG * UG)

    def exists(j, c):
        return not isinstance(j, int) or 0 <= UG * j + c < NU

    def back(j, c, n):
        c -= n
        return (j, c) if c >= 0 else (j - 1, c + UG)

    def split_at(j, c):
        if isinstance(j, int) and j == NG:
            return (CB - 1, CB - 1, LASTC) if c == 2 else None
        if 3 <= c <= 18 and c % 3 == 0:
            return CB + c // 3 - 1, c // 3 - 1, P
        if c >= 24 and c % 4 == 0 and c // 4 - 6 < CA:
            return c // 4 - 6, c // 4 - 6, P
        return None

    def split_count(j, c):
        if isinstance(j, int) and j == NG:
            return CG * NG + CB - 1
        return CG * j + (CA + c // 3 - 1 if c <= 18 else CG + c // 4 - 6)

    def raw_wait(eng, j, c):
        if isinstance(j, int) and j == NG:
            eng.wait_ge(raw_tail, 16)
        else:
            eng.wait_ge(raw_in, 16 * GROUP_DMAS * (2 * j + (2 if c <= 18 else 3)))

    with nc.Block() as block:
        @block.sync
        def _(sp):
            down = io["w_down"].rearrange("e i n -> (e i) n")

            def columns(e, n, lo, first, width):
                for w, name in enumerate(("w_gate", "w_up")):
                    for k in range(KC):
                        sp.dma_start(raw_gu[:, w, k, lo:lo + n * width].rearrange("p (e i) -> p e i", e=n),
                                     io[name][e:e + n, P * k:P * k + P, first:first + width].rearrange("e p i -> p e i")).then_inc(raw_in, 16)

            for j in range(NG):
                need(sp, w_lo, CG * j)
                cut = CA * P - 3 * FE
                columns(8 * j, 3, 0, 0, FE)
                columns(8 * j + 3, 1, 3 * FE, 0, cut)
                row = CG * P * j
                sp.dma_start(raw_d[:, 0:CA, :], down[row:row + CA * P, :].rearrange("(c p) n -> p c n", p=P)).then_inc(raw_in, 16)
                sp.wait_ge(w_lo, CG * j + CA)
                columns(8 * j + 3, 1, 0, cut, FE - cut)
                columns(8 * j + 4, 4, FE - cut, 0, FE)
                row += CA * P
                sp.dma_start(raw_d[:, 0:CB, :], down[row:row + CB * P, :].rearrange("(c p) n -> p c n", p=P)).then_inc(raw_in, 16)
            sp.wait_ge(w_lo, CG * NG)
            for w, name in enumerate(("sh_gate", "sh_up")):
                for k in range(KC):
                    for half in range(2):
                        cols = slice(2 * FE * half, 2 * FE * (half + 1))
                        sp.dma_start(raw_gu[:, w, k, cols], io[name][P * k:P * k + P, cols]).then_inc(raw_in, 16)
            sp.dma_start(raw_d[:, 0:CA, :], io["sh_down"][0:CA * P, :].rearrange("(c p) n -> p c n", p=P)).then_inc(raw_in, 16)
            sp.dma_start(raw_d[0:LASTC, CA, :], io["sh_down"][CA * P:NSH * FE, :]).then_inc(raw_tail, 16)
            for n in range(4):
                sp.wait_ge(x_final, 4 * n + 4)
                sp.dma_start(out[4 * n:4 * n + 4].rearrange("b p d -> p b d"), x[:, 4 * n:4 * n + 4, :]).then_inc(stored, 16)
            sp.wait_ge(stored, 64)

        @block.gpsimd
        def _(pool):
            def split_lo(slot, raw, rows, n):
                pool.wait_ge(w_hi, n + 1)
                nc.gpsimd.tensor_tensor(wgu[:, slot, :, :, 1, 0:rows].rearrange("p w k n -> p (w k) n"),
                                        raw_gu[:, :, :, P * raw:P * raw + rows].rearrange("p w k n -> p (w k) n"),
                                        wgu[:, slot, :, :, 0, 0:rows].rearrange("p w k n -> p (w k) n").bitcast(F32), ALU.subtract)
                nc.gpsimd.tensor_tensor(wd[0:rows, slot, 1, :], raw_d[0:rows, raw, :],
                                        wd[0:rows, slot, 0, :].bitcast(F32), ALU.subtract).then_inc(w_lo, 1)

            for n in range(NR):
                four = slice(BT * n, BT * n + BT)
                pool.wait_ge(ln_aggr, BT * n + BT)
                nc.gpsimd.tensor_tensor(rstd[:, 0, four], mv[:, four, 1], g["ln_eps"][:, 0:1].broadcast_to([P, BT]), ALU.add).then_inc(eps_done, 1)
                pool.wait_ge(eps_done, n + 1)
                nc.gpsimd.tensor_tensor(rstd[:, 1, four], rstd[:, 0, four], g["ln_pow"][:, 0:1].broadcast_to([P, BT]), ALU.pow).then_inc(rstd_done, 1)
            nc.gpsimd.memset(c3[:], 0.0).then_inc(y_zero, 1)
            nc.gpsimd.memset(sel[:], 1.0).then_inc(sel_ok, 1)
            pool.wait_ge(sel_ok, 1)
            nc.gpsimd.affine_select(out=sel[0:32], in_=sel[0:32], compare_op=ALU.is_ge, fill=0.0, base=0,
                                    pattern=[[1, FH]], channel_multiplier=-FE).then_inc(sel_ok, 1)
            pool.wait_ge(sel_ok, 2)
            nc.gpsimd.affine_select(out=sel[0:32], in_=sel[0:32], compare_op=ALU.is_ge, fill=0.0, base=FE - 1,
                                    pattern=[[-1, FH]], channel_multiplier=FE).then_inc(sel_ok, 1)
            nc.gpsimd.memset(y[:, 0], 0.0).then_inc(down_done, FREE)
            nc.gpsimd.memset(y[:, 1], 0.0).then_inc(y_added, 1)
            for q in range(CA):
                split_lo(q, q, P, q)

            def step(j, c):
                u = UG * j + c
                if exists(j, c):
                    rows = unit(j, c)[5]
                    pool.wait_ge(h_hi, u + 1)
                    pool.wait_ge(down_done, u - 3 + FREE)
                    nc.gpsimd.tensor_tensor(hlo[0:rows, c % 4, :], h[0:rows, c % 2, :], hhi[0:rows, c % 4, :].bitcast(F32),
                                            ALU.subtract).then_inc(h_lo, 1)
                at = split_at(j, c)
                if at:
                    split_lo(*at, split_count(j, c))

            mix_steps(pool, step, NU - 1)

        @block.scalar
        def _(act):
            def split_hi(slot, raw, rows, n):
                nc.scalar.copy(wgu[:, slot, :, :, 0, 0:rows].rearrange("p w k n -> p (w k) n"),
                               raw_gu[:, :, :, P * raw:P * raw + rows].rearrange("p w k n -> p (w k) n"))
                nc.scalar.copy(wd[0:rows, slot, 0, :], raw_d[0:rows, raw, :]).then_inc(w_hi, 1)

            def logits_out(n):
                act.wait_ge(lgT_done, n + 1)
                need(act, logit_done, n)
                nc.scalar.copy(lgT[0:NE + 1, :], s2[0:NE + 1, 0, 0, :]).then_inc(lgT_out, 1)

            for n in range(NR):
                if n:
                    act.wait_ge(lgT_done, n)
                    act.wait_ge(x_lo, n)
                for a in range(2):
                    act.wait_ge(trx_done, 2 * n + a + 1)
                    src = s1[:, a, :].rearrange("p (i k t) -> p i k t", i=2, k=KC)
                    nc.scalar.copy(xf[:, :, 2 * P * a:2 * P * a + 2 * P].rearrange("p k (i t) -> p i k t", i=2), src).then_inc(x_full, 1)
                    nc.scalar.copy(xhi[:, :, TT * n + 2 * P * a:TT * n + 2 * P * a + 2 * P].rearrange("p k (i t) -> p i k t", i=2), src).then_inc(x_hi, 1)
                logits_out(n)
            act.wait_ge(raw_in, 16 * GROUP_DMAS)
            split_hi(0, 0, P, 0)
            act.wait_ge(r_dve, 2)
            nc.scalar.activation(pr[:, :, 0:NE], lg[:], ACT.Exp).then_inc(r_exp, 1)
            nc.scalar.activation(comb[:, :, NE], logits_ps[:, 0:NB * (NE + 1)].rearrange("p (b e) -> p b e", b=NB)[:, :, NE],
                                 ACT.Exp, scale=-1.0).then_inc(r_exp, 1)
            for q in range(1, CA):
                split_hi(q, q, P, q)
            for n in range(4):
                act.wait_ge(comb_trans, n + 1)
                nc.scalar.copy(combT[:, TT * n:TT * n + TT], s2[0:96, n % 2, 1, 0:TT // 2].bitcast(BF16)).then_inc(comb_out, 1)

            def step(j, c):
                u = UG * j + c
                if exists(j, c):
                    rows = unit(j, c)[5]
                    act.wait_ge(gate_done, u + 1)
                    need(act, prod_done, u - 1)
                    nc.scalar.activation(sg[0:rows, c % 2, :], s1[0:rows, c % 2, :], ACT.Silu).then_inc(silu_done, 1)
                jb, cb = back(j, c, 1)
                if exists(jb, cb):
                    rows = unit(jb, cb)[5]
                    act.wait_ge(h_done, u)
                    act.wait_ge(down_done, u - 4 + FREE)
                    nc.scalar.copy(hhi[0:rows, cb % 4, :], h[0:rows, cb % 2, :]).then_inc(h_hi, 1)
                at = split_at(j, c)
                if at:
                    raw_wait(act, j, c)
                    act.wait_ge(down_done, FREE + UG * j + (0 if c <= 18 else CA * NT))
                    split_hi(*at, None)

            mix_steps(act, step, NU)

        @block.vector
        def _(dve):
            nc.vector.memset(pr[:, :, NE:NE + 4], -1.0).then_inc(r_dve, 1)

            def moments(n):
                for b in range(BT * n, BT * n + BT):
                    nc.vector.bn_stats(stats[:, b, :], x[:, b, :]).then_inc(ln_stats, 1)
                dve.wait_ge(ln_stats, BT * n + BT)
                for b in range(BT * n, BT * n + BT):
                    nc.vector.bn_aggr(mv[:, b, :], stats[:, b, :]).then_inc(ln_aggr, 1)

            def normalised(n):
                dve.wait_ge(rstd_done, n + 1)
                need(dve, trx_done, 2 * n)
                for i in range(BT):
                    b = BT * n + i
                    last = nc.vector.tensor_scalar(xn[:, i, :], x[:, b, :], mv[:, b, 0:1], rstd[:, 1, b:b + 1], ALU.subtract, ALU.mult)
                last.then_inc(xn_done, 1)

            def lo_parts(n):
                dve.wait_ge(x_hi, 2 * n + 2)
                nc.vector.tensor_tensor(xlo[:, :, TT * n:TT * n + TT], xf[:], xhi[:, :, TT * n:TT * n + TT].bitcast(F32),
                                        ALU.subtract).then_inc(x_lo, 1)

            moments(0)
            for n in range(NR):
                if n + 1 < NR:
                    moments(n + 1)
                normalised(n)
                if n:
                    lo_parts(n - 1)
            lo_parts(NR - 1)
            dve.wait_ge(sel_ok, 3)
            nc.vector.tensor_copy(sel[32:64], sel[0:32]).then_inc(sel_ok, 1)
            nc.vector.tensor_copy(sel[64:96], sel[0:32]).then_inc(sel_ok, 1)
            made = [1]

            def then(ins, *more):
                made[0] += 1
                ins.then_inc(r_dve, 1)
                dve.wait_ge(r_dve, made[0])

            lps = logits_ps[:, 0:NB * (NE + 1)].rearrange("p (b e) -> p b e", b=NB)[:, :, 0:NE]
            wide = lambda a: a.unsqueeze(2).broadcast_to([P, NB, NE])
            dve.wait_ge(logit_done, NR)
            nc.vector.tensor_reduce(red[:, 0, :], lps, AX.X, ALU.max).then_inc(ln_stats, 1)
            dve.wait_ge(ln_stats, NB + 1)
            then(nc.vector.tensor_tensor(lg[:], lps, wide(red[:, 0, :]), ALU.subtract))
            dve.wait_ge(r_exp, 1)
            then(nc.vector.tensor_reduce(red[:, 1, :], pr[:, :, 0:NE], AX.X, ALU.add))
            then(nc.vector.reciprocal(red[:, 1, :], red[:, 1, :]))
            then(nc.vector.tensor_tensor(pr[:, :, 0:NE], pr[:, :, 0:NE], wide(red[:, 1, :]), ALU.mult))
            for b in range(NB):
                last = nc.vector.max(out=top[:, b, :], in_=pr[:, b, 0:NE])
            then(last)
            then(nc.vector.memset(top[:, :, TOPK:8], -1.0))
            for b in range(NB):
                last = nc.vector.match_replace(out=rest[:, b, :], in_to_replace=top[:, b, :], in_values=pr[:, b, :], imm_value=0.0)
            then(last)
            then(nc.vector.tensor_tensor(comb[:, :, 0:NE], pr[:, :, 0:NE], rest[:, :, 0:NE], ALU.subtract))
            then(nc.vector.tensor_reduce(red[:, 2, :], comb[:, :, 0:NE], AX.X, ALU.add))
            then(nc.vector.tensor_scalar(red[:, 2, :], red[:, 2, :], 1e-9, None, ALU.max))
            then(nc.vector.reciprocal(red[:, 2, :], red[:, 2, :]))
            then(nc.vector.tensor_tensor(comb[:, :, 0:NE], comb[:, :, 0:NE], wide(red[:, 2, :]), ALU.mult))
            dve.wait_ge(r_exp, 2)
            then(nc.vector.tensor_scalar(red[:, 3, :], comb[:, :, NE], 1.0, None, ALU.add))
            then(nc.vector.reciprocal(red[:, 3, :], red[:, 3, :]))
            then(nc.vector.tensor_copy(comb[:, :, NE:NE + NSH], red[:, 3, :].unsqueeze(2).broadcast_to([P, NB, NSH])))
            dve.wait_ge(y_zero, 1)
            for i in range(3):
                part = nc.vector.tensor_copy(c3[:, :, 32 * i:32 * i + NE + NSH], comb[:])
                if i == 2:
                    part.then_inc(comb_ready, 1)
                else:
                    then(part)
                    then(nc.vector.tensor_tensor(comb[:], comb[:], c3[:, :, 32 * i:32 * i + NE + NSH], ALU.subtract))
            def step(j, c):
                u = UG * j + c
                if exists(j, c):
                    rows = unit(j, c)[5]
                    need(dve, h_done, u)
                    dve.wait_ge(silu_done, u + 1)
                    dve.wait_ge(up_done, u + 1)
                    nc.vector.tensor_tensor(prod[0:rows, :], s2[0:rows, c % 2, 0, :], sg[0:rows, c % 2, :], ALU.mult).then_inc(prod_done, 1)
                    dve.wait_ge(prod_done, u + 1)
                    need(dve, h_lo, u - 1)
                    nc.vector.tensor_tensor(h[0:rows, c % 2, :], s2[0:rows, c % 2, 1, :], prod[0:rows, :], ALU.mult).then_inc(h_done, 1)
                jb, cb = back(j, c, 2)
                if exists(jb, cb) and unit(jb, cb)[7]:
                    gj, gc, t = unit(jb, cb)[0:3]
                    dve.wait_ge(down_done, UG * jb + cb + 1 + FREE)
                    nc.vector.tensor_tensor(y[:, :, TT * t:TT * t + TT], last2[:], y[:, :, TT * t:TT * t + TT], ALU.add).then_inc(y_added, 1)

            mix_steps(dve, step, NU + 1)
            for b in range(NB):
                dve.wait_ge(yt_done, b + 1)
                nc.vector.tensor_tensor(x[:, b, :], s1[:, b % 2, 0:D], x[:, b, :], ALU.add).then_inc(x_final, 1)

        def tiles(j, c):
            if isinstance(j, int) and j == NG:
                return 2 * NT * NG + c // CB
            return 2 * NT * j + (c // CA if c < CA * NT else NT + (c - CA * NT) // CB)

        @block.tensor
        def _(pe):
            def transposes(n):
                pe.wait_ge(xn_done, n + 1)
                need(pe, x_hi, 2 * n)
                for a in range(2):
                    for i in range(2):
                        for k in range(KC):
                            last = nc.tensor.transpose(s1[:, a, D * i + P * k:D * i + P * k + P], xn[:, 2 * a + i, P * k:P * k + P], ident[:])
                    last.then_inc(trx_done, 1)

            transposes(0)
            for n in range(NR):
                pe.wait_ge(x_full, 2 * n + 2)
                for k in range(KC):
                    last = nc.tensor.matmul(s2[0:NE + 1, 0, 0, :], g["wr"][:, k, :], xf[:, k, :], start=(k == 0), stop=(k == KC - 1))
                last.then_inc(lgT_done, 1)
                if n + 1 < NR:
                    transposes(n + 1)
                pe.wait_ge(lgT_out, n + 1)
                for i in range(BT):
                    col = (NE + 1) * (BT * n + i)
                    last = nc.tensor.transpose(logits_ps[:, col:col + NE + 1], lgT[0:NE + 1, P * i:P * i + P], ident[0:NE + 1, 0:NE + 1])
                last.then_inc(logit_done, 1)

            def comb_transposes():
                pe.wait_ge(comb_ready, 1)
                for n in range(4):
                    need(pe, comb_out, n - 1)
                    for q in range(4):
                        last = nc.tensor.transpose(s2[0:96, n % 2, 1, 0:TT // 2].bitcast(BF16)[:, P * q:P * q + P], c3[:, 4 * n + q, :], identb[:])
                    last.then_inc(comb_trans, 1)
                pe.wait_ge(sel_ok, 5)
                pe.wait_ge(comb_out, 4)

            pe.wait_ge(x_lo, NR)
            pe.wait_ge(x_hi, NB // 2)

            def three(ps, w_hi_ap, w_lo_ap, m_hi, m_lo, start, stop):
                nc.tensor.matmul(ps, w_hi_ap, m_hi, start=start, stop=False)
                nc.tensor.matmul(ps, w_hi_ap, m_lo, start=False, stop=False)
                return nc.tensor.matmul(ps, w_lo_ap, m_hi, start=False, stop=stop)

            def step(j, c):
                u = UG * j + c
                if exists(j, c):
                    gj, gc, t, slot, chunk, rows, first, last_of = unit(j, c)
                    pe.wait_ge(w_lo, chunk + 1)
                    toks = slice(TT * t, TT * t + TT)
                    need(pe, silu_done, u - 1)
                    for w, ps, done in ((0, s1[0:rows, c % 2, :], gate_done), (1, s2[0:rows, c % 2, 0, :], up_done)):
                        if w == 1:
                            need(pe, prod_done, u - 1)
                        for k in range(KC):
                            last = three(ps, wgu[:, slot, w, k, 0, 0:rows], wgu[:, slot, w, k, 1, 0:rows], xhi[:, k, toks], xlo[:, k, toks],
                                         k == 0, k == KC - 1)
                        if w == 0:
                            last.then_inc(gate_done, 1)
                    if isinstance(u, int) and u == 0:
                        comb_transposes()
                    need(pe, h_done, u - 1)
                    nc.tensor.matmul(s2[0:rows, c % 2, 1, :], sel[:, bass.ds(P * chunk, rows)], combT[:, toks], start=True, stop=True).then_inc(up_done, 1)
                jb, cb = back(j, c, 2)
                if exists(jb, cb):
                    gj, gc, t, slot, chunk, rows, first, last_of = unit(jb, cb)
                    if first:
                        pe.wait_ge(y_added, tiles(gj, gc) + 1)
                    pe.wait_ge(h_lo, u - 1)
                    r = cb % 4
                    for m in range(2):
                        last = three(last2[:, m, :], wd[0:rows, slot, 0, P * m:P * m + P], wd[0:rows, slot, 1, P * m:P * m + P],
                                     hhi[0:rows, r, :], hlo[0:rows, r, :], first, last_of)
                    last.then_inc(down_done, 1)

            mix_steps(pe, step, NU + 1)
            pe.wait_ge(silu_done, NU)
            for b in range(NB):
                pe.wait_ge(y_added, (2 * NG + 1) * NT + 1)
                need(pe, x_final, b - 1)
                for m in range(2):
                    last = nc.tensor.transpose(s1[:, b % 2, P * m:P * m + P], y[:, m, P * b:P * b + P], ident[:])
                last.then_inc(yt_done, 1)


def build(nc, io, out):
    with ExitStack() as ctx:
        def sb(name, shape, dt=F32):
            return ctx.enter_context(nc.sbuf_tensor(name, shape, dt))

        g = {
            "x": sb("x_sb", [P, NB, D]),
            "ident": sb("ident", [P, P]), "nident": sb("nident", [P, P]), "identb": sb("identb", [P, P], BF16),
            "ln_eps": sb("ln_eps", [P, 4]), "ln_pow": sb("ln_pow", [P, 4]), "ones_row": sb("ones_row", [1, P]), "zero": sb("zero", [P, 4]),
            "wr": sb("wr", [P, KC, NE + 1]),
            "s1": ctx.enter_context(nc.psum_tensor("s1", [P, 2, 512], F32)),
            "s2": ctx.enter_context(nc.psum_tensor("s2", [P, 2, 2, 512], F32)),
            "x_in": ctx.enter_context(nc.semaphore("x_in")),
        }
        last2 = ctx.enter_context(nc.psum_tensor("last2", [P, 2, 512], F32))
        g["last2"], g["mid"], g["acc"] = last2, last2[:, 0, :], last2[:, 1, :]
        with ExitStack() as att:
            def sa(name, shape, dt=F32):
                return att.enter_context(nc.sbuf_tensor(name, shape, dt))

            g.update({
                "ob": sa("ob", [P, 2, D]), "vb_row": sa("vb_row", [1, HD_A]),
                "wqT": sa("wqT", [P, KC, D]), "woT": sa("woT", [P, KC, D]), "wkT": sa("wkT", [P, KC, 96]),
                "wvT": sa("wvT", [P, KC, HD_A]), "qkb": sa("qkb", [P, 3]),
                "wqB": sa("wqB", [P, KC, 2, P]), "wkB": sa("wkB", [P, 2, P]), "wkv": sa("wkv", [P, 2 * D]),
                "wout": sa("wout", [P, KC, D]), "rope": sa("rope", [P, 2, NB, P]),
                "kst": sa("kst", [MROW + 2, SLOTS, 4, P], F32R), "of_head": sa("of_head", [P, 4]), "qs": sa("qs", [P, SLOTS, UH, P], F32R),
                "gather": sa("gather", [P, 4 * (HD_B + 1)]),
                "mask_q": sa("mask_q", [P, 4, P], BF16), "mask_k": sa("mask_k", [P, 4, P], BF16),
            })
            with ExitStack() as tmp:
                prepare(nc, io, g, tmp)
            with ExitStack() as tmp:
                self_attention(nc, g, tmp)
            with ExitStack() as tmp:
                cross_attention(nc, io, g, tmp)
        with ExitStack() as tmp:
            mixture(nc, io, g, out, tmp)


_INS = [("x", "x"), ("ctx", "ctx_1024"), ("pos", "fside_BxSx2_0"), ("q_w", "L0_attn_q_w"), ("q_b", "L0_attn_q_b"),
        ("k_w", "L0_attn_k_w"), ("k_b", "L0_attn_k_b"), ("v_w", "L0_attn_v_w"), ("v_b", "L0_attn_v_b"),
        ("o_w", "L0_attn_o_w"), ("o_b", "L0_attn_o_b"), ("Wq", "L0_xattn_Wq"), ("Wkv", "L0_xattn_Wkv"),
        ("Wout", "L0_xattn_Wout"), ("bout", "L0_xattn_bout"), ("router_w", "L0_ffn_router_w"),
        ("w_gate", "L0_ffn_w_gate"), ("w_up", "L0_ffn_w_up"), ("w_down", "L0_ffn_w_down"),
        ("sh_gate", "L0_ffn_sh_gate"), ("sh_up", "L0_ffn_sh_up"), ("sh_down", "L0_ffn_sh_down"),
        ("sh_gate_w", "L0_ffn_sh_gate_w")]


def kernel(**inputs):
    import numpy as _np
    import concourse.bacc as _bacc
    from concourse import mybir as _mybir
    from concourse.bass_utils import run_bass_kernel_spmd as _run

    nc = _bacc.Bacc("TRN2", target_bir_lowering=False, num_devices=1)
    arrays, io = {}, {}
    for short, name in _INS:
        a = _np.ascontiguousarray(inputs[name])
        arrays[f"in_{short}"] = a
        io[short] = nc.dram_tensor(f"in_{short}", a.shape, _mybir.dt.from_np(a.dtype), kind="ExternalInput").ap()
    out = nc.dram_tensor("out_0", inputs["x"].shape, _mybir.dt.float32, kind="ExternalOutput").ap()
    build(nc, io, out)
    r = _run(nc, [arrays], core_ids=[0])
    return r.results[0]["out_0"]
```

```python
from contextlib import ExitStack

import concourse.bass as bass
from concourse import mybir

F32 = mybir.dt.float32
F32R = mybir.dt.float32r
BF16 = mybir.dt.bfloat16
ALU = mybir.AluOpType
ACT = mybir.ActivationFunctionType
AX = mybir.AxisListType

P = 128
NB = 16
D = 256
KC = D // P
UH = 16
HD_A = 16
HD_B = 8
NH_B = 32
CTX = 128
EPS = 1e-5
MASKED = -1e30
SLOTS = 4
MROW = 96
VW = 32
STACK_DMAS = 6

NE, TOPK, FE = 16, 4, 176
NSH = 4
FH = (NE + NSH) * FE
TOK = NB * P
TT = 512
NT = TOK // TT
CA, CB = 5, 6
CG = CA + CB
UG = CG * NT
NG = 2
NU = NG * UG + CB * NT
RAW = CB * P
LASTC = FH - (FH // P) * P

FREQ1 = 10000.0 ** -0.5
TWO_PI_HI = 6.28125
TWO_PI_LO = 2 * 3.141592653589793 - 6.28125
ROUND = 1.5 * 2 ** 23
PI_IN = 3.1415925


def need(eng, sem, value):
    if isinstance(value, int) and value <= 0:
        return
    eng.wait_ge(sem, value)


def valid(j, c, n):
    return not isinstance(j, int) or 0 <= 4 * j + c < n


def cap(value, most):
    return min(value, most) if isinstance(value, int) else value


def steps(eng, step, first, enter, looped, last):
    for c in range(first, enter):
        step(0, c)
    with eng.Fori(0, looped) as j:
        for c in range(enter, enter + 4):
            step(j, c)
    for c in range(enter + 4 * looped, last + 1):
        step(0, c)


def prepare(nc, io, g, tmp):
    def sb(name, shape, dt=F32):
        return tmp.enter_context(nc.sbuf_tensor(name, shape, dt))

    def sem(name):
        return tmp.enter_context(nc.semaphore(name))

    qo_nat = sb("qo_nat", [P, 2, KC, D])
    kvr_nat = sb("kvr_nat", [NE + 1, 3, D])
    bias_row = sb("bias_row", [1, D + 96])
    qb_dh = sb("qb_dh", [1, D])
    vb_row = sb("vb_row", [1, HD_A])
    vb_heads = sb("vb_heads", [1, P])
    vb_wide = sb("vb_wide", [P, P])
    one = sb("one", [1, 1])
    wq_nat = sb("wq_nat", [P, KC, D])
    pos = sb("pos", [P, NB, 2])
    ang = sb("ang", [P, 2, NB, 4])
    turns = sb("turns", [P, 2, NB * 4])
    trig = g["trig"]
    x, s1, mid, acc = g["x"], g["s1"], g["mid"], g["acc"]
    ident, nident, identb = g["ident"], g["nident"], g["identb"]

    w_in, row_in, pos_in, ob_in, wb_in = (sem(n) for n in ("w_in", "row_in", "pos_in", "ob_in", "wb_in"))
    cleared, built, consts = sem("cleared"), sem("built"), sem("consts")
    wT_done, wT_out, turned, trig_done = (sem(n) for n in ("wT_done", "wT_out", "turned", "trig_done"))
    rows_zero, permuted = sem("rows_zero"), sem("permuted")
    turned_row, vb_out = sem("turned_row"), sem("vb_out")

    with nc.Block() as block:
        @block.sync
        def _(sp):
            for i, name in enumerate(("q_w", "o_w")):
                sp.dma_start(qo_nat[:, i], io[name].rearrange("(r p) n -> p r n", p=P)).then_inc(w_in, 16)
            for i, name in enumerate(("k_w", "v_w", "router_w")):
                sp.dma_start(kvr_nat[0:UH, i], io[name]).then_inc(w_in, 16)
            sp.dma_start(kvr_nat[NE:NE + 1, 2], io["sh_gate_w"].rearrange("k n -> n k")).then_inc(w_in, 16)
            sp.dma_start(pos[:], io["pos"].rearrange("b p c -> p b c")).then_inc(pos_in, 16)
            for n in range(4):
                sp.dma_start(x[:, 4 * n:4 * n + 4, :], io["x"][4 * n:4 * n + 4].rearrange("b p d -> p b d")).then_inc(g["x_in"][min(n, 1)], 16)
            sp.dma_start(g["ob"][:, 0, :], io["o_b"].rearrange("(a n) -> a n", a=1).partition_broadcast(P)).then_inc(ob_in, 16)
            sp.dma_start(g["ob"][:, 1, :], io["bout"].rearrange("(a n) -> a n", a=1).partition_broadcast(P)).then_inc(ob_in, 16)
            sp.wait_ge(ob_in, 32)

        @block.scalar
        def _(act):
            act.wait_ge(rows_zero, 1)
            act.dma_start(bias_row[:, 0:D], io["q_b"].rearrange("(a n) -> a n", a=1)).then_inc(row_in, 16)
            for r in range(3):
                act.dma_start(bias_row[:, D + 32 * r:D + 32 * r + HD_A], io["k_b"].rearrange("(a n) -> a n", a=1)).then_inc(row_in, 16)
            act.dma_start(vb_row[:], io["v_b"].rearrange("(a n) -> a n", a=1)).then_inc(row_in, 16)
            act.dma_start(wq_nat[:], io["Wq"].rearrange("(k p) n -> p k n", p=P)).then_inc(wb_in, 16)
            act.dma_start(g["wkv"][:], io["Wkv"]).then_inc(wb_in, 16)
            act.dma_start(g["wout"][:], io["Wout"].rearrange("(k p) n -> p k n", p=P)).then_inc(wb_in, 16)
            act.wait_ge(turned, 7)
            nc.scalar.activation(trig[:].rearrange("p s b f -> p (s b f)"), ang[:].rearrange("p s b f -> p (s b f)"),
                                 ACT.Sin).then_inc(trig_done, 1)
            act.wait_ge(row_in, 80)
            act.wait_ge(wb_in, 48)

        @block.gpsimd
        def _(pool):
            nc.gpsimd.memset(bias_row[:], 0.0).then_inc(rows_zero, 1)
            nc.gpsimd.memset(ident[:], 0.0).then_inc(cleared, 1)
            nc.gpsimd.memset(nident[:], 0.0).then_inc(cleared, 1)
            nc.gpsimd.memset(g["mask_q"][:], 0.0).then_inc(cleared, 1)
            pool.wait_ge(cleared, 3)
            for t, v in ((ident, 1.0), (nident, -1.0)):
                nc.gpsimd.affine_select(out=t[:], in_=t[:], compare_op=ALU.not_equal, fill=v, base=0,
                                        pattern=[[-1, P]], channel_multiplier=1).then_inc(built, 1)
            nc.gpsimd.affine_select(out=g["mask_q"][:], in_=g["mask_q"][:], compare_op=ALU.is_ge, fill=MASKED, base=0,
                                    pattern=[[0, 4], [-1, P]], channel_multiplier=1).then_inc(built, 1)
            pool.wait_ge(built, 1)
            nc.gpsimd.tensor_copy(identb[:], ident[:]).then_inc(built, 1)
            nc.gpsimd.memset(g["ln_eps"][:], EPS).then_inc(built, 1)
            nc.gpsimd.memset(g["zero"][:], 0.0).then_inc(built, 1)
            nc.gpsimd.memset(g["ln_pow"][:], -0.5).then_inc(built, 1)
            nc.gpsimd.memset(g["qs"][:].bitcast(F32), 0.0).then_inc(built, 1)

        @block.vector
        def _(dve):
            nc.vector.memset(one[:], 1.0).then_inc(consts, 1)
            nc.vector.memset(g["kst"][MROW:MROW + 2].bitcast(F32), 1.0)
            nc.vector.memset(g["wkT"][:], 0.0).then_inc(consts, 1)
            dve.wait_ge(built, 1)
            gather = g["gather"][:].rearrange("p (g w) -> p g w", g=4)
            parts = ident[:].rearrange("p (g w) -> p g w", g=4)
            nc.vector.tensor_copy(gather, parts[:, :, 0:HD_B + 1])
            nc.vector.tensor_reduce(g["of_head"][:], ident[:].rearrange("p (r i) -> p i r", i=4), AX.X, ALU.add)
            dve.wait_ge(row_in, 80)
            nc.vector.tensor_copy(qb_dh[:].rearrange("p (d h) -> p h d", h=UH), bias_row[:, 0:D].rearrange("p (h d) -> p h d", d=HD_A)).then_inc(turned_row, 1)
            nc.vector.tensor_copy(vb_heads[:].rearrange("p (h d) -> p h d", d=HD_A),
                                  vb_row[:].unsqueeze(1).broadcast_to([1, P // HD_A, HD_A])).then_inc(turned_row, 1)
            dve.wait_ge(pos_in, 16)
            av = ang[:].rearrange("p s b (c f) -> p s b c f", f=2)
            nc.vector.tensor_copy(av[:, 0, :, :, 0], pos[:]).then_inc(turned, 1)
            nc.vector.tensor_scalar(av[:, 0, :, :, 1], pos[:], FREQ1, None, ALU.mult).then_inc(turned, 1)
            dve.wait_ge(turned, 2)
            af = ang[:].rearrange("p s b f -> p s (b f)")
            nc.vector.tensor_scalar(af[:, 1, :], af[:, 0, :], 3.141592653589793 / 2, None, ALU.add).then_inc(turned, 1)
            dve.wait_ge(turned, 3)
            nc.vector.tensor_scalar(turns[:], af, 1 / (2 * 3.141592653589793), ROUND, ALU.mult, ALU.add).then_inc(turned, 1)
            dve.wait_ge(turned, 4)
            nc.vector.tensor_scalar(turns[:], turns[:], ROUND, None, ALU.subtract).then_inc(turned, 1)
            dve.wait_ge(turned, 5)
            a1, t1 = (v.rearrange("p s b f -> p (s b f)") if v is not turns else v for v in (ang[:], turns))
            tf = turns[:].rearrange("p s n -> p (s n)")
            nc.vector.scalar_tensor_tensor(a1, tf, -TWO_PI_HI, a1, ALU.mult, ALU.add).then_inc(turned, 1)
            dve.wait_ge(turned, 6)
            nc.vector.scalar_tensor_tensor(a1, tf, -TWO_PI_LO, a1, ALU.mult, ALU.add).then_inc(consts, 1)
            dve.wait_ge(consts, 3)
            nc.vector.tensor_scalar(a1, a1, PI_IN, -PI_IN, ALU.min, ALU.max).then_inc(turned, 1)
            dve.wait_ge(wb_in, 48)
            for half in range(2):
                for k in range(KC):
                    nc.vector.tensor_copy(g["wqB"][:, k, half, :].rearrange("p (c f h) -> p h f c", c=2, f=4),
                                          wq_nat[:, k, P * half:P * half + P].rearrange("p (h f c) -> p h f c", h=UH, f=4)).then_inc(permuted, 1)
                nc.vector.tensor_copy(g["wkB"][:, half, :].rearrange("p (c f h) -> p h f c", c=2, f=4),
                                      g["wkv"][:, P * half:P * half + P].rearrange("p (h f c) -> p h f c", h=UH, f=4)).then_inc(permuted, 1)
            dve.wait_ge(wT_done, 1)
            for k in range(KC):
                for r in range(2):
                    nc.vector.tensor_copy(g["wqT"][:, k, :].rearrange("p (d h) -> p h d", h=UH)[:, 8 * r:8 * r + 8, :],
                                          s1[:, 0, P * (2 * k + r):P * (2 * k + r) + P].rearrange("p (h d) -> p h d", d=HD_A)).then_inc(wT_out, 1)
            dve.wait_ge(wT_done, 2)
            nc.vector.tensor_copy(g["woT"][:].rearrange("p k n -> p (k n)"), s1[:, 1, :]).then_inc(wT_out, 1)
            dve.wait_ge(wT_done, 3)
            small = mid[:, 0:192].rearrange("p (w k n) -> p w k n", w=3, k=KC)
            for r in range(3):
                nc.vector.tensor_copy(g["wkT"][:, :, 32 * r:32 * r + HD_A], small[:, 0, :, 0:HD_A]).then_inc(wT_out, 1)
            nc.vector.tensor_copy(g["wvT"][:], small[:, 1, :, 0:HD_A]).then_inc(wT_out, 1)
            nc.vector.tensor_copy(g["wr"][:], small[:, 2, :, 0:NE + 1]).then_inc(wT_out, 1)
            dve.wait_ge(wT_done, 4)
            nc.vector.tensor_copy(g["qkb"][:, 0:2], acc[:, 0:2]).then_inc(wT_out, 1)
            nc.vector.tensor_copy(g["qkb"][0:96, 2:3], acc[0:96, 2:3]).then_inc(wT_out, 1)
            nc.vector.tensor_copy(vb_wide[:], acc[:, 3:4].broadcast_to([P, P])).then_inc(vb_out, 1)
            dve.wait_ge(wT_done, 5)
            dve.wait_ge(ob_in, 32)
            nc.vector.tensor_tensor(g["ob"][:, 0, :], s1[:, 0, 0:D], g["ob"][:, 0, :], ALU.add)

        @block.tensor
        def _(pe):
            pe.wait_ge(built, 2)
            pe.wait_ge(w_in, 96)
            for i in range(2):
                for k in range(KC):
                    for r in range(2):
                        last = nc.tensor.transpose(s1[:, i, P * (2 * k + r):P * (2 * k + r) + P], qo_nat[:, i, r, P * k:P * k + P], ident[:])
                last.then_inc(wT_done, 1)
            for w in range(3):
                for k in range(KC):
                    n = NE + 1 if w == 2 else UH
                    last = nc.tensor.transpose(mid[:, 64 * w + 32 * k:64 * w + 32 * k + n], kvr_nat[0:n, w, P * k:P * k + P], ident[0:n, 0:n])
            last.then_inc(wT_done, 1)
            pe.wait_ge(row_in, 80)
            pe.wait_ge(consts, 1)
            pe.wait_ge(turned_row, 2)
            for c in range(2):
                nc.tensor.matmul(acc[:, c:c + 1], qb_dh[:, P * c:P * c + P], one[:], start=True, stop=True)
            nc.tensor.matmul(acc[:, 3:4], vb_heads[:], one[:], start=True, stop=True)
            nc.tensor.matmul(acc[0:96, 2:3], bias_row[:, D:D + 96], one[:], start=True, stop=True).then_inc(wT_done, 1)
            pe.wait_ge(vb_out, 1)
            pe.wait_ge(wT_out, 5)
            for k in range(KC):
                last = nc.tensor.matmul(s1[:, 0, 0:D], vb_wide[:], g["woT"][:, k, :], start=(k == 0), stop=(k == KC - 1))
            last.then_inc(wT_done, 1)


def self_attention(nc, g, tmp):
    def sb(name, shape, dt=F32):
        return tmp.enter_context(nc.sbuf_tensor(name, shape, dt))

    def sem(name):
        return tmp.enter_context(nc.semaphore(name))

    x, s1, s2, mid, acc = g["x"], g["s1"], g["s2"], g["mid"], g["acc"]
    qs = g["qs"]
    gate = sb("a_gate", [P, 2])
    ks = sb("ks", [P, SLOTS, P], F32R)
    v = sb("v", [P, SLOTS, VW])
    stats = sb("stats", [P, SLOTS, 6])
    mv = sb("mv", [P, SLOTS, 2])
    rstd = sb("rstd", [P, SLOTS, 2])
    xn = sb("xn", [P, 2, D])
    xnT = sb("xnT", [P, 2, KC, P])
    qf = sb("qf", [P, 2, KC, P])
    qhi = sb("qhi", [P, 2, KC, P], F32R)
    qlo = sb("qlo", [P, 2, KC, P], F32R)
    kf = sb("kf", [96, 2, P])
    mx = sb("mx", [P, UH])
    mxs = sb("mxs", [P, 2, 2, UH])
    mT = sb("mT", [32, 2, P], F32R)
    pt = sb("pt", [P, 2, 8, P])
    rc = sb("rc", [P, UH])
    sums = sb("sums", [P, 512])
    o = sb("o", [P, 2, D])
    oT = sb("oT", [P, 2, KC, P])

    stack_in = [sem(f"stack_in{i}") for i in range(SLOTS)]
    mrow_in = [sem(f"mrow_in{i}") for i in range(SLOTS)]
    (init, ln_stats, ln_aggr, eps_done, rstd_done, xn_done, trx_done, xnT_done, proj_done, qkv_out, q_hi, q_split,
     k_hi, ks_done, ob_added, s1_done, max_done, mx_hi, mx_split, mT_done, mT_out, s2_done, exp_done, pv_done, sums_out, tb_done, rc_done,
     o_normed, trO_done, oT_done, out_done, x_added) = (sem("a_" + n) for n in (
        "init", "ln_stats", "ln_aggr", "eps_done", "rstd_done", "xn_done", "trx_done", "xnT_done", "proj_done", "qkv_out",
        "q_hi", "q_split", "k_hi", "ks_done", "ob_added", "s1_done", "max_done", "mx_hi", "mx_split", "mT_done", "mT_out",
        "s2_done", "exp_done", "pv_done", "sums_out", "tb_done", "rc_done", "o_normed", "trO_done", "oT_done", "out_done", "x_added"))
    AHEAD = 4
    LN_AHEAD = 5
    widened, tab_done, tab_out, causal_done = sem("widened"), sem("tab_done"), sem("tab_out"), sem("causal_done")
    trig, wide, rope = g["trig"], g["wide"], g["rope"]

    def tables(c):
        return (2 * (c + AHEAD), 2 * (c + AHEAD) + 1) if -AHEAD <= c < 0 else ()

    def at(j, c):
        return 4 * j + c, c % SLOTS, j + c // SLOTS

    with nc.Block() as block:
        @block.sync
        def _(sp):
            def step(j, c):
                if valid(j, c + 3, NB):
                    b, s, r = at(j, c + 3)
                    sp.wait_ge(q_split, b + 1)
                    need(sp, s2_done, 2 * b - 6)
                    for row, part in ((0, qhi), (32, qhi), (64, qlo)):
                        for k in range(KC):
                            sp.dma_start(qs[row + 8 * k:row + 8 * k + 8, s].bitcast(F32),
                                         part[:, s % 2, k, :].bitcast(F32)).then_inc(stack_in[s], 16)
                if valid(j, c + 1, NB):
                    b, s, r = at(j, c + 1)
                    sp.wait_ge(mT_out, b + 1)
                    sp.dma_start(qs[MROW:MROW + 2, s].bitcast(F32), mT[:, s % 2, :].bitcast(F32)).then_inc(mrow_in[s], 16)

            steps(sp, step, -LN_AHEAD, 1, 2, NB)

        @block.gpsimd
        def _(pool):
            nc.gpsimd.memset(v[:], 1.0).then_inc(init, 1)

            def step(j, c):
                def causal(u):
                    if valid(j, c, NB):
                        b, _, _ = at(j, c)
                        pool.wait_ge(exp_done, 2 * b + u + 1)
                        nc.gpsimd.tensor_tensor(gate[:, u:u + 1], g["zero"][:, 0:1], g["zero"][:, 0:1], ALU.add)
                        nc.gpsimd.affine_select(out=pt[:, u], in_=pt[:, u], compare_op=ALU.is_ge, fill=0.0, base=0,
                                                pattern=[[0, 8], [1, P]], channel_multiplier=-1).then_inc(causal_done, 1)

                if valid(j, c + 3, NB):
                    b, s, r = at(j, c + 3)
                    p = s % 2
                    pool.wait_ge(qkv_out, b + 1)
                    if not (isinstance(b, int) and b < 2):
                        _, s_2, r_2 = at(j, c + 1)
                        pool.wait_ge(stack_in[s_2], 16 * STACK_DMAS * (r_2 + 1))
                    nc.gpsimd.tensor_tensor(qhi[:, p].rearrange("p k t -> p (k t)"), qf[:, p].rearrange("p k t -> p (k t)"), g["zero"][:, 0:1].broadcast_to([P, D]), ALU.add).then_inc(q_hi, 1)
                    pool.wait_ge(q_hi, b + 1)
                    nc.gpsimd.tensor_tensor(qlo[:, p], qf[:, p], qhi[:, p].bitcast(F32), ALU.subtract).then_inc(q_split, 1)
                    need(pool, s2_done, 2 * b - 6)
                    if isinstance(b, int) and b == 0:
                        pool.wait_ge(init, 2)
                    nc.gpsimd.tensor_tensor(ks[0:96, s], kf[:, p], g["zero"][0:96, 0:1].broadcast_to([96, P]), ALU.add).then_inc(k_hi, 1)
                causal(0)
                causal(1)
                if valid(j, c + LN_AHEAD, NB):
                    b, s, r = at(j, c + LN_AHEAD)
                    pool.wait_ge(ln_aggr, b + 1)
                    nc.gpsimd.tensor_tensor(rstd[:, s, 0:1], mv[:, s, 1:2], g["ln_eps"][:, 0:1], ALU.add).then_inc(eps_done, 1)
                    pool.wait_ge(eps_done, b + 1)
                    nc.gpsimd.tensor_tensor(rstd[:, s, 1:2], rstd[:, s, 0:1], g["ln_pow"][:, 0:1], ALU.pow).then_inc(rstd_done, 1)
                if valid(j, c + AHEAD, NB):
                    b, s, r = at(j, c + AHEAD)
                    pool.wait_ge(xn_done, b + 1)
                    nc.gpsimd.tensor_tensor(x[:, b, :], x[:, b, :], g["ob"][:, 0, :], ALU.add).then_inc(ob_added, 1)

            steps(pool, step, -LN_AHEAD, 1, 2, NB)

        @block.vector
        def _(dve):
            nc.vector.memset(ks[:].bitcast(F32), 1.0).then_inc(init, 1)

            def step(j, c):
                moments, ahead, split, p1, done = (valid(j, c + d, NB) for d in (LN_AHEAD, AHEAD, 3, 2, -1))
                bm, sm, _ = at(j, c + LN_AHEAD)
                b, s, r = at(j, c + AHEAD)
                b1, sl1, _ = at(j, c + 2)
                b0, sl0, _ = at(j, c - 1)
                done = done and not (isinstance(b0, int) and b0 < 0)

                def row_max(n):
                    if p1:
                        if n == 0:
                            need(dve, mx_split, b1)
                        dve.wait_ge(s1_done, 4 * b1 + n + 1)
                        nc.vector.tensor_reduce(mx[:, 4 * n:4 * n + 4], s1[:, n % 2, :].rearrange("p (h k) -> p h k", h=4),
                                                AX.X, ALU.max).then_inc(max_done, 1)

                if ahead:
                    dve.wait_ge(rstd_done, b + 1)
                    need(dve, trx_done, b - 1)
                    nc.vector.tensor_scalar(xn[:, s % 2, :], x[:, b, :], mv[:, s, 0:1], rstd[:, s, 1:2],
                                            ALU.subtract, ALU.mult).then_inc(xn_done, 1)
                for n in tables(c):
                    need(dve, tab_done, n - 1)
                    for pair in range(2):
                        src = trig[:, n // 4, 4 * (n % 4):4 * (n % 4) + 4, :].unsqueeze(3).broadcast_to([P, 4, 4, UH])
                        nc.vector.tensor_scalar(wide[:, n % 2, :, 64 * pair:64 * pair + 64].rearrange("p b (f h) -> p b f h", h=UH), src,
                                                -1.0 if (n // 4, pair) == (0, 0) else 1.0, None, ALU.mult).then_inc(widened, 1)
                row_max(0)
                if done:
                    dve.wait_ge(tb_done, b0 + 1)
                    pv = acc[:].rearrange("p (i g w) -> p i g w", i=4, g=4)
                    rcv = rc[:].rearrange("p (i g) -> p i g", i=4)
                    nc.vector.reciprocal(rcv, pv[:, :, :, HD_A]).then_inc(rc_done, 1)
                    dve.wait_ge(rc_done, b0 + 1)
                    nc.vector.tensor_tensor(o[:, sl0 % 2, :].rearrange("p (g i d) -> p i g d", i=4, g=4), pv[:, :, :, 0:HD_A],
                                            rcv.unsqueeze(3).broadcast_to([P, 4, 4, HD_A]), ALU.mult).then_inc(o_normed, 1)
                if moments:
                    if isinstance(bm, int) and bm in (0, 4):
                        dve.wait_ge(g["x_in"][bm // 4], (16, 48)[bm // 4])
                    nc.vector.bn_stats(stats[:, sm, :], x[:, bm, :]).then_inc(ln_stats, 1)
                row_max(1)
                if split:
                    b3, s3, _ = at(j, c + 3)
                    dve.wait_ge(k_hi, b3 + 1)
                    nc.vector.tensor_tensor(ks[32:64, s3], kf[32:64, s3 % 2], ks[32:64, s3].bitcast(F32), ALU.subtract).then_inc(ks_done, 1)
                if moments:
                    dve.wait_ge(ln_stats, bm + 1)
                row_max(2)
                if moments:
                    nc.vector.bn_aggr(mv[:, sm, :], stats[:, sm, :]).then_inc(ln_aggr, 1)
                if done:
                    dve.wait_ge(out_done, b0 + 1)
                    dve.wait_ge(ob_added, b0 + 1)
                    nc.vector.tensor_tensor(x[:, b0, :], mid[:, 0:D], x[:, b0, :], ALU.add).then_inc(x_added, 1)
                row_max(3)
                if p1:
                    dve.wait_ge(max_done, 4 * b1 + 4)
                    need(dve, mT_done, b1 - 1)
                    nc.vector.tensor_copy(mxs[:, sl1 % 2, 0, :].bitcast(F32R), mx[:]).then_inc(mx_hi, 1)
                    dve.wait_ge(mx_hi, b1 + 1)
                    nc.vector.tensor_tensor(mxs[:, sl1 % 2, 1, :], mx[:], mxs[:, sl1 % 2, 0, :], ALU.subtract).then_inc(mx_split, 1)

            steps(dve, step, -LN_AHEAD, 1, 2, NB)

        @block.scalar
        def _(act):
            def step(j, c):
                def exps(u):
                    if valid(j, c, NB):
                        b, s, _ = at(j, c)
                        act.wait_ge(s2_done, 2 * b + u + 1)
                        need(act, pv_done, 2 * b + u - 1)
                        nc.scalar.activation(pt[:, u].rearrange("p h q -> p (h q)"), s2[:, u].rearrange("p a n -> p (a n)"),
                                             ACT.Exp, scale=HD_A ** -0.5).then_inc(exp_done, 1)

                exps(0)
                if valid(j, c - 1, NB):
                    b, s, _ = at(j, c - 1)
                    act.wait_ge(trO_done, b + 1)
                    nc.scalar.copy(oT[:, s % 2].rearrange("p k t -> p (k t)"), mid[:, 0:D]).then_inc(oT_done, 1)
                if valid(j, c + 1, NB):
                    b, s, _ = at(j, c + 1)
                    act.wait_ge(mT_done, b + 1)
                    if not (isinstance(b, int) and b < 2):
                        _, s_2, r_2 = at(j, c - 1)
                        act.wait_ge(mrow_in[s_2], 16 * (r_2 + 1))
                    nc.scalar.copy(mT[:, s % 2, :], acc[0:32, 384:512]).then_inc(mT_out, 1)
                exps(1)
                if valid(j, c + AHEAD, NB):
                    b, s, _ = at(j, c + AHEAD)
                    p = s % 2
                    act.wait_ge(trx_done, b + 1)
                    nc.scalar.copy(xnT[:, p].rearrange("p k t -> p (k t)"), mid[:, 0:D]).then_inc(xnT_done, 1)
                if valid(j, c, NB):
                    b, s, _ = at(j, c)
                    act.wait_ge(pv_done, 2 * b + 2)
                    need(act, tb_done, b)
                    nc.scalar.copy(sums[:], acc[:]).then_inc(sums_out, 1)
                if valid(j, c + AHEAD, NB):
                    b, s, _ = at(j, c + AHEAD)
                    p = s % 2
                    act.wait_ge(proj_done, b + 1)
                    need(act, q_split, b - 1)
                    need(act, ks_done, b - 1)
                    if isinstance(b, int) and b == 0:
                        act.wait_ge(init, 2)
                    for k in range(KC):
                        nc.scalar.activation(qf[:, p, k, :], mid[:, P * k:P * k + P], ACT.Identity, bias=g["qkb"][:, k:k + 1])
                    nc.scalar.activation(kf[:, p, :], mid[0:96, 256:384], ACT.Identity, bias=g["qkb"][0:96, 2:3])
                    nc.scalar.copy(v[:, s, 0:HD_A], mid[:, 384:400]).then_inc(qkv_out, 1)
                for n in tables(c):
                    act.wait_ge(tab_done, n + 1)
                    nc.scalar.copy(rope[:, n // 4, 4 * (n % 4):4 * (n % 4) + 4, :].rearrange("p b t -> p (b t)"),
                                   s2[:, n % 2, 0, :]).then_inc(tab_out, 1)

            steps(act, step, -LN_AHEAD, 1, 2, NB)

        @block.tensor
        def _(pe):
            def step(j, c):
                b1, sl1, r1 = at(j, c + 2)
                b2, sl2, r2 = at(j, c)
                b0, sl0, _ = at(j, c - 1)
                b3, sl3, _ = at(j, c + AHEAD)
                ahead, p1, pm, p2, done = (valid(j, c + d, NB) for d in (AHEAD, 2, 1, 0, -1))

                def scores(n):
                    if not p1:
                        return
                    if n == 0:
                        pe.wait_ge(stack_in[sl1], 16 * STACK_DMAS * (r1 + 1))
                        pe.wait_ge(ks_done, b1 + 1)
                    need(pe, max_done, 4 * b1 + n - 1)
                    nc.tensor.matmul(s1[:, n % 2, :], g["identb"][:], g["mask_q"][:], start=True, stop=False)
                    for h in range(4):
                        last = nc.tensor.matmul(s1[:, n % 2, P * h:P * h + P], qs[0:MROW, sl1, 4 * n + h, :], ks[0:MROW, sl1, :],
                                                start=False, stop=(h == 3))
                    last.then_inc(s1_done, 1)

                def shifted(u):
                    if not p2:
                        return
                    if u == 0:
                        pe.wait_ge(mrow_in[sl2], 16 * (r2 + 1))
                        if isinstance(b2, int) and b2 == 0:
                            pe.wait_ge(tab_out, 8)
                    need(pe, exp_done, 2 * b2 + u - 1)
                    for q in range(2):
                        last = nc.tensor.matmul(s2[:, u, q, :], ks[:, sl2, :], qs[:, sl2, 8 * u + 4 * q:8 * u + 4 * q + 4, :],
                                                start=True, stop=True)
                    last.then_inc(s2_done, 1)

                def values(u):
                    if not p2:
                        return
                    pe.wait_ge(causal_done, 2 * b2 + u + 1)
                    if u == 0:
                        need(pe, o_normed, b2)
                        pe.wait_ge(mT_out, cap(b2 + 2, NB))
                    for q in range(2):
                        row = VW * (2 * u + q)
                        last = nc.tensor.matmul(acc[row:row + VW, :], v[:, sl2, :], pt[:, u, 4 * q:4 * q + 4, :], start=True, stop=True)
                    last.then_inc(pv_done, 1)

                def turn_x():
                    if ahead:
                        pe.wait_ge(xn_done, b3 + 1)
                        need(pe, qkv_out, b3)
                        need(pe, x_added, b3 - AHEAD)
                        for k in range(KC):
                            last = nc.tensor.transpose(mid[:, P * k:P * k + P], xn[:, sl3 % 2, P * k:P * k + P], g["ident"][:])
                        last.then_inc(trx_done, 1)
                    for n in tables(c):
                        pe.wait_ge(widened, 2 * n + 2)
                        need(pe, tab_out, n - 1)
                        for q in range(4):
                            last = nc.tensor.transpose(s2[:, n % 2, 0, P * q:P * q + P], wide[:, n % 2, q, :], g["ident"][:])
                        last.then_inc(tab_done, 1)

                def project():
                    if ahead:
                        pe.wait_ge(xnT_done, b3 + 1)
                        for m in range(2):
                            for k in range(KC):
                                nc.tensor.matmul(mid[:, P * m:P * m + P], g["wqT"][:, k, P * m:P * m + P], xnT[:, sl3 % 2, k, :],
                                                 start=(k == 0), stop=(k == KC - 1))
                        for k in range(KC):
                            nc.tensor.matmul(mid[0:96, 256:384], g["wkT"][:, k, :], xnT[:, sl3 % 2, k, :], start=(k == 0), stop=(k == KC - 1))
                        for k in range(KC):
                            last = nc.tensor.matmul(mid[:, 384:400], xnT[:, sl3 % 2, k, :], g["wvT"][:, k, :], start=(k == 0),
                                                    stop=(k == KC - 1))
                        last.then_inc(proj_done, 1)

                if c == -2:
                    turn_x()
                    project()
                scores(0)
                shifted(0)
                if done:
                    pe.wait_ge(sums_out, b0 + 1)
                    for i in range(4):
                        last = nc.tensor.transpose(acc[:, P * i:P * i + P], sums[:, P * i:P * i + P], g["ident"][:])
                    last.then_inc(tb_done, 1)
                scores(1)
                shifted(1)
                if done:
                    pe.wait_ge(o_normed, b0 + 1)
                    pe.wait_ge(qkv_out, cap(b0 + AHEAD + 1, NB))
                    for k in range(KC):
                        last = nc.tensor.transpose(mid[:, P * k:P * k + P], o[:, sl0 % 2, P * k:P * k + P], g["ident"][:])
                    last.then_inc(trO_done, 1)
                if pm:
                    pe.wait_ge(mx_split, b2 + 2)
                    need(pe, o_normed, b2)
                    if isinstance(b2, int) and b2 <= 0:
                        need(pe, mT_out, b2 + 1)
                    nc.tensor.matmul(acc[0:32, 384:512], mxs[:, (sl2 + 1) % 2].rearrange("p a h -> p (a h)"), g["nident"][:],
                                     start=True, stop=True).then_inc(mT_done, 1)
                scores(2)
                if done:
                    pe.wait_ge(oT_done, b0 + 1)
                    for k in range(KC):
                        last = nc.tensor.matmul(mid[:, 0:D], oT[:, sl0 % 2, k, :], g["woT"][:, k, :], start=(k == 0), stop=(k == KC - 1))
                    last.then_inc(out_done, 1)
                values(0)
                if c != -2:
                    turn_x()
                scores(3)
                values(1)
                if c != -2:
                    project()

            steps(pe, step, -LN_AHEAD, 1, 2, NB)


def cross_attention(nc, io, g, tmp):
    def sb(name, shape, dt=F32):
        return tmp.enter_context(nc.sbuf_tensor(name, shape, dt))

    def sem(name):
        return tmp.enter_context(nc.semaphore(name))

    x, s1, s2, mid, acc = g["x"], g["s1"], g["s2"], g["mid"], g["acc"]
    NUNIT = 2 * NB
    QK = 4 * P
    kst, of_head = g["kst"], g["of_head"]
    qst = sb("b_qst", [MROW, SLOTS, 4, P], F32R)
    q_spread = sb("b_q_spread", [MROW + 2, 2, UH, P], F32R)
    k_spread = sb("b_k_spread", [MROW, 2, UH, P], F32R)
    v = sb("b_v", [P, 2, NH_B, VW])
    stats = sb("b_stats", [P, 2, 6])
    mv = sb("b_mv", [P, 2, 2])
    rstd = sb("b_rstd", [P, 2, 2])
    xn = sb("b_xn", [P, 2, D])
    ctx = sb("b_ctx", [P, 2, CTX])
    xcT = sb("b_xcT", [P, 2, KC + 1, P])
    swapped = sb("b_swapped", [P, QK])
    by_cos = sb("b_by_cos", [P, QK])
    by_sin = sb("b_by_sin", [P, QK])
    qkhi = sb("b_qkhi", [P, 2, 2, 2, P], F32R)
    qklo = sb("b_qklo", [P, 2, 2, 2, P], F32R)
    mx = sb("b_mx", [P, UH])
    mxs = sb("b_mxs", [P, 2, 2, UH])
    mT = sb("b_mT", [32, 2, P], F32R)
    pt = sb("b_pt", [P, 2, 8, P])
    sums = sb("b_sums", [P, 512])
    rc = sb("b_rc", [P, UH])
    o = sb("b_o", [P, 2, D])
    oT = sb("b_oT", [P, 2, KC, P])

    q_in = [sem(f"q_in{i}") for i in range(SLOTS)]
    k_in = [sem(f"k_in{i}") for i in range(SLOTS)]
    mrow_in = [sem(f"b_mrow_in{i}") for i in range(SLOTS)]
    ctx_in = [sem(f"ctx_in{i}") for i in range(2)]
    (init, ln_stats, ln_aggr, eps_done, rstd_done, xn_done, trx_done, xcT_done, qk_done, qk_swapped, qk_out, sin_done,
     turned, qk_hi, qk_lo, ob_added, v_done, v_out, s1_done, max_done, mx_hi, mx_split, mT_done, mT_out, s2_done, exp_done,
     q_spread_a, q_spread_p, k_spread_p, k_spread_v, sums_out, tb_done, pv_done, rc_done, o_normed, trO_done, oT_done, out_done, x_added) = (sem("b_s_" + n) for n in (
        "init", "ln_stats", "ln_aggr", "eps_done", "rstd_done", "xn_done", "trx_done", "xcT_done", "qk_done", "qk_swapped",
        "qk_out", "sin_done", "turned", "qk_hi", "qk_lo", "ob_added", "v_done", "v_out", "s1_done", "max_done", "mx_hi",
        "mx_split", "mT_done", "mT_out", "s2_done", "exp_done", "q_spread_a", "q_spread_p", "k_spread_p", "k_spread_v", "sums_out", "tb_done", "pv_done", "rc_done", "o_normed", "trO_done", "oT_done",
        "out_done", "x_added"))
    LN_AHEAD, PROJ_AHEAD, TURN_AHEAD, V_AHEAD = 7, 6, 5, 2
    FIRST, ENTER, LOOPED, LAST = -7, 5, 5, NUNIT + 1
    TERMS = 3

    def at(j, c):
        return 4 * j + c, c % SLOTS, j + c // SLOTS

    def batch(j, c):
        return 2 * j + c // 2, (c // 2) % 2

    def has(j, c):
        return valid(j, c, NUNIT)

    def k_spread_half(eng, ops, j, c, u, done):
        if not has(j, c + 3):
            return
        b, s, r = at(j, c + 3)
        eng.wait_ge(k_in[s], 16 * TERMS * (r + 1))
        need(eng, s1_done, 4 * b - 4)
        ops.tensor_tensor(k_spread[:, s % 2, 8 * u:8 * u + 8, :].rearrange("p (n i) t -> p n i t", n=2),
                          kst[0:MROW, s, 2 * u:2 * u + 2, :].unsqueeze(2).broadcast_to([MROW, 2, 4, P]),
                          of_head[0:MROW].unsqueeze(1).unsqueeze(3).broadcast_to([MROW, 2, 4, P]), ALU.mult).then_inc(done, 1)

    with nc.Block() as block:
        @block.sync
        def _(sp):
            def stack(j, c, dst, w, parts, done):
                b, s, r = at(j, c + 4)
                half = c % 2
                bt, par = batch(j, c + 4 - half)
                sp.wait_ge(qk_lo, bt + 1)
                for n in range(TERMS):
                    sp.dma_start(dst[32 * n:32 * n + 32, s].bitcast(F32),
                                 parts[n][:, par, w, half, :].bitcast(F32)).then_inc(done[s], 16)

            def step(j, c):
                if has(j, c + 4):
                    b, s, r = at(j, c + 4)
                    need(sp, q_spread_a, b - 3)
                    need(sp, q_spread_p, b - 3)
                    stack(j, c, qst, 0, (qkhi, qkhi, qklo), q_in)
                if has(j, c + 1):
                    b, s, r = at(j, c + 1)
                    sp.wait_ge(mT_out, b + 1)
                    sp.dma_start(q_spread[MROW:MROW + 2, s % 2].bitcast(F32), mT[:, s % 2, :].bitcast(F32)).then_inc(mrow_in[s], 16)
                if c % 2 and has(j, c + LN_AHEAD):
                    b, p = batch(j, c + LN_AHEAD)
                    need(sp, trx_done, b - 1)
                    sp.dma_start(ctx[:, p, :], io["ctx"][b]).then_inc(ctx_in[p], 16)
                if has(j, c + 4):
                    b, s, r = at(j, c + 4)
                    need(sp, s2_done, 2 * b - 6)
                    stack(j, c, kst, 1, (qkhi, qklo, qkhi), k_in)

            steps(sp, step, FIRST, ENTER, LOOPED, LAST)

        @block.gpsimd
        def _(pool):
            nc.gpsimd.memset(v[:], 1.0).then_inc(init, 1)

            def step(j, c):
                if has(j, c + 1):
                    b, s, r = at(j, c + 1)
                    pool.wait_ge(q_in[s], 16 * TERMS * (r + 1))
                    need(pool, s2_done, 2 * b - 2)
                    nc.gpsimd.tensor_tensor(q_spread[0:MROW, s % 2, 8:16, :].rearrange("p (n i) t -> p n i t", n=2),
                                            qst[:, s, 2:4, :].unsqueeze(2).broadcast_to([MROW, 2, 4, P]),
                                            of_head[0:MROW].unsqueeze(1).unsqueeze(3).broadcast_to([MROW, 2, 4, P]), ALU.mult).then_inc(q_spread_p, 1)
                k_spread_half(pool, nc.gpsimd, j, c, 0, k_spread_p)
                if c % 2 == 0 and has(j, c + PROJ_AHEAD):
                    b, p = batch(j, c + PROJ_AHEAD)
                    pool.wait_ge(qk_swapped, b + 1)
                    need(pool, turned, b)
                    nc.gpsimd.tensor_tensor(by_sin[:].rearrange("p (a t) -> p a t", a=4), swapped[:].rearrange("p (a t) -> p a t", a=4),
                                            g["rope"][:, 0, b, :].unsqueeze(1).broadcast_to([P, 4, P]), ALU.mult).then_inc(sin_done, 1)
                if c % 2 and has(j, c + TURN_AHEAD):
                    b, p = batch(j, c + TURN_AHEAD)
                    pool.wait_ge(qk_hi, b + 1)
                    nc.gpsimd.tensor_tensor(qklo[:, p].rearrange("p a b t -> p (a b t)"), by_cos[:],
                                            qkhi[:, p].rearrange("p a b t -> p (a b t)").bitcast(F32), ALU.subtract).then_inc(qk_lo, 1)
                if c % 2 and has(j, c + LN_AHEAD):
                    b, p = batch(j, c + LN_AHEAD)
                    pool.wait_ge(ln_aggr, b + 1)
                    nc.gpsimd.tensor_tensor(rstd[:, p, 0:1], mv[:, p, 1:2], g["ln_eps"][:, 0:1], ALU.add).then_inc(eps_done, 1)
                    pool.wait_ge(eps_done, b + 1)
                    nc.gpsimd.tensor_tensor(rstd[:, p, 1:2], rstd[:, p, 0:1], g["ln_pow"][:, 0:1], ALU.pow).then_inc(rstd_done, 1)
                    pool.wait_ge(xn_done, b + 1)
                    nc.gpsimd.tensor_tensor(x[:, b, :], x[:, b, :], g["ob"][:, 1, :], ALU.add).then_inc(ob_added, 1)

            steps(pool, step, FIRST, ENTER, LOOPED, LAST)

        @block.vector
        def _(dve):
            def step(j, c):
                even = c % 2 == 0
                b1, sl1, _ = at(j, c + 2)
                p1, done = has(j, c + 2), has(j, c - 1)

                def row_max(n):
                    if p1:
                        if n == 0:
                            need(dve, mx_split, b1)
                        dve.wait_ge(s1_done, 4 * b1 + n + 1)
                        nc.vector.tensor_reduce(mx[:, 4 * n:4 * n + 4], s1[:, n % 2, :].rearrange("p (h k) -> p h k", h=4),
                                                AX.X, ALU.max).then_inc(max_done, 1)

                row_max(0)
                row_max(1)
                if done:
                    b0, _, _ = at(j, c - 1)
                    half = (c - 1) % 2
                    bt, par = batch(j, c - 1 - half)
                    dve.wait_ge(tb_done, b0 + 1)
                    pv = acc[:].rearrange("p (i n) -> p i n", i=4)[:, :, 0:4 * (HD_B + 1)].rearrange("p i (g w) -> p i g w", g=4)
                    rcv = rc[:].rearrange("p (i g) -> p i g", i=4)
                    nc.vector.reciprocal(rcv, pv[:, :, :, HD_B]).then_inc(rc_done, 1)
                    dve.wait_ge(rc_done, b0 + 1)
                    nc.vector.tensor_tensor(o[:, par, P * half:P * half + P].rearrange("p (i g d) -> p i g d", i=4, g=4), pv[:, :, :, 0:HD_B],
                                            rcv.unsqueeze(3).broadcast_to([P, 4, 4, HD_B]), ALU.mult).then_inc(o_normed, 1)
                if not even and has(j, c + TURN_AHEAD):
                    b, _ = batch(j, c + TURN_AHEAD)
                    dve.wait_ge(sin_done, b + 1)
                    dve.wait_ge(qk_out, b + 1)
                    nc.vector.tensor_tensor(by_cos[:], by_cos[:], by_sin[:], ALU.add).then_inc(turned, 1)
                ln = not even and has(j, c + LN_AHEAD)
                b, p = batch(j, c + LN_AHEAD) if ln else (0, 0)
                if ln:
                    nc.vector.bn_stats(stats[:, p, :], x[:, b, :]).then_inc(ln_stats, 1)
                if ln:
                    dve.wait_ge(ln_stats, b + 1)
                row_max(2)
                if ln:
                    nc.vector.bn_aggr(mv[:, p, :], stats[:, p, :]).then_inc(ln_aggr, 1)
                row_max(3)
                if not even and has(j, c - 3) and has(j, c - 2):
                    b0, _ = batch(j, c - 3)
                    dve.wait_ge(out_done, b0 + 1)
                    dve.wait_ge(ob_added, b0 + 1)
                    nc.vector.tensor_tensor(x[:, b0, :], mid[:, 0:D], x[:, b0, :], ALU.add).then_inc(x_added, 1)
                if p1:
                    dve.wait_ge(max_done, 4 * b1 + 4)
                    need(dve, mT_done, b1 - 1)
                    nc.vector.tensor_copy(mxs[:, sl1 % 2, 0, :].bitcast(F32R), mx[:]).then_inc(mx_hi, 1)
                    dve.wait_ge(mx_hi, b1 + 1)
                    nc.vector.tensor_tensor(mxs[:, sl1 % 2, 1, :], mx[:], mxs[:, sl1 % 2, 0, :], ALU.subtract).then_inc(mx_split, 1)
                k_spread_half(dve, nc.vector, j, c, 1, k_spread_v)
                if ln:
                    dve.wait_ge(rstd_done, b + 1)
                    need(dve, trx_done, b - 1)
                    nc.vector.tensor_scalar(xn[:, p, :], x[:, b, :], mv[:, p, 0:1], rstd[:, p, 1:2],
                                            ALU.subtract, ALU.mult).then_inc(xn_done, 1)
                if even and has(j, c + PROJ_AHEAD):
                    b, p = batch(j, c + PROJ_AHEAD)
                    dve.wait_ge(qk_swapped, b + 1)
                    need(dve, qk_lo, b)
                    nc.vector.tensor_tensor(by_cos[:].rearrange("p (a t) -> p a t", a=4), mid[:].rearrange("p (a t) -> p a t", a=4),
                                            g["rope"][:, 1, b, :].unsqueeze(1).broadcast_to([P, 4, P]), ALU.mult).then_inc(qk_out, 1)

            steps(dve, step, FIRST, ENTER, LOOPED, LAST)

        @block.scalar
        def _(act):
            def step(j, c):
                even = c % 2 == 0

                def exps(u):
                    if has(j, c):
                        b, s, _ = at(j, c)
                        act.wait_ge(s2_done, 2 * b + u + 1)
                        need(act, pv_done, 2 * b + u - 1)
                        nc.scalar.activation(pt[:, u].rearrange("p h q -> p (h q)"), s2[:, u].rearrange("p a n -> p (a n)"),
                                             ACT.Exp, scale=HD_B ** -0.5).then_inc(exp_done, 1)

                def spread_queries(heads):
                    if has(j, c + 1):
                        b, s, r = at(j, c + 1)
                        if heads[0] == 0:
                            act.wait_ge(q_in[s], 16 * TERMS * (r + 1))
                            need(act, s2_done, 2 * b - 2)
                        for i in heads:
                            last = nc.scalar.activation(q_spread[0:MROW, s % 2, 0:8].rearrange("p (n i) t -> p n i t", i=4)[:, :, i, :], qst[:, s, 0:2, :],
                                                        ACT.Copy, scale=of_head[0:MROW, i:i + 1])
                        if heads[-1] == 3:
                            last.then_inc(q_spread_a, 1)

                if has(j, c - 1):
                    b, s, _ = at(j, c - 1)
                    act.wait_ge(pv_done, 2 * b + 2)
                    need(act, tb_done, b)
                    nc.scalar.copy(sums[:], acc[:]).then_inc(sums_out, 1)
                if even and has(j, c + V_AHEAD):
                    b, p = batch(j, c + V_AHEAD)
                    act.wait_ge(v_done, b + 1)
                    if isinstance(b, int) and b == 0:
                        act.wait_ge(init, 1)
                    nc.scalar.copy(v[:, p, :, 0:HD_B], mid[:, 0:D].rearrange("p (h d) -> p h d", h=NH_B)).then_inc(v_out, 1)
                exps(0)
                if not even:
                    spread_queries((0,))
                if not even and has(j, c - 3) and has(j, c - 2):
                    b, p = batch(j, c - 3)
                    act.wait_ge(trO_done, b + 1)
                    nc.scalar.copy(oT[:, p].rearrange("p k t -> p (k t)"), mid[:, 0:D]).then_inc(oT_done, 1)
                if not even and has(j, c + TURN_AHEAD):
                    b, p = batch(j, c + TURN_AHEAD)
                    act.wait_ge(turned, b + 1)
                    if not (isinstance(b, int) and b < 2):
                        _, s_2, r_2 = at(j, c + 2)
                        act.wait_ge(q_in[s_2], 16 * TERMS * (r_2 + 1))
                        act.wait_ge(k_in[s_2], 16 * TERMS * (r_2 + 1))
                    nc.scalar.copy(qkhi[:, p].rearrange("p a b t -> p (a b t)"), by_cos[:]).then_inc(qk_hi, 1)
                if even and has(j, c + PROJ_AHEAD):
                    b, p = batch(j, c + PROJ_AHEAD)
                    act.wait_ge(trx_done, b + 1)
                    nc.scalar.copy(xcT[:, p].rearrange("p k t -> p (k t)"), mid[:, 0:3 * P]).then_inc(xcT_done, 1)
                if even:
                    spread_queries((0, 1))
                if has(j, c + 1):
                    b, s, _ = at(j, c + 1)
                    act.wait_ge(mT_done, b + 1)
                    if not (isinstance(b, int) and b < 2):
                        _, s_2, r_2 = at(j, c - 1)
                        act.wait_ge(mrow_in[s_2], 16 * (r_2 + 1))
                    nc.scalar.copy(mT[:, s % 2, :], acc[0:32, 384:512]).then_inc(mT_out, 1)
                exps(1)
                spread_queries((2, 3) if even else (1, 2, 3))
                if even and has(j, c + PROJ_AHEAD):
                    b, p = batch(j, c + PROJ_AHEAD)
                    act.wait_ge(qk_done, b + 1)
                    need(act, sin_done, b)
                    nc.scalar.copy(swapped[0:64, :], mid[64:P, :])
                    nc.scalar.copy(swapped[64:P, :], mid[0:64, :]).then_inc(qk_swapped, 1)

            steps(act, step, FIRST, ENTER, LOOPED, LAST)

        @block.tensor
        def _(pe):
            def step(j, c):
                odd = c % 2 == 1
                b1, sl1, r1 = at(j, c + 2)
                b2, sl2, r2 = at(j, c)
                p1, p2 = has(j, c + 2), has(j, c)
                half2 = c % 2
                _, vpar = batch(j, c - half2)

                def scores(n):
                    if not p1:
                        return
                    if n == 0:
                        pe.wait_ge(q_in[sl1], 16 * TERMS * (r1 + 1))
                        pe.wait_ge(k_spread_p, b1 + 1)
                    if n == 2:
                        pe.wait_ge(k_spread_v, b1 + 1)
                    need(pe, max_done, 4 * b1 + n - 1)
                    nc.tensor.matmul(s1[:, n % 2, :], qst[:, sl1, n, :], k_spread[:, sl1 % 2, 4 * n:4 * n + 4, :],
                                     start=True, stop=True).then_inc(s1_done, 1)

                def shifted(u):
                    if not p2:
                        return
                    if u == 0:
                        pe.wait_ge(q_spread_a, b2 + 1)
                        pe.wait_ge(mrow_in[sl2], 16 * (r2 + 1))
                    else:
                        pe.wait_ge(q_spread_p, b2 + 1)
                    need(pe, exp_done, 2 * b2 + u - 1)
                    for q in range(2):
                        last = nc.tensor.matmul(s2[:, u, q, :], kst[:, sl2, 2 * u + q, :], q_spread[:, sl2 % 2, 8 * u + 4 * q:8 * u + 4 * q + 4, :],
                                                start=True, stop=True)
                    last.then_inc(s2_done, 1)

                def values(u, d):
                    if not has(j, c + d):
                        return
                    b, _, _ = at(j, c + d)
                    half = (c + d) % 2
                    bt, par = batch(j, c + d - half)
                    pe.wait_ge(exp_done, 2 * b + u + 1)
                    if u == 0:
                        need(pe, o_normed, b)
                        pe.wait_ge(mT_out, cap(b + 2, NUNIT))
                        if half == 0:
                            pe.wait_ge(v_out, bt + 1)
                    for h in range(8):
                        row, col = VW * (2 * u + h // 4), P * (h % 4)
                        head = UH * half + 4 * (h % 4) + 2 * u + h // 4
                        last = nc.tensor.matmul(acc[row:row + VW, col:col + P], v[:, par, head, :], pt[:, u, h, :],
                                                start=True, stop=True)
                    last.then_inc(pv_done, 1)

                scores(0)
                values(1, -1)
                if not odd and has(j, c + V_AHEAD):
                    b, p = batch(j, c + V_AHEAD)
                    need(pe, x_added, b - 2)
                    pe.wait_ge(qk_out, cap(b + 2, NB))
                    nc.tensor.matmul(mid[:, 0:D], xcT[:, p, KC, :], g["wkv"][:, D:2 * D], start=True, stop=True).then_inc(v_done, 1)
                shifted(0)
                scores(1)
                if has(j, c - 1):
                    b0, _, _ = at(j, c - 1)
                    pe.wait_ge(sums_out, b0 + 1)
                    for i in range(4):
                        last = nc.tensor.matmul(acc[:, P * i:P * i + 4 * (HD_B + 1)], sums[:, P * i:P * i + P], g["gather"][:], start=True, stop=True)
                    last.then_inc(tb_done, 1)
                if not odd and has(j, c + PROJ_AHEAD):
                    b, p = batch(j, c + PROJ_AHEAD)
                    pe.wait_ge(xn_done, b + 1)
                    need(pe, v_out, b - 1)
                    need(pe, qk_out, b)
                    pe.wait_ge(ctx_in[p], 16 * (j + (c + PROJ_AHEAD) // 4 + 1))
                    for k in range(KC):
                        nc.tensor.transpose(mid[:, P * k:P * k + P], xn[:, p, P * k:P * k + P], g["ident"][:])
                    nc.tensor.transpose(mid[:, 2 * P:3 * P], ctx[:, p, :], g["ident"][:]).then_inc(trx_done, 1)
                scores(2)
                if odd and has(j, c - 3) and has(j, c - 2):
                    b, p = batch(j, c - 3)
                    pe.wait_ge(o_normed, 2 * b + 2)
                    pe.wait_ge(qk_out, cap(b + 5, NB))
                    pe.wait_ge(v_out, cap(b + 3, NB))
                    for k in range(KC):
                        last = nc.tensor.transpose(mid[:, P * k:P * k + P], o[:, p, P * k:P * k + P], g["ident"][:])
                    last.then_inc(trO_done, 1)
                shifted(1)
                if has(j, c + 1):
                    pe.wait_ge(mx_split, b2 + 2)
                    need(pe, o_normed, b2)
                    if isinstance(b2, int) and b2 <= 0:
                        need(pe, mT_out, b2 + 1)
                    nc.tensor.matmul(acc[0:32, 384:512], mxs[:, (sl2 + 1) % 2].rearrange("p a h -> p (a h)"), g["nident"][:],
                                     start=True, stop=True).then_inc(mT_done, 1)
                scores(3)
                if odd and has(j, c - 3) and has(j, c - 2):
                    b, p = batch(j, c - 3)
                    pe.wait_ge(oT_done, b + 1)
                    for k in range(KC):
                        last = nc.tensor.matmul(mid[:, 0:D], oT[:, p, k, :], g["wout"][:, k, :], start=(k == 0), stop=(k == KC - 1))
                    last.then_inc(out_done, 1)
                if not odd and has(j, c + PROJ_AHEAD):
                    b, p = batch(j, c + PROJ_AHEAD)
                    pe.wait_ge(xcT_done, b + 1)
                    for half in range(2):
                        for k in range(KC):
                            nc.tensor.matmul(mid[:, P * half:P * half + P], g["wqB"][:, k, half, :], xcT[:, p, k, :], start=(k == 0), stop=(k == KC - 1))
                    for half in range(2):
                        last = nc.tensor.matmul(mid[:, P * (2 + half):P * (3 + half)], g["wkB"][:, half, :], xcT[:, p, KC, :], start=True, stop=True)
                    last.then_inc(qk_done, 1)
                values(0, 0)

            steps(pe, step, FIRST, ENTER, LOOPED, LAST)


def unit(j, c):
    if c >= UG:
        j, c = j + 1, c - UG
    if isinstance(j, int) and j == NG:
        t, q = divmod(c, CB)
        rows = LASTC if q == CB - 1 else P
        return NG, c, t, q, CG * NG + q, rows, q == 0, q == CB - 1
    if c < CA * NT:
        t, q = divmod(c, CA)
        return j, c, t, q, CG * j + q, P, q == 0, q == CA - 1
    t, q = divmod(c - CA * NT, CB)
    return j, c, t, CB + q, CG * j + CA + q, P, q == 0, q == CB - 1


def mixture(nc, io, g, out, tmp):
    def sb(name, shape, dt=F32):
        return tmp.enter_context(nc.sbuf_tensor(name, shape, dt))

    def sem(name):
        return tmp.enter_context(nc.semaphore(name))

    x, ident, s1, s2, last2 = g["x"], g["ident"], g["s1"], g["s2"], g["last2"]
    NSLOT = 2 * CB
    xhi = sb("xhi", [P, KC, TOK], F32R)
    xlo = sb("xlo", [P, KC, TOK], F32R)
    y = sb("y", [P, 2, TOK])
    ROWS = NE + NSH
    stored_weights = nc.dram_tensor("token_weights", [ROWS, TOK], F32, kind="Internal").ap()
    combT = sb("combT", [ROWS, 2, TT])
    per_row = sb("per_row", [P, 4, TT])
    wgu = sb("wgu", [P, NSLOT, 2, KC, 2, P], F32R)
    wd = sb("wd", [P, NSLOT, 2, D], F32R)
    raw_gu = sb("raw_gu", [P, 2, KC, RAW])
    raw_d = sb("raw_d", [P, CB, D])
    logits_ps, yT = last2[:, 1, :], last2

    raw_in, w_hi, w_lo = sem("raw_in"), sem("w_hi"), sem("w_lo")
    weights_stored = [sem(f"weights_stored{i}") for i in range(2)]
    wide_in = [sem(f"wide_in{i}") for i in range(4)]
    (ln_stats, ln_aggr, eps_done, rstd_done, xn_done, trx_done, x_full, x_hi, x_lo, lgT_done, lgT_out, logit_done) = (sem("m_" + n) for n in (
        "ln_stats", "ln_aggr", "eps_done", "rstd_done", "xn_done", "trx_done", "x_full", "x_hi", "x_lo", "lgT_done", "lgT_out", "logit_done"))
    r_dve, r_exp, comb_trans, comb_out = sem("r_dve"), sem("r_exp"), sem("comb_trans"), sem("comb_out")
    (gate_done, up_done, silu_done, prod_done, h_done, h_hi, h_lo, down_done, y_added) = (sem("u_" + n) for n in (
        "gate_done", "up_done", "silu_done", "prod_done", "h_done", "h_hi", "h_lo", "down_done", "y_added"))
    yt_done, x_final, stored = sem("yt_done"), sem("x_final"), sem("stored")
    comb_ready, raw_tail = sem("comb_ready"), sem("raw_tail")
    GROUP_DMAS = 9
    FREE = 4

    BT = TT // P
    NR = NB // BT
    stats = sb("m_stats", [P, NB, 6])
    mv = sb("m_mv", [P, NB, 2])
    rstd = sb("m_rstd", [P, 2, NB])
    lg = sb("lg", [P, NB, NE])
    pr = sb("pr", [P, NB, NE + 4])
    rest = sb("rest", [P, NB, NE + 4])
    top = sb("top", [P, NB, 8])
    red = sb("red", [P, 4, NB])
    comb = sb("comb", [P, NB, NE + NSH])
    sg = sb("silu_gate", [P, 2, TT])
    prod = sb("prod", [P, TT])
    h = sb("h_full", [P, 2, TT])
    xn = h[:].rearrange("p a (i d) -> p (a i) d", d=D)
    xf = sg
    lgT = prod
    hhi = sb("h_hi", [P, 4, TT], F32R)
    hlo = sb("h_lo", [P, 4, TT], F32R)

    def mix_steps(eng, step, last):
        for c in range(2):
            step(0, c)
        with eng.Fori(0, NG) as j:
            for c in range(2, UG + 2):
                step(j, c)
        for c in range(NG * UG + 2, last + 1):
            step(c // UG, c % UG) if c < (NG + 1) * UG else step(NG, c - NG * UG)

    def exists(j, c):
        return not isinstance(j, int) or 0 <= UG * j + c < NU

    def back(j, c, n):
        c -= n
        return (j, c) if c >= 0 else (j - 1, c + UG)

    def pieces(j, c):
        slot, rows = unit(j, c)[3], unit(j, c)[5]
        start = P * (slot if slot < CB else CA + slot - CB)
        found, row = [], 0
        while row < rows:
            e = (start + row) // FE
            end = min(rows, FE * (e + 1) - start)
            found.append((row, end, e))
            row = end
        return found

    def wide_loads(j, c):
        if c >= UG:
            j, c = j + 1, c - UG
        def loads(g, last):
            return sum(len(pieces(g, i)) for i in range(c % 4, last + 1, 4))
        return loads(0, UG - 1) * j + loads(j if isinstance(j, int) else 0, c)

    def spread_weights(eng, j, c):
        if exists(j, c):
            t = unit(j, c)[2]
            for first, last, e in pieces(j, c):
                row = e + 8 * (j + 1 if c >= UG else j)
                eng.dma_start(per_row[first:last, c % 4, :],
                              stored_weights[bass.ds(row, 1), TT * t:TT * t + TT].partition_broadcast(last - first)).then_inc(wide_in[c % 4], 16)

    def final_tile(j, c):
        if not (isinstance(j, int) and j == NG):
            return None
        t, over = divmod(c - (CB + 3), CB)
        return t if over == 0 and 0 <= t < NT - 1 else None

    def split_at(j, c):
        if isinstance(j, int) and j == NG:
            return (CB - 1, CB - 1, LASTC) if c == 2 else None
        if 3 <= c <= 18 and c % 3 == 0:
            return CB + c // 3 - 1, c // 3 - 1, P
        if c >= 24 and c % 4 == 0 and c // 4 - 6 < CA:
            return c // 4 - 6, c // 4 - 6, P
        return None

    def split_count(j, c):
        if isinstance(j, int) and j == NG:
            return CG * NG + CB - 1
        return CG * j + (CA + c // 3 - 1 if c <= 18 else CG + c // 4 - 6)

    def raw_wait(eng, j, c):
        if isinstance(j, int) and j == NG:
            eng.wait_ge(raw_tail, 16)
        else:
            eng.wait_ge(raw_in, 16 * GROUP_DMAS * (2 * j + (2 if c <= 18 else 3)))

    with nc.Block() as block:
        @block.sync
        def _(sp):
            down = io["w_down"].rearrange("e i n -> (e i) n")

            def columns(e, n, lo, first, width):
                for w, name in enumerate(("w_gate", "w_up")):
                    for k in range(KC):
                        sp.dma_start(raw_gu[:, w, k, lo:lo + n * width].rearrange("p (e i) -> p e i", e=n),
                                     io[name][e:e + n, P * k:P * k + P, first:first + width].rearrange("e p i -> p e i")).then_inc(raw_in, 16)

            def store_weights():
                for n in range(NT):
                    sp.wait_ge(comb_out, n + 1)
                    sp.dma_start(stored_weights[:, TT * n:TT * n + TT], combT[:, n % 2, :]).then_inc(weights_stored[n % 2], 16)

            for j in range(NG):
                need(sp, w_lo, CG * j)
                cut = CA * P - 3 * FE
                columns(8 * j, 3, 0, 0, FE)
                columns(8 * j + 3, 1, 3 * FE, 0, cut)
                row = CG * P * j
                sp.dma_start(raw_d[:, 0:CA, :], down[row:row + CA * P, :].rearrange("(c p) n -> p c n", p=P)).then_inc(raw_in, 16)
                if j == 0:
                    store_weights()
                    for i in range(2):
                        sp.wait_ge(weights_stored[i], 32)
                    for c in range(4):
                        spread_weights(sp, 0, c)
                sp.wait_ge(w_lo, CG * j + CA)
                columns(8 * j + 3, 1, 0, cut, FE - cut)
                columns(8 * j + 4, 4, FE - cut, 0, FE)
                row += CA * P
                sp.dma_start(raw_d[:, 0:CB, :], down[row:row + CB * P, :].rearrange("(c p) n -> p c n", p=P)).then_inc(raw_in, 16)
            sp.wait_ge(w_lo, CG * NG)
            for w, name in enumerate(("sh_gate", "sh_up")):
                for k in range(KC):
                    for half in range(2):
                        cols = slice(2 * FE * half, 2 * FE * (half + 1))
                        sp.dma_start(raw_gu[:, w, k, cols], io[name][P * k:P * k + P, cols]).then_inc(raw_in, 16)
            sp.dma_start(raw_d[:, 0:CA, :], io["sh_down"][0:CA * P, :].rearrange("(c p) n -> p c n", p=P)).then_inc(raw_in, 16)
            sp.dma_start(raw_d[0:LASTC, CA, :], io["sh_down"][CA * P:NSH * FE, :]).then_inc(raw_tail, 16)
            for n in range(4):
                sp.wait_ge(x_final, 2 * n + 2)
                sp.dma_start(out[4 * n:4 * n + 4].rearrange("b p d -> p b d"), x[:, 4 * n:4 * n + 4, :]).then_inc(stored, 16)
            sp.wait_ge(stored, 64)

        @block.gpsimd
        def _(pool):
            def split_lo(slot, raw, rows, n):
                pool.wait_ge(w_hi, n + 1)
                nc.gpsimd.tensor_tensor(wgu[:, slot, :, :, 1, 0:rows].rearrange("p w k n -> p (w k) n"),
                                        raw_gu[:, :, :, P * raw:P * raw + rows].rearrange("p w k n -> p (w k) n"),
                                        wgu[:, slot, :, :, 0, 0:rows].rearrange("p w k n -> p (w k) n").bitcast(F32), ALU.subtract)
                nc.gpsimd.tensor_tensor(wd[0:rows, slot, 1, :], raw_d[0:rows, raw, :],
                                        wd[0:rows, slot, 0, :].bitcast(F32), ALU.subtract).then_inc(w_lo, 1)

            for n in range(NR):
                four = slice(BT * n, BT * n + BT)
                pool.wait_ge(ln_aggr, BT * n + BT)
                nc.gpsimd.tensor_tensor(rstd[:, 0, four], mv[:, four, 1], g["ln_eps"][:, 0:1].broadcast_to([P, BT]), ALU.add).then_inc(eps_done, 1)
                pool.wait_ge(eps_done, n + 1)
                nc.gpsimd.tensor_tensor(rstd[:, 1, four], rstd[:, 0, four], g["ln_pow"][:, 0:1].broadcast_to([P, BT]), ALU.pow).then_inc(rstd_done, 1)
            split_lo(0, 0, P, 0)
            nc.gpsimd.memset(y[:, 0], 0.0).then_inc(down_done, FREE)
            nc.gpsimd.memset(y[:, 1], 0.0).then_inc(y_added, 1)
            for q in range(1, CA):
                split_lo(q, q, P, q)

            def step(j, c):
                u = UG * j + c
                if exists(j, c):
                    rows = unit(j, c)[5]
                    pool.wait_ge(h_hi, u + 1)
                    pool.wait_ge(down_done, u - 3 + FREE)
                    nc.gpsimd.tensor_tensor(hlo[0:rows, c % 4, :], h[0:rows, c % 2, :], hhi[0:rows, c % 4, :].bitcast(F32),
                                            ALU.subtract).then_inc(h_lo, 1)
                at = split_at(j, c)
                if at:
                    split_lo(*at, split_count(j, c))

            mix_steps(pool, step, NU - 1)

        @block.scalar
        def _(act):
            def split_hi(slot, raw, rows, n):
                nc.scalar.copy(wgu[:, slot, :, :, 0, 0:rows].rearrange("p w k n -> p (w k) n"),
                               raw_gu[:, :, :, P * raw:P * raw + rows].rearrange("p w k n -> p (w k) n"))
                nc.scalar.copy(wd[0:rows, slot, 0, :], raw_d[0:rows, raw, :]).then_inc(w_hi, 1)

            def logits_out(n):
                act.wait_ge(lgT_done, n + 1)
                need(act, logit_done, n)
                nc.scalar.copy(lgT[0:NE + 1, :], s2[0:NE + 1, 0, 0, :]).then_inc(lgT_out, 1)

            for n in range(NR):
                if n:
                    act.wait_ge(lgT_done, n)
                    act.wait_ge(x_lo, n)
                for a in range(2):
                    act.wait_ge(trx_done, 2 * n + a + 1)
                    src = s1[:, a, :].rearrange("p (i k t) -> p i k t", i=2, k=KC)
                    nc.scalar.copy(xf[:, :, 2 * P * a:2 * P * a + 2 * P].rearrange("p k (i t) -> p i k t", i=2), src).then_inc(x_full, 1)
                    nc.scalar.copy(xhi[:, :, TT * n + 2 * P * a:TT * n + 2 * P * a + 2 * P].rearrange("p k (i t) -> p i k t", i=2), src).then_inc(x_hi, 1)
                if n == 1:
                    act.wait_ge(raw_in, 16 * GROUP_DMAS)
                    split_hi(0, 0, P, 0)
                logits_out(n)
            act.wait_ge(r_dve, 2)
            nc.scalar.activation(pr[:, :, 0:NE], lg[:], ACT.Exp).then_inc(r_exp, 1)
            nc.scalar.activation(comb[:, :, NE], logits_ps[:, 0:NB * (NE + 1)].rearrange("p (b e) -> p b e", b=NB)[:, :, NE],
                                 ACT.Exp, scale=-1.0).then_inc(r_exp, 1)
            for q in range(1, CA):
                split_hi(q, q, P, q)
            for n in range(4):
                act.wait_ge(comb_trans, n + 1)
                need(act, weights_stored[n % 2], 16 * (n // 2))
                nc.scalar.copy(combT[:, n % 2, :], s2[0:ROWS, n % 2, 1, :]).then_inc(comb_out, 1)

            def step(j, c):
                u = UG * j + c
                if exists(j, c):
                    rows = unit(j, c)[5]
                    act.wait_ge(gate_done, u + 1)
                    need(act, prod_done, u - 1)
                    nc.scalar.activation(sg[0:rows, c % 2, :], s1[0:rows, c % 2, :], ACT.Silu).then_inc(silu_done, 1)
                jb, cb = back(j, c, 1)
                if exists(jb, cb):
                    rows = unit(jb, cb)[5]
                    act.wait_ge(h_done, u)
                    act.wait_ge(down_done, u - 4 + FREE)
                    nc.scalar.copy(hhi[0:rows, cb % 4, :], h[0:rows, cb % 2, :]).then_inc(h_hi, 1)
                if not isinstance(j, int) or UG * j + c > 0:
                    spread_weights(act, j, c + 3)
                at = split_at(j, c)
                if at:
                    raw_wait(act, j, c)
                    act.wait_ge(down_done, FREE + UG * j + (0 if c <= 18 else CA * NT))
                    split_hi(*at, None)

            mix_steps(act, step, NU)

        @block.vector
        def _(dve):
            nc.vector.memset(pr[:, :, NE:NE + 4], -1.0).then_inc(r_dve, 1)

            def moments(n):
                for b in range(BT * n, BT * n + BT):
                    nc.vector.bn_stats(stats[:, b, :], x[:, b, :]).then_inc(ln_stats, 1)
                dve.wait_ge(ln_stats, BT * n + BT)
                for b in range(BT * n, BT * n + BT):
                    nc.vector.bn_aggr(mv[:, b, :], stats[:, b, :]).then_inc(ln_aggr, 1)

            def normalised(n):
                dve.wait_ge(rstd_done, n + 1)
                need(dve, trx_done, 2 * n)
                for i in range(BT):
                    b = BT * n + i
                    last = nc.vector.tensor_scalar(xn[:, i, :], x[:, b, :], mv[:, b, 0:1], rstd[:, 1, b:b + 1], ALU.subtract, ALU.mult)
                last.then_inc(xn_done, 1)

            def lo_parts(n):
                dve.wait_ge(x_hi, 2 * n + 2)
                nc.vector.tensor_tensor(xlo[:, :, TT * n:TT * n + TT], xf[:], xhi[:, :, TT * n:TT * n + TT].bitcast(F32),
                                        ALU.subtract).then_inc(x_lo, 1)

            moments(0)
            for n in range(NR):
                if n + 1 < NR:
                    moments(n + 1)
                normalised(n)
                if n:
                    lo_parts(n - 1)
            lo_parts(NR - 1)
            made = [1]

            def then(ins, *more):
                made[0] += 1
                ins.then_inc(r_dve, 1)
                dve.wait_ge(r_dve, made[0])

            lps = logits_ps[:, 0:NB * (NE + 1)].rearrange("p (b e) -> p b e", b=NB)[:, :, 0:NE]
            wide = lambda a: a.unsqueeze(2).broadcast_to([P, NB, NE])
            dve.wait_ge(logit_done, NR)
            nc.vector.tensor_reduce(red[:, 0, :], lps, AX.X, ALU.max).then_inc(ln_stats, 1)
            dve.wait_ge(ln_stats, NB + 1)
            then(nc.vector.tensor_tensor(lg[:], lps, wide(red[:, 0, :]), ALU.subtract))
            dve.wait_ge(r_exp, 1)
            then(nc.vector.tensor_reduce(red[:, 1, :], pr[:, :, 0:NE], AX.X, ALU.add))
            then(nc.vector.reciprocal(red[:, 1, :], red[:, 1, :]))
            then(nc.vector.tensor_tensor(pr[:, :, 0:NE], pr[:, :, 0:NE], wide(red[:, 1, :]), ALU.mult))
            for b in range(NB):
                last = nc.vector.max(out=top[:, b, :], in_=pr[:, b, 0:NE])
            then(last)
            then(nc.vector.memset(top[:, :, TOPK:8], -1.0))
            for b in range(NB):
                last = nc.vector.match_replace(out=rest[:, b, :], in_to_replace=top[:, b, :], in_values=pr[:, b, :], imm_value=0.0)
            then(last)
            then(nc.vector.tensor_tensor(comb[:, :, 0:NE], pr[:, :, 0:NE], rest[:, :, 0:NE], ALU.subtract))
            then(nc.vector.tensor_reduce(red[:, 2, :], comb[:, :, 0:NE], AX.X, ALU.add))
            then(nc.vector.tensor_scalar(red[:, 2, :], red[:, 2, :], 1e-9, None, ALU.max))
            then(nc.vector.reciprocal(red[:, 2, :], red[:, 2, :]))
            then(nc.vector.tensor_tensor(comb[:, :, 0:NE], comb[:, :, 0:NE], wide(red[:, 2, :]), ALU.mult))
            dve.wait_ge(r_exp, 2)
            then(nc.vector.tensor_scalar(red[:, 3, :], comb[:, :, NE], 1.0, None, ALU.add))
            then(nc.vector.reciprocal(red[:, 3, :], red[:, 3, :]))
            nc.vector.tensor_copy(comb[:, :, NE:NE + NSH], red[:, 3, :].unsqueeze(2).broadcast_to([P, NB, NSH])).then_inc(comb_ready, 1)
            def final_add(t):
                for a in range(2):
                    b = BT * t + 2 * a
                    dve.wait_ge(yt_done, 2 * t + a + 1)
                    nc.vector.tensor_tensor(x[:, b:b + 2, :].rearrange("p b d -> p (b d)"), s2[:, a, 1, :],
                                            x[:, b:b + 2, :].rearrange("p b d -> p (b d)"), ALU.add).then_inc(x_final, 1)

            def step(j, c):
                u = UG * j + c
                if exists(j, c):
                    rows = unit(j, c)[5]
                    need(dve, h_done, u)
                    dve.wait_ge(silu_done, u + 1)
                    dve.wait_ge(up_done, u + 1)
                    nc.vector.tensor_tensor(prod[0:rows, :], s2[0:rows, c % 2, 0, :], sg[0:rows, c % 2, :], ALU.mult).then_inc(prod_done, 1)
                    dve.wait_ge(prod_done, u + 1)
                    need(dve, h_lo, u - 1)
                    dve.wait_ge(wide_in[c % 4], 16 * wide_loads(j, c))
                    nc.vector.tensor_tensor(h[0:rows, c % 2, :], per_row[0:rows, c % 4, :], prod[0:rows, :], ALU.mult).then_inc(h_done, 1)
                jb, cb = back(j, c, 2)
                if exists(jb, cb) and unit(jb, cb)[7]:
                    gj, gc, t = unit(jb, cb)[0:3]
                    dve.wait_ge(down_done, UG * jb + cb + 1 + FREE)
                    nc.vector.tensor_tensor(y[:, :, TT * t:TT * t + TT], last2[:], y[:, :, TT * t:TT * t + TT], ALU.add).then_inc(y_added, 1)
                if final_tile(j, c) is not None:
                    final_add(final_tile(j, c))

            mix_steps(dve, step, NU + 1)
            final_add(NT - 1)

        def tiles(j, c):
            if isinstance(j, int) and j == NG:
                return 2 * NT * NG + c // CB
            return 2 * NT * j + (c // CA if c < CA * NT else NT + (c - CA * NT) // CB)

        @block.tensor
        def _(pe):
            def transposes(n):
                pe.wait_ge(xn_done, n + 1)
                need(pe, x_hi, 2 * n)
                for a in range(2):
                    for i in range(2):
                        for k in range(KC):
                            last = nc.tensor.transpose(s1[:, a, D * i + P * k:D * i + P * k + P], xn[:, 2 * a + i, P * k:P * k + P], ident[:])
                    last.then_inc(trx_done, 1)

            transposes(0)
            for n in range(NR):
                pe.wait_ge(x_full, 2 * n + 2)
                for k in range(KC):
                    last = nc.tensor.matmul(s2[0:NE + 1, 0, 0, :], g["wr"][:, k, :], xf[:, k, :], start=(k == 0), stop=(k == KC - 1))
                last.then_inc(lgT_done, 1)
                if n + 1 < NR:
                    transposes(n + 1)
                pe.wait_ge(lgT_out, n + 1)
                for i in range(BT):
                    col = (NE + 1) * (BT * n + i)
                    last = nc.tensor.transpose(logits_ps[:, col:col + NE + 1], lgT[0:NE + 1, P * i:P * i + P], ident[0:NE + 1, 0:NE + 1])
                last.then_inc(logit_done, 1)

            def comb_transposes():
                pe.wait_ge(comb_ready, 1)
                for n in range(4):
                    need(pe, comb_out, n - 1)
                    for q in range(4):
                        last = nc.tensor.transpose(s2[0:ROWS, n % 2, 1, P * q:P * q + P], comb[:, 4 * n + q, :], ident[:])
                    last.then_inc(comb_trans, 1)

            pe.wait_ge(x_lo, NR)
            pe.wait_ge(x_hi, NB // 2)

            def three(ps, w_hi_ap, w_lo_ap, m_hi, m_lo, start, stop):
                nc.tensor.matmul(ps, w_hi_ap, m_hi, start=start, stop=False)
                nc.tensor.matmul(ps, w_hi_ap, m_lo, start=False, stop=False)
                return nc.tensor.matmul(ps, w_lo_ap, m_hi, start=False, stop=stop)

            def final_transposes(t):
                pe.wait_ge(y_added, 2 * NT * NG + t + 2)
                need(pe, x_final, 2 * t)
                for a in range(2):
                    for i in range(2):
                        for m in range(2):
                            last = nc.tensor.transpose(s2[:, a, 1, D * i + P * m:D * i + P * m + P], y[:, m, P * (BT * t + 2 * a + i):P * (BT * t + 2 * a + i) + P], ident[:])
                    last.then_inc(yt_done, 1)

            def step(j, c):
                u = UG * j + c
                if exists(j, c):
                    gj, gc, t, slot, chunk, rows, first, last_of = unit(j, c)
                    pe.wait_ge(w_lo, chunk + 1)
                    toks = slice(TT * t, TT * t + TT)
                    need(pe, silu_done, u - 1)
                    for w, ps, done in ((0, s1[0:rows, c % 2, :], gate_done), (1, s2[0:rows, c % 2, 0, :], up_done)):
                        if w == 1:
                            need(pe, prod_done, u - 1)
                        for k in range(KC):
                            last = three(ps, wgu[:, slot, w, k, 0, 0:rows], wgu[:, slot, w, k, 1, 0:rows], xhi[:, k, toks], xlo[:, k, toks],
                                         k == 0, k == KC - 1)
                        last.then_inc(done, 1)
                    if isinstance(u, int) and u == 0:
                        comb_transposes()
                jb, cb = back(j, c, 2)
                if exists(jb, cb):
                    gj, gc, t, slot, chunk, rows, first, last_of = unit(jb, cb)
                    if first:
                        pe.wait_ge(y_added, tiles(gj, gc) + 1)
                    pe.wait_ge(h_lo, u - 1)
                    r = cb % 4
                    for m in range(2):
                        last = three(last2[:, m, :], wd[0:rows, slot, 0, P * m:P * m + P], wd[0:rows, slot, 1, P * m:P * m + P],
                                     hhi[0:rows, r, :], hlo[0:rows, r, :], first, last_of)
                    last.then_inc(down_done, 1)
                if final_tile(j, c) is not None:
                    final_transposes(final_tile(j, c))

            mix_steps(pe, step, NU + 1)
            final_transposes(NT - 1)


def build(nc, io, out):
    with ExitStack() as ctx:
        def sb(name, shape, dt=F32):
            return ctx.enter_context(nc.sbuf_tensor(name, shape, dt))

        g = {
            "x": sb("x_sb", [P, NB, D]),
            "ident": sb("ident", [P, P]), "nident": sb("nident", [P, P]), "identb": sb("identb", [P, P], BF16),
            "ln_eps": sb("ln_eps", [P, 4]), "ln_pow": sb("ln_pow", [P, 4]), "zero": sb("zero", [P, 4]),
            "wr": sb("wr", [P, KC, NE + 1]),
            "s1": ctx.enter_context(nc.psum_tensor("s1", [P, 2, 512], F32)),
            "s2": ctx.enter_context(nc.psum_tensor("s2", [P, 2, 2, 512], F32)),
            "x_in": [ctx.enter_context(nc.semaphore(n)) for n in ("first_x_in", "rest_x_in")],
        }
        last2 = ctx.enter_context(nc.psum_tensor("last2", [P, 2, 512], F32))
        g["last2"], g["mid"], g["acc"] = last2, last2[:, 0, :], last2[:, 1, :]
        with ExitStack() as att:
            def sa(name, shape, dt=F32):
                return att.enter_context(nc.sbuf_tensor(name, shape, dt))

            g.update({
                "ob": sa("ob", [P, 2, D]),
                "wqT": sa("wqT", [P, KC, D]), "woT": sa("woT", [P, KC, D]), "wkT": sa("wkT", [P, KC, 96]),
                "wvT": sa("wvT", [P, KC, HD_A]), "qkb": sa("qkb", [P, 3]),
                "wqB": sa("wqB", [P, KC, 2, P]), "wkB": sa("wkB", [P, 2, P]), "wkv": sa("wkv", [P, 2 * D]),
                "wout": sa("wout", [P, KC, D]), "rope": sa("rope", [P, 2, NB, P]),
                "trig": sa("trig", [P, 2, NB, 4]), "wide": sa("wide", [P, 2, 4, P]),
                "kst": sa("kst", [MROW + 2, SLOTS, 4, P], F32R), "of_head": sa("of_head", [P, 4]), "qs": sa("qs", [P, SLOTS, UH, P], F32R),
                "gather": sa("gather", [P, 4 * (HD_B + 1)]),
                "mask_q": sa("mask_q", [P, 4, P], BF16),
            })
            with ExitStack() as tmp:
                prepare(nc, io, g, tmp)
            with ExitStack() as tmp:
                self_attention(nc, g, tmp)
            with ExitStack() as tmp:
                cross_attention(nc, io, g, tmp)
        with ExitStack() as tmp:
            mixture(nc, io, g, out, tmp)


_INS = [("x", "x"), ("ctx", "ctx_1024"), ("pos", "fside_BxSx2_0"), ("q_w", "L0_attn_q_w"), ("q_b", "L0_attn_q_b"),
        ("k_w", "L0_attn_k_w"), ("k_b", "L0_attn_k_b"), ("v_w", "L0_attn_v_w"), ("v_b", "L0_attn_v_b"),
        ("o_w", "L0_attn_o_w"), ("o_b", "L0_attn_o_b"), ("Wq", "L0_xattn_Wq"), ("Wkv", "L0_xattn_Wkv"),
        ("Wout", "L0_xattn_Wout"), ("bout", "L0_xattn_bout"), ("router_w", "L0_ffn_router_w"),
        ("w_gate", "L0_ffn_w_gate"), ("w_up", "L0_ffn_w_up"), ("w_down", "L0_ffn_w_down"),
        ("sh_gate", "L0_ffn_sh_gate"), ("sh_up", "L0_ffn_sh_up"), ("sh_down", "L0_ffn_sh_down"),
        ("sh_gate_w", "L0_ffn_sh_gate_w")]


def kernel(**inputs):
    import numpy as _np
    import concourse.bacc as _bacc
    from concourse import mybir as _mybir
    from concourse.bass_utils import run_bass_kernel_spmd as _run

    nc = _bacc.Bacc("TRN2", target_bir_lowering=False, num_devices=1)
    arrays, io = {}, {}
    for short, name in _INS:
        a = _np.ascontiguousarray(inputs[name])
        arrays[f"in_{short}"] = a
        io[short] = nc.dram_tensor(f"in_{short}", a.shape, _mybir.dt.from_np(a.dtype), kind="ExternalInput").ap()
    out = nc.dram_tensor("out_0", inputs["x"].shape, _mybir.dt.float32, kind="ExternalOutput").ap()
    build(nc, io, out)
    r = _run(nc, [arrays], core_ids=[0])
    return r.results[0]["out_0"]
```
